# Optimizing a Trainium2 kernel written in Bass

```python
import numpy as np
import jax
import jax.numpy as jnp

def _softmax(x, axis=-1):
    return jax.nn.softmax(x, axis=axis)

def _gelu(x):
    return jax.nn.gelu(x, approximate=True)

def _silu(x):
    return jax.nn.silu(x)

def _sigmoid(x):
    return jax.nn.sigmoid(x)

def _layernorm(x, axis=-1, eps=1e-05):
    m = jnp.mean(x, axis=axis, keepdims=True)
    v = jnp.var(x, axis=axis, keepdims=True)
    return (x - m) / jnp.sqrt(v + eps)

def _scatter_add(tgt, idx, src, axis=0):
    return tgt.at[idx].add(src)

def _segment_sum(src, seg, n):
    return jax.ops.segment_sum(src, seg, n)
kernel_name = 'mk_xattn_seq_d4_seqx_r8_0d7540'

def setup_inputs(seed: int=0):
    np.random.seed(seed)
    _w = jnp.asarray

    def _rec_inputs():
        import jax
        import jax.numpy as jnp
        _rk = jax.random.key(seed)
        x = -0.0002928 + 1 * jax.random.normal(jax.random.fold_in(_rk, 1), (8, 128, 128), jnp.float32)
        _lenS = 128 - jax.random.randint(jax.random.fold_in(_rk, 7), (8,), 0, max(1, 128 // 4) + 1, jnp.int32)
        _lenS2 = 128 - jax.random.randint(jax.random.fold_in(_rk, 8), (8,), 0, max(1, 128 // 4) + 1, jnp.int32)
        _ctx_1024P = jax.random.normal(jax.random.fold_in(_rk, 11), (8, 16, 128), jnp.float32)
        _ctx_1024c = jax.random.dirichlet(jax.random.fold_in(_rk, 511), 0.3 * jnp.ones((16,), jnp.float32), (8, 128))
        _ctx_1024t = jnp.einsum('bsk,bkd->bsd', _ctx_1024c, _ctx_1024P)
        _ctx_1024t = _ctx_1024t * jax.lax.rsqrt(jnp.mean(jnp.square(_ctx_1024t)) + 1e-12) * 0.953939
        ctx_1024 = -1.39393e-06 + 0.999914 * (_ctx_1024t + 0.3 * jax.random.normal(jax.random.fold_in(_rk, 611), (8, 128, 128), jnp.float32))
        _validS = jnp.arange(128)[None, :] < _lenS[:, None]
        _validS2 = jnp.arange(128)[None, :] < _lenS2[:, None]
        _causal = jnp.tril(jnp.ones((128, 128), dtype=bool))
        mask_BxS2_ff1 = jnp.where(jnp.ones((8, 128), dtype=bool), 1.0, 0.0).astype(jnp.float32)
        return (x, ctx_1024, mask_BxS2_ff1)
    x, ctx_1024, mask_BxS2_ff1 = _rec_inputs()

    def _L0_xattn_setup():
        import jax, jax.numpy as jnp
        import numpy as np
        NUM_HEADS = 16
        EMBED_DIM = 128
        HEAD_DIM = EMBED_DIM // NUM_HEADS
        N_LAYERS = 12
        B, TQ, TK = (2, 256, 256)

        def _layer_norm(x, gamma, beta, eps=1e-05):
            mean = jnp.mean(x, axis=-1, keepdims=True)
            var = jnp.var(x, axis=-1, keepdims=True)
            return (x - mean) * jax.lax.rsqrt(var + eps) * gamma + beta
        key = jax.random.key(seed)
        ks = jax.random.split(key, 8)
        target = jax.random.normal(ks[0], (B, TQ, EMBED_DIM), dtype=jnp.float32)
        context = jax.random.normal(ks[1], (B, TK, EMBED_DIM), dtype=jnp.float32)
        pad_mask = jnp.ones((B, TK), dtype=jnp.float32)
        std = 0.02
        wq = std * jax.random.normal(ks[2], (EMBED_DIM, EMBED_DIM), dtype=jnp.float32)
        wk = std * jax.random.normal(ks[3], (EMBED_DIM, EMBED_DIM), dtype=jnp.float32)
        wv = std * jax.random.normal(ks[4], (EMBED_DIM, EMBED_DIM), dtype=jnp.float32)
        proj_std = 0.02 / np.sqrt(2.0 * N_LAYERS)
        wo = proj_std * jax.random.normal(ks[5], (EMBED_DIM, EMBED_DIM), dtype=jnp.float32)
        bo = jnp.zeros((EMBED_DIM,), dtype=jnp.float32)
        ln_gamma = jnp.ones((EMBED_DIM,), dtype=jnp.float32)
        ln_beta = jnp.zeros((EMBED_DIM,), dtype=jnp.float32)
        return {'target': target, 'context': context, 'pad_mask': pad_mask, 'wq': wq, 'wk': wk, 'wv': wv, 'wo': wo, 'bo': bo, 'ln_gamma': ln_gamma, 'ln_beta': ln_beta}
    _L0_xattn_all = _L0_xattn_setup()
    _L0_xattn_in = {k: v for k, v in _L0_xattn_all.items() if k in ('wq', 'wk', 'wv', 'wo', 'bo', 'ln_gamma', 'ln_beta')}
    del _L0_xattn_all

    def _L1_xattn_setup():
        import jax, jax.numpy as jnp
        import numpy as np
        B, Q, KV = (2, 256, 256)
        D_MODEL = 128
        N_HEADS = 16
        D_KV = 64
        EPS = 1e-06
        key = jax.random.key(seed)
        ks = jax.random.split(key, 7)
        s = 0.02
        return {'hidden_states': jax.random.normal(ks[0], (B, Q, D_MODEL), jnp.float32), 'key_value_states': jax.random.normal(ks[1], (B, KV, D_MODEL), jnp.float32), 'wq': jax.random.normal(ks[2], (D_MODEL, N_HEADS * D_KV), jnp.float32) * s, 'wk': jax.random.normal(ks[3], (D_MODEL, N_HEADS * D_KV), jnp.float32) * s, 'wv': jax.random.normal(ks[4], (D_MODEL, N_HEADS * D_KV), jnp.float32) * s, 'wo': jax.random.normal(ks[5], (N_HEADS * D_KV, D_MODEL), jnp.float32) * s, 'norm_w': jnp.ones((D_MODEL,), jnp.float32)}
    _L1_xattn_all = _L1_xattn_setup()
    _L1_xattn_in = {k: v for k, v in _L1_xattn_all.items() if k in ('wq', 'wk', 'wv', 'wo', 'norm_w')}
    del _L1_xattn_all

    def _L2_xattn_setup():
        import jax, jax.numpy as jnp
        import numpy as np
        D_MODEL = 128
        N_HEADS = 16
        D_FF = 512
        BLOCK = 64
        ROUTER_H = 128
        NEG = -1000000000.0

        def _layernorm(x, g, b, eps=1e-05):
            mu = x.mean(-1, keepdims=True)
            var = ((x - mu) ** 2).mean(-1, keepdims=True)
            return (x - mu) * jax.lax.rsqrt(var + eps) * g + b

        def _block_sparse_self_attn(x, qkv_w, sa_out_w, sa_out_b, r_w1, r_b1, r_w2, r_b2):
            B, S, D = x.shape
            H, Dh = (N_HEADS, D // N_HEADS)
            nb = S // BLOCK
            qkv = x @ qkv_w.T
            q, k, v = jnp.split(qkv, 3, axis=-1)
            q = q.reshape(B, S, H, Dh).transpose(0, 2, 1, 3)
            kh = k.reshape(B, S, H, Dh).transpose(0, 2, 1, 3)
            vh = v.reshape(B, S, H, Dh).transpose(0, 2, 1, 3)
            scores = jnp.einsum('bhqd,bhkd->bhqk', q, kh) / jnp.sqrt(jnp.float32(D))
            block_repr = k.reshape(B, nb, BLOCK, D).mean(axis=2)
            r = jax.nn.relu(block_repr @ r_w1.T + r_b1) @ r_w2.T + r_b2
            keep0 = jax.nn.sigmoid(r[0, :, 0]) > 0.5
            allowed = keep0[:, None] & keep0[None, :]
            allowed_pos = jnp.repeat(jnp.repeat(allowed, BLOCK, 0), BLOCK, 1)
            scores = jnp.where(allowed_pos[None, None], scores, NEG)
            causal = jnp.triu(jnp.ones((S, S), bool), k=1)
            scores = jnp.where(causal[None, None], -jnp.inf, scores)
            p = jax.nn.softmax(scores, axis=-1)
            out = jnp.einsum('bhqk,bhkd->bhqd', p, vh)
            out = out.transpose(0, 2, 1, 3).reshape(B, S, D)
            return out @ sa_out_w.T + sa_out_b

        def _mha_cross(q_in, kv_in, in_w, in_b, out_w, out_b):
            B, S, D = q_in.shape
            M = kv_in.shape[1]
            H, Dh = (N_HEADS, D // N_HEADS)
            wq, wk, wv = jnp.split(in_w, 3, axis=0)
            bq, bk, bv = jnp.split(in_b, 3, axis=0)
            q = (q_in @ wq.T + bq).reshape(B, S, H, Dh).transpose(0, 2, 1, 3)
            k = (kv_in @ wk.T + bk).reshape(B, M, H, Dh).transpose(0, 2, 1, 3)
            v = (kv_in @ wv.T + bv).reshape(B, M, H, Dh).transpose(0, 2, 1, 3)
            scores = jnp.einsum('bhqd,bhkd->bhqk', q, k) / jnp.sqrt(jnp.float32(Dh))
            p = jax.nn.softmax(scores, axis=-1)
            out = jnp.einsum('bhqk,bhkd->bhqd', p, v).transpose(0, 2, 1, 3).reshape(B, S, D)
            return out @ out_w.T + out_b
        key = jax.random.key(seed)
        ks = jax.random.split(key, 24)
        B, S, M, D = (2, 256, 128, D_MODEL)
        s = lambda k, shape, fan: jax.random.normal(k, shape, jnp.float32) * (1.0 / np.sqrt(fan))
        return {'tgt': jax.random.normal(ks[0], (B, S, D), jnp.float32), 'memory': jax.random.normal(ks[1], (B, M, D), jnp.float32), 'qkv_w': s(ks[2], (3 * D, D), D), 'sa_out_w': s(ks[3], (D, D), D), 'sa_out_b': jnp.zeros((D,), jnp.float32), 'r_w1': s(ks[4], (ROUTER_H, D), D), 'r_b1': jnp.zeros((ROUTER_H,), jnp.float32), 'r_w2': s(ks[5], (1, ROUTER_H), ROUTER_H), 'r_b2': jnp.zeros((1,), jnp.float32), 'ca_in_w': s(ks[6], (3 * D, D), D), 'ca_in_b': jnp.zeros((3 * D,), jnp.float32), 'ca_out_w': s(ks[7], (D, D), D), 'ca_out_b': jnp.zeros((D,), jnp.float32), 'ff_w1': s(ks[8], (D_FF, D), D), 'ff_b1': jnp.zeros((D_FF,), jnp.float32), 'ff_w2': s(ks[9], (D, D_FF), D_FF), 'ff_b2': jnp.zeros((D,), jnp.float32), 'n1_g': jnp.ones((D,), jnp.float32), 'n1_b': jnp.zeros((D,), jnp.float32), 'n2_g': jnp.ones((D,), jnp.float32), 'n2_b': jnp.zeros((D,), jnp.float32), 'n3_g': jnp.ones((D,), jnp.float32), 'n3_b': jnp.zeros((D,), jnp.float32)}
    _L2_xattn_all = _L2_xattn_setup()
    _L2_xattn_in = {k: v for k, v in _L2_xattn_all.items() if k in ('qkv_w', 'sa_out_w', 'sa_out_b', 'r_w1', 'r_b1', 'r_w2', 'r_b2', 'ca_in_w', 'ca_in_b', 'ca_out_w', 'ca_out_b', 'ff_w1', 'ff_b1', 'ff_w2', 'ff_b2', 'n1_g', 'n1_b', 'n2_g', 'n2_b', 'n3_g', 'n3_b')}
    del _L2_xattn_all

    def _L3_xattn_setup():
        import jax, jax.numpy as jnp
        import numpy as np
        B, S, D, H = (2, 256, 128, 16)
        E = D // H
        LN_EPS = 1e-05

        def _attention(q, k, v, Wq, bq, Wk, bk, Wv, bv, Wo, bo, gamma, beta):
            qh = jnp.einsum('bsd,hde->bhse', q, Wq) + bq[None, :, None, :]
            kh = jnp.einsum('bsd,hde->bhse', k, Wk) + bk[None, :, None, :]
            vh = jnp.einsum('bsd,hde->bhse', v, Wv) + bv[None, :, None, :]
            scale = jnp.asarray(E, qh.dtype) ** 0.5
            scores = jnp.einsum('bhse,bhte->bhst', qh, kh) / scale
            attn = jax.nn.softmax(scores, axis=-1)
            ctx = jnp.einsum('bhst,bhte->bhse', attn, vh)
            cat = ctx.transpose(0, 2, 1, 3).reshape(q.shape[0], q.shape[1], H * E)
            out = cat @ Wo + bo
            x = q + out
            mu = jnp.mean(x, axis=-1, keepdims=True)
            var = jnp.mean((x - mu) ** 2, axis=-1, keepdims=True)
            return (x - mu) * jax.lax.rsqrt(var + LN_EPS) * gamma + beta
        key = jax.random.key(seed)
        ks = jax.random.split(key, 12)
        s_in = 1.0 / np.sqrt(D)
        s_cat = 1.0 / np.sqrt(H * E)
        return {'q': jax.random.normal(ks[0], (B, S, D), jnp.float32), 'k': jax.random.normal(ks[1], (B, S, D), jnp.float32), 'v': jax.random.normal(ks[2], (B, S, D), jnp.float32), 'Wq': jax.random.uniform(ks[3], (H, D, E), jnp.float32, -s_in, s_in), 'bq': jax.random.uniform(ks[4], (H, E), jnp.float32, -s_in, s_in), 'Wk': jax.random.uniform(ks[5], (H, D, E), jnp.float32, -s_in, s_in), 'bk': jax.random.uniform(ks[6], (H, E), jnp.float32, -s_in, s_in), 'Wv': jax.random.uniform(ks[7], (H, D, E), jnp.float32, -s_in, s_in), 'bv': jax.random.uniform(ks[8], (H, E), jnp.float32, -s_in, s_in), 'Wo': jax.random.uniform(ks[9], (H * E, D), jnp.float32, -s_cat, s_cat), 'bo': jax.random.uniform(ks[10], (D,), jnp.float32, -s_cat, s_cat), 'gamma': jnp.ones((D,), jnp.float32), 'beta': jnp.zeros((D,), jnp.float32)}
    _L3_xattn_all = _L3_xattn_setup()
    _L3_xattn_in = {k: v for k, v in _L3_xattn_all.items() if k in ('Wq', 'bq', 'Wk', 'bk', 'Wv', 'bv', 'Wo', 'bo', 'gamma', 'beta')}
    del _L3_xattn_all
    return {'x': x, 'ctx_1024': ctx_1024, 'mask_BxS2_ff1': mask_BxS2_ff1, 'L0_xattn_wq': _L0_xattn_in['wq'], 'L0_xattn_wk': _L0_xattn_in['wk'], 'L0_xattn_wv': _L0_xattn_in['wv'], 'L0_xattn_wo': _L0_xattn_in['wo'], 'L0_xattn_bo': _L0_xattn_in['bo'], 'L0_xattn_ln_gamma': _L0_xattn_in['ln_gamma'], 'L0_xattn_ln_beta': _L0_xattn_in['ln_beta'], 'L1_xattn_wq': _L1_xattn_in['wq'], 'L1_xattn_wk': _L1_xattn_in['wk'], 'L1_xattn_wv': _L1_xattn_in['wv'], 'L1_xattn_wo': _L1_xattn_in['wo'], 'L1_xattn_norm_w': _L1_xattn_in['norm_w'], 'L2_xattn_qkv_w': _L2_xattn_in['qkv_w'], 'L2_xattn_sa_out_w': _L2_xattn_in['sa_out_w'], 'L2_xattn_sa_out_b': _L2_xattn_in['sa_out_b'], 'L2_xattn_r_w1': _L2_xattn_in['r_w1'], 'L2_xattn_r_b1': _L2_xattn_in['r_b1'], 'L2_xattn_r_w2': _L2_xattn_in['r_w2'], 'L2_xattn_r_b2': _L2_xattn_in['r_b2'], 'L2_xattn_ca_in_w': _L2_xattn_in['ca_in_w'], 'L2_xattn_ca_in_b': _L2_xattn_in['ca_in_b'], 'L2_xattn_ca_out_w': _L2_xattn_in['ca_out_w'], 'L2_xattn_ca_out_b': _L2_xattn_in['ca_out_b'], 'L2_xattn_ff_w1': _L2_xattn_in['ff_w1'], 'L2_xattn_ff_b1': _L2_xattn_in['ff_b1'], 'L2_xattn_ff_w2': _L2_xattn_in['ff_w2'], 'L2_xattn_ff_b2': _L2_xattn_in['ff_b2'], 'L2_xattn_n1_g': _L2_xattn_in['n1_g'], 'L2_xattn_n1_b': _L2_xattn_in['n1_b'], 'L2_xattn_n2_g': _L2_xattn_in['n2_g'], 'L2_xattn_n2_b': _L2_xattn_in['n2_b'], 'L2_xattn_n3_g': _L2_xattn_in['n3_g'], 'L2_xattn_n3_b': _L2_xattn_in['n3_b'], 'L3_xattn_Wq': _L3_xattn_in['Wq'], 'L3_xattn_bq': _L3_xattn_in['bq'], 'L3_xattn_Wk': _L3_xattn_in['Wk'], 'L3_xattn_bk': _L3_xattn_in['bk'], 'L3_xattn_Wv': _L3_xattn_in['Wv'], 'L3_xattn_bv': _L3_xattn_in['bv'], 'L3_xattn_Wo': _L3_xattn_in['Wo'], 'L3_xattn_bo': _L3_xattn_in['bo'], 'L3_xattn_gamma': _L3_xattn_in['gamma'], 'L3_xattn_beta': _L3_xattn_in['beta']}

def reference(x, ctx_1024, mask_BxS2_ff1, L0_xattn_wq, L0_xattn_wk, L0_xattn_wv, L0_xattn_wo, L0_xattn_bo, L0_xattn_ln_gamma, L0_xattn_ln_beta, L1_xattn_wq, L1_xattn_wk, L1_xattn_wv, L1_xattn_wo, L1_xattn_norm_w, L2_xattn_qkv_w, L2_xattn_sa_out_w, L2_xattn_sa_out_b, L2_xattn_r_w1, L2_xattn_r_b1, L2_xattn_r_w2, L2_xattn_r_b2, L2_xattn_ca_in_w, L2_xattn_ca_in_b, L2_xattn_ca_out_w, L2_xattn_ca_out_b, L2_xattn_ff_w1, L2_xattn_ff_b1, L2_xattn_ff_w2, L2_xattn_ff_b2, L2_xattn_n1_g, L2_xattn_n1_b, L2_xattn_n2_g, L2_xattn_n2_b, L2_xattn_n3_g, L2_xattn_n3_b, L3_xattn_Wq, L3_xattn_bq, L3_xattn_Wk, L3_xattn_bk, L3_xattn_Wv, L3_xattn_bv, L3_xattn_Wo, L3_xattn_bo, L3_xattn_gamma, L3_xattn_beta):
    import jax
    import jax.numpy as jnp

    def _L0_xattn_ref(target, context, pad_mask, wq, wk, wv, wo, bo, ln_gamma, ln_beta):
        import jax, jax.numpy as jnp
        import numpy as np
        NUM_HEADS = 16
        EMBED_DIM = 128
        HEAD_DIM = EMBED_DIM // NUM_HEADS
        N_LAYERS = 12
        B, TQ, TK = (2, 256, 256)

        def _layer_norm(x, gamma, beta, eps=1e-05):
            mean = jnp.mean(x, axis=-1, keepdims=True)
            var = jnp.var(x, axis=-1, keepdims=True)
            return (x - mean) * jax.lax.rsqrt(var + eps) * gamma + beta
        b, tq, d = target.shape
        tk = context.shape[1]
        resid = target
        q = (target @ wq).reshape(b, tq, NUM_HEADS, HEAD_DIM)
        k = (context @ wk).reshape(b, tk, NUM_HEADS, HEAD_DIM)
        v = (context @ wv).reshape(b, tk, NUM_HEADS, HEAD_DIM)
        scores = jnp.einsum('bqhd,bkhd->bhqk', q, k) * (1.0 / np.sqrt(HEAD_DIM))
        m = pad_mask[:, None, None, :]
        scores = scores * m - (1.0 - m) * jnp.asarray(10000000000.0, scores.dtype)
        attn = jax.nn.softmax(scores, axis=-1)
        out = jnp.einsum('bhqk,bkhd->bqhd', attn, v).reshape(b, tq, d)
        out = out @ wo + bo
        return _layer_norm(out + resid, ln_gamma, ln_beta)

    def _L1_xattn_ref(hidden_states, key_value_states, wq, wk, wv, wo, norm_w):
        import jax, jax.numpy as jnp
        import numpy as np
        B, Q, KV = (2, 256, 256)
        D_MODEL = 128
        N_HEADS = 16
        D_KV = 64
        EPS = 1e-06
        var = jnp.mean(jnp.square(hidden_states), axis=-1, keepdims=True)
        normed = hidden_states * jax.lax.rsqrt(var + EPS) * norm_w
        b, q_len, _ = hidden_states.shape
        kv_len = key_value_states.shape[1]

        def split_heads(x):
            return x.reshape(b, -1, N_HEADS, D_KV).transpose(0, 2, 1, 3)
        q = split_heads(normed @ wq)
        k = split_heads(key_value_states @ wk)
        v = split_heads(key_value_states @ wv)
        scores = jnp.einsum('bhqd,bhkd->bhqk', q, k)
        attn = jax.nn.softmax(scores.astype(jnp.float32), axis=-1).astype(scores.dtype)
        ctx = jnp.einsum('bhqk,bhkd->bhqd', attn, v)
        ctx = ctx.transpose(0, 2, 1, 3).reshape(b, q_len, N_HEADS * D_KV)
        attn_out = ctx @ wo
        return hidden_states + attn_out

    def _L2_xattn_ref(tgt, memory, qkv_w, sa_out_w, sa_out_b, r_w1, r_b1, r_w2, r_b2, ca_in_w, ca_in_b, ca_out_w, ca_out_b, ff_w1, ff_b1, ff_w2, ff_b2, n1_g, n1_b, n2_g, n2_b, n3_g, n3_b):
        import jax, jax.numpy as jnp
        import numpy as np
        D_MODEL = 128
        N_HEADS = 16
        D_FF = 512
        BLOCK = 64
        ROUTER_H = 128
        NEG = -1000000000.0

        def _layernorm(x, g, b, eps=1e-05):
            mu = x.mean(-1, keepdims=True)
            var = ((x - mu) ** 2).mean(-1, keepdims=True)
            return (x - mu) * jax.lax.rsqrt(var + eps) * g + b

        def _block_sparse_self_attn(x, qkv_w, sa_out_w, sa_out_b, r_w1, r_b1, r_w2, r_b2):
            B, S, D = x.shape
            H, Dh = (N_HEADS, D // N_HEADS)
            nb = S // BLOCK
            qkv = x @ qkv_w.T
            q, k, v = jnp.split(qkv, 3, axis=-1)
            q = q.reshape(B, S, H, Dh).transpose(0, 2, 1, 3)
            kh = k.reshape(B, S, H, Dh).transpose(0, 2, 1, 3)
            vh = v.reshape(B, S, H, Dh).transpose(0, 2, 1, 3)
            scores = jnp.einsum('bhqd,bhkd->bhqk', q, kh) / jnp.sqrt(jnp.float32(D))
            block_repr = k.reshape(B, nb, BLOCK, D).mean(axis=2)
            r = jax.nn.relu(block_repr @ r_w1.T + r_b1) @ r_w2.T + r_b2
            keep0 = jax.nn.sigmoid(r[0, :, 0]) > 0.5
            allowed = keep0[:, None] & keep0[None, :]
            allowed_pos = jnp.repeat(jnp.repeat(allowed, BLOCK, 0), BLOCK, 1)
            scores = jnp.where(allowed_pos[None, None], scores, NEG)
            causal = jnp.triu(jnp.ones((S, S), bool), k=1)
            scores = jnp.where(causal[None, None], -jnp.inf, scores)
            p = jax.nn.softmax(scores, axis=-1)
            out = jnp.einsum('bhqk,bhkd->bhqd', p, vh)
            out = out.transpose(0, 2, 1, 3).reshape(B, S, D)
            return out @ sa_out_w.T + sa_out_b

        def _mha_cross(q_in, kv_in, in_w, in_b, out_w, out_b):
            B, S, D = q_in.shape
            M = kv_in.shape[1]
            H, Dh = (N_HEADS, D // N_HEADS)
            wq, wk, wv = jnp.split(in_w, 3, axis=0)
            bq, bk, bv = jnp.split(in_b, 3, axis=0)
            q = (q_in @ wq.T + bq).reshape(B, S, H, Dh).transpose(0, 2, 1, 3)
            k = (kv_in @ wk.T + bk).reshape(B, M, H, Dh).transpose(0, 2, 1, 3)
            v = (kv_in @ wv.T + bv).reshape(B, M, H, Dh).transpose(0, 2, 1, 3)
            scores = jnp.einsum('bhqd,bhkd->bhqk', q, k) / jnp.sqrt(jnp.float32(Dh))
            p = jax.nn.softmax(scores, axis=-1)
            out = jnp.einsum('bhqk,bhkd->bhqd', p, v).transpose(0, 2, 1, 3).reshape(B, S, D)
            return out @ out_w.T + out_b
        x = _layernorm(tgt, n1_g, n1_b)
        tgt = tgt + _block_sparse_self_attn(x, qkv_w, sa_out_w, sa_out_b, r_w1, r_b1, r_w2, r_b2)
        x = _layernorm(tgt, n2_g, n2_b)
        tgt = tgt + _mha_cross(x, memory, ca_in_w, ca_in_b, ca_out_w, ca_out_b)
        x = _layernorm(tgt, n3_g, n3_b)
        ff = jax.nn.relu(x @ ff_w1.T + ff_b1) @ ff_w2.T + ff_b2
        return tgt + ff

    def _L3_xattn_ref(q, k, v, Wq, bq, Wk, bk, Wv, bv, Wo, bo, gamma, beta):
        import jax, jax.numpy as jnp
        import numpy as np
        B, S, D, H = (2, 256, 128, 16)
        E = D // H
        LN_EPS = 1e-05

        def _attention(q, k, v, Wq, bq, Wk, bk, Wv, bv, Wo, bo, gamma, beta):
            qh = jnp.einsum('bsd,hde->bhse', q, Wq) + bq[None, :, None, :]
            kh = jnp.einsum('bsd,hde->bhse', k, Wk) + bk[None, :, None, :]
            vh = jnp.einsum('bsd,hde->bhse', v, Wv) + bv[None, :, None, :]
            scale = jnp.asarray(E, qh.dtype) ** 0.5
            scores = jnp.einsum('bhse,bhte->bhst', qh, kh) / scale
            attn = jax.nn.softmax(scores, axis=-1)
            ctx = jnp.einsum('bhst,bhte->bhse', attn, vh)
            cat = ctx.transpose(0, 2, 1, 3).reshape(q.shape[0], q.shape[1], H * E)
            out = cat @ Wo + bo
            x = q + out
            mu = jnp.mean(x, axis=-1, keepdims=True)
            var = jnp.mean((x - mu) ** 2, axis=-1, keepdims=True)
            return (x - mu) * jax.lax.rsqrt(var + LN_EPS) * gamma + beta
        return _attention(q, k, v, Wq, bq, Wk, bk, Wv, bv, Wo, bo, gamma, beta)
    x = _L0_xattn_ref(x, ctx_1024, mask_BxS2_ff1, L0_xattn_wq, L0_xattn_wk, L0_xattn_wv, L0_xattn_wo, L0_xattn_bo, L0_xattn_ln_gamma, L0_xattn_ln_beta)
    x = _L1_xattn_ref(x, ctx_1024, L1_xattn_wq, L1_xattn_wk, L1_xattn_wv, L1_xattn_wo, L1_xattn_norm_w)
    x = _L2_xattn_ref(x, ctx_1024, L2_xattn_qkv_w, L2_xattn_sa_out_w, L2_xattn_sa_out_b, L2_xattn_r_w1, L2_xattn_r_b1, L2_xattn_r_w2, L2_xattn_r_b2, L2_xattn_ca_in_w, L2_xattn_ca_in_b, L2_xattn_ca_out_w, L2_xattn_ca_out_b, L2_xattn_ff_w1, L2_xattn_ff_b1, L2_xattn_ff_w2, L2_xattn_ff_b2, L2_xattn_n1_g, L2_xattn_n1_b, L2_xattn_n2_g, L2_xattn_n2_b, L2_xattn_n3_g, L2_xattn_n3_b)
    x = _L3_xattn_ref(x, ctx_1024, ctx_1024, L3_xattn_Wq, L3_xattn_bq, L3_xattn_Wk, L3_xattn_bk, L3_xattn_Wv, L3_xattn_bv, L3_xattn_Wo, L3_xattn_bo, L3_xattn_gamma, L3_xattn_beta)
    return x

_drawn_inputs = setup_inputs


def setup_inputs(seed=0):
    import zlib

    import numpy as np

    out = dict(_drawn_inputs(seed))
    spreads = {'L0_xattn_bo': (0.0, 0.1),
     'L0_xattn_ln_gamma': (1.0, 0.2),
     'L0_xattn_ln_beta': (0.0, 0.1),
     'L1_xattn_norm_w': (1.0, 0.6),
     'L2_xattn_sa_out_b': (0.0, 0.1),
     'L2_xattn_r_b1': (0.0, 0.1),
     'L2_xattn_ca_in_b': (0.0, 0.1),
     'L2_xattn_ca_out_b': (0.0, 0.1),
     'L2_xattn_ff_b1': (0.0, 0.1),
     'L2_xattn_ff_b2': (0.0, 0.1),
     'L2_xattn_n1_g': (1.0, 0.2),
     'L2_xattn_n1_b': (0.0, 0.1),
     'L2_xattn_n2_g': (1.0, 0.2),
     'L2_xattn_n2_b': (0.0, 0.377),
     'L2_xattn_n3_g': (1.0, 0.2),
     'L2_xattn_n3_b': (0.0, 0.1),
     'L3_xattn_gamma': (1.0, 0.2),
     'L3_xattn_beta': (0.0, 0.1)}
    factors = {'L0_xattn_wq': 8.0,
     'L0_xattn_wk': 8.0,
     'L0_xattn_wv': 8.0,
     'L0_xattn_wo': 8.0,
     'L1_xattn_wq': 5.553,
     'L1_xattn_wk': 5.522,
     'L2_xattn_r_w1': 3.232,
     'L2_xattn_r_w2': 3.232,
     'L3_xattn_bq': 42.52,
     'L3_xattn_bk': 64.0}
    for name, (base, spread) in spreads.items():
        noise = np.random.default_rng([zlib.crc32(name.encode()), seed]).standard_normal(out[name].shape)
        drawn = base * np.exp(spread * noise) if base else spread * noise
        out[name] = jnp.asarray(drawn.astype(out[name].dtype))
    for name, factor in factors.items():
        out[name] = (out[name] * factor).astype(out[name].dtype)
    return out
```

```python
from contextlib import ExitStack

import numpy as np

import concourse.bass as bass
from concourse import mybir

P = 128
B = 8
T = B * P
HALF = T // 2
H = 16
E = 8
HD = 64
NT = H * HD // P
FF = 512
BLOCK = 64
SLOT = 160

F32 = mybir.dt.float32
BF16 = mybir.dt.bfloat16
ACT = mybir.ActivationFunctionType
ALU = mybir.AluOpType
AX = mybir.AxisListType

Q_SLOTS = (0, 0, 0, 1, 1, 2)
K_SLOTS = (0, 1, 2, 0, 1, 0)
ROW_ZERO = E * len(Q_SLOTS)
ROW_KEY = 64
ROW_MAX = 96
ROW_BLOCK = ROW_MAX + 3
PAD = -1e10
NEG = -float(2 ** 30)
CAUSAL = -1e30

MATS = ["q0", "k0", "v0", "o0", "q2", "k2", "v2", "o2", "qc", "kc", "vc", "oc", "q3", "k3", "v3",
        "o3", "r1", "q1", "k1", "v1", "o1", "f1", "f2"]
WIDTH = {"q1": H * HD, "k1": H * HD, "v1": H * HD, "o1": H * HD, "f1": FF, "f2": FF}
MAT_AT = {}
_at = 0
for _m in MATS:
    MAT_AT[_m] = (_at, _at + WIDTH.get(_m, P))
    _at += WIDTH.get(_m, P)
N_MAT = _at
COLS = ["norm_w", "n1_g", "n1_b", "n2_g", "n2_b", "n3_g", "n3_b", "bq_c", "bk_c", "bq_3", "bk_3",
        "r_b1", "r_w2", "r_b2", "f_b0", "f_b1", "f_b2", "f_b3"]
ROWS = ["bo_0", "g_0", "b_0", "bo_2", "bv_c", "bo_c", "b_ff", "bv_3", "bo_3", "g_3", "b_3"]


def build(nc, xt_d, x_d, ctxt_d, mask_d, wmat_d, wcol_d, wrow_d, out_d):
    ctx = ExitStack()
    with ctx:
        def sb(name, shape, dt=F32):
            return ctx.enter_context(nc.sbuf_tensor(name, shape, dt))

        sems = {}

        def sem(name):
            if name not in sems:
                sems[name] = ctx.enter_context(nc.semaphore(name))
            return sems[name]

        wmat = sb("wmat", [P, N_MAT])
        wcol = sb("wcol", [P, len(COLS)])
        wrow = sb("wrow", [P, len(ROWS) * P])
        x = sb("x", [P, B, P])
        resid = sb("resid", [P, B, P])
        xn = sb("xn", [P, B, P])
        xnT = sb("xnT", [P, T])
        ctxT = sb("ctxT", [P, T])
        pad = xn[:, :, :].rearrange("p b t -> p (b t)")
        stackA = sb("stackA", [P, H * T], BF16)
        stackB = sb("stackB", [P, H * T], BF16)
        region = sb("region", [P, 8832])
        parts = sb("parts", [P, 6, T], BF16)
        rest = sb("rest", [P, 4, HALF])
        probs = sb("probs", [P, 2, T])
        vall = sb("vall", [P, B, P])
        vpad = sb("vpad", [P, 2, 4, SLOT])
        opad = sb("opad", [P, SLOT])
        onorm = sb("onorm", [P, 2, P])
        rsum = sb("rsum", [P, 2, P])
        maxs = sb("maxs", [P, 2, H])
        mres = sb("mres", [P, 2, 2, H])
        mparts = sb("mparts", [P, 2, 3, H], BF16)
        mrow = sb("mrow", [3 * H, 2, P], BF16)
        stats6 = sb("stats6", [P, B, 6])
        stats = sb("stats", [P, B, 2])
        rstd = sb("rstd", [P, B])
        half_ = sb("half_", [P, B])
        small = sb("small", [P, 8])
        keep = sb("keep", [P, 2])
        keepn = sb("keepn", [P, 3, 2])
        identF = sb("identF", [P, P])
        identB = sb("identB", [P, P], BF16)
        causal = sb("causal", [P, 2, HALF], BF16)
        zeros = sb("zeros", [P, T], BF16)
        ones = sb("ones", [P, T], BF16)
        rows = sb("rows", [H, 3, T], BF16)
        stackC = region[:, 0:8192].bitcast(BF16)
        qdiag = stackA[:, 0:8192].bitcast(F32).rearrange("p (t e q) -> p t e q", e=2, q=P)
        kdiag = stackA[:, 8192:16384].bitcast(F32).rearrange("p (t e q) -> p t e q", e=2, q=P)
        psum = ctx.enter_context(nc.psum_tensor("psum", [P, 8, 512], F32))

        def bank(n, k=1):
            return psum[:, n, :] if k == 1 else psum[:, n:n + k, :].rearrange("p a n -> p (a n)")

        def mat(name):
            return wmat[:, MAT_AT[name][0]:MAT_AT[name][1]]

        def col(name):
            i = COLS.index(name)
            return wcol[:, i:i + 1]

        def row(name, n=1):
            i = ROWS.index(name)
            return wrow[:, i * P:(i + 1) * P].unsqueeze(1).broadcast_to([P, n, P])

        def tok(ap):
            return ap.rearrange("p (b t) -> p b t", t=P)

        class Layer:
            def __init__(self, n, q, k, v, o, scale, kstack, k_in, v_in, bq=None, bk=None, bv=None,
                         self_attn=False, padded=False):
                self.n, self.q, self.k, self.v, self.o = n, q, k, v, o
                self.scale, self.kstack, self.k_in, self.v_in = scale, kstack, k_in, v_in
                self.bq, self.bk, self.bv = bq, bk, bv
                self.self_attn, self.padded = self_attn, padded

            PER = dict(q_mm=2, k_mm=2, v_mm=2, q_p0=2, q_p1=2, q_p2=2, k_p0=2, k_p1=2, k_p2=2, q_rest=2,
                       k_rest=2, q_stacked0=96, q_stacked1=96, k_stacked0=96, k_stacked1=96, smax_mm=2 * B,
                       max_done=2 * B, msplit=4 * B, mparts=B, mT_mm=B, mT_read=B, mrow_in0=8 * B, mrow_in1=8 * B,
                       s_mm=2 * B, exp_done=2 * B, pv_mm=2 * B, vpad_in=B, v_out=2, rsum=B, onorm=B,
                       z_mm=B, z_read=B, q_kept=0, k_kept=0, rows_done=0)

            def sem(self, what):
                return sem(what)

            def past(self, what):
                return ["L0", "L2", "LC", "L3"].index(self.n) * self.PER[what]

        L0 = Layer("L0", "q0", "k0", "v0", "o0", E ** -0.5, stackB, pad, ctxT, padded=True)
        L2 = Layer("L2", "q2", "k2", "v2", "o2", P ** -0.5, stackC, xnT, xnT, self_attn=True)
        LC = Layer("LC", "qc", "kc", "vc", "oc", E ** -0.5, stackB, ctxT, ctxT, "bq_c", "bk_c", "bv_c")
        L3 = Layer("L3", "q3", "k3", "v3", "o3", E ** -0.5, stackC, ctxT, ctxT, "bq_3", "bk_3", "bv_3")

        def heads(e):
            return [(s, 2 * e + s // 4, s % 4) for s in range(8)]

        def pe_kv(e, L):
            for g in range(2):
                mm = e.matmul(bank(2 + g), mat(L.k), L.k_in[:, g * HALF:(g + 1) * HALF], start=True, stop=True)
                mm.then_inc(L.sem("k_mm"), 1)
            for g in range(2):
                for b in range(4):
                    at = (4 * g + b) * P
                    mm = e.matmul(bank(4 + g)[:, b * P:(b + 1) * P], L.v_in[:, at:at + P], mat(L.v),
                                  start=True, stop=True)
                mm.then_inc(L.sem("v_mm"), 1)

        def pe_q(e, L, source):
            for g in range(2):
                e.matmul(bank(6 + g), mat(L.q), source[:, g * HALF:(g + 1) * HALF],
                         start=True, stop=True).then_inc(L.sem("q_mm"), 1)

        def src_of(L, which, g):
            if L.self_attn:
                return rest[:, 2 + (g if which else g), :] if False else None
            return bank((2 if which else 6) + g)

        def act_split(e, L, which):
            name = "qk"[which]
            bias = L.bk if which else L.bq
            for g in range(2):
                e.wait_ge(L.sem(f"{name}_mm"), L.past(f"{name}_mm") + g + 1)
                if L.self_attn:
                    e.wait_ge(L.sem(f"{name}_kept"), L.past(f"{name}_kept") + g + 1)
                    src = masked(which, g)
                else:
                    src = bank((2 if which else 6) + g)
                e.activation(parts[:, 3 * which, g * HALF:(g + 1) * HALF], src, ACT.Identity,
                             bias=col(bias) if bias else 0.0).then_inc(L.sem(f"{name}_p0"), 1)

        def masked(which, g):
            return probs[:, which, g * HALF:(g + 1) * HALF]

        def dve_split(e, L, which):
            name = "qk"[which]
            bias = L.bk if which else L.bq
            for g in range(2):
                if L.self_attn:
                    e.wait_ge(L.sem(f"{name}_mm"), L.past(f"{name}_mm") + g + 1)
                    e.tensor_tensor(
                        masked(which, g).rearrange("p (b c t) -> p b c t", c=2, t=BLOCK),
                        bank((2 if which else 6) + g).rearrange("p (b c t) -> p b c t", c=2, t=BLOCK),
                        keep[:, :].unsqueeze(1).unsqueeze(3).broadcast_to([P, 4, 2, BLOCK]),
                        ALU.mult).then_inc(L.sem(f"{name}_kept"), 1)
                    src = masked(which, g)
                else:
                    src = bank((2 if which else 6) + g)
                e.wait_ge(L.sem(f"{name}_p0"), L.past(f"{name}_p0") + g + 1)
                e.scalar_tensor_tensor(out=rest[:, 2 * which + g, :], in0=src,
                                       scalar=col(bias) if bias else 0.0,
                                       in1=parts[:, 3 * which, g * HALF:(g + 1) * HALF],
                                       op0=ALU.add, op1=ALU.subtract).then_inc(L.sem(f"{name}_rest"), 1)

        def pool_split(e, L, which):
            name = "qk"[which]
            for g in range(2):
                e.wait_ge(L.sem(f"{name}_rest"), L.past(f"{name}_rest") + g + 1)
                at = slice(g * HALF, (g + 1) * HALF)
                e.tensor_copy(parts[:, 3 * which + 1, at], rest[:, 2 * which + g, :])\
                 .then_inc(L.sem(f"{name}_p1"), 1)
                e.wait_ge(L.sem(f"{name}_p1"), L.past(f"{name}_p1") + g + 1)
                e.tensor_tensor(parts[:, 3 * which + 2, at], rest[:, 2 * which + g, :],
                                parts[:, 3 * which + 1, at], ALU.subtract).then_inc(L.sem(f"{name}_p2"), 1)

        def sync_stack(e, L, which, g):
            name = "qk"[which]
            stack = L.kstack if which else stackA
            slots = K_SLOTS if which else Q_SLOTS
            at = slice(g * HALF, (g + 1) * HALF)
            for n, part in sorted(enumerate(slots), key=lambda s: s[1]):
                e.wait_ge(L.sem(f"{name}_p{part}"), L.past(f"{name}_p{part}") + g + 1)
                e.dma_start(stack_rows(stack, E * n, E)[:, :, at], parts[:, 3 * which + part, at])\
                 .then_inc(L.sem(f"{name}_stacked{g}"), 16)

        def stack_rows(stack, r, n):
            return stack[r:r + n, :].rearrange("d (h t) -> d h t", h=H)

        N_ST = 16 * len(Q_SLOTS)

        def pe_scores_max(e, L, b):
            if b == 0:
                e.wait_ge(L.sem("q_stacked0"), L.past("q_stacked0") + N_ST)
                e.wait_ge(L.sem("k_stacked0"), L.past("k_stacked0") + N_ST)
                for extra, count in L.extra:
                    e.wait_ge(sem(extra), count)
                e.wait_ge(L.sem("v_out"), L.past("v_out") + 2)
                e.wait_ge(L.sem("q_rest"), L.past("q_rest") + 2)
                e.wait_ge(L.sem("k_rest"), L.past("k_rest") + 2)
                if L.self_attn:
                    e.wait_ge(L.sem("rows_done"), L.past("rows_done") + 1)
            if b == 4:
                e.wait_ge(L.sem("q_stacked1"), L.past("q_stacked1") + N_ST)
                e.wait_ge(L.sem("k_stacked1"), L.past("k_stacked1") + N_ST)
            for half in range(2):
                if b >= 1:
                    e.wait_ge(L.sem("max_done"), L.past("max_done") + 2 * b + half - 1)
                for s, i, j in heads(half):
                    at = (4 * i + j) * T + b * P
                    first = not L.self_attn or s % 4 == 0
                    mm = e.matmul(bank(2 * half, 2)[:, s * P:(s + 1) * P], stackA[:, at:at + P],
                                  L.kstack[:, at:at + P], start=(s % 4 == 0 or not L.self_attn),
                                  stop=not L.self_attn, skip_group_check=True)
                    if L.self_attn and s % 4 == 3:
                        mm = e.matmul(bank(2 * half + s // 4), identB[:, :], causal[:, 0, :],
                                      start=False, stop=True, skip_group_check=True)
                mm.then_inc(L.sem("smax_mm"), 1)

        def pe_max_rows(e, L, b):
            e.wait_ge(L.sem("mparts"), L.past("mparts") + b + 1)
            if b >= 3:
                e.wait_ge(L.sem("z_read"), L.past("z_read") + b - 2)
            t = bank(6 + (b + 1) % 2)[0:3 * H, 384:384 + P // 2].bitcast(BF16)
            e.transpose(t, mparts[:, b % 2, :, :].rearrange("p a h -> p (a h)"), identB[:, :])\
             .then_inc(L.sem("mT_mm"), 1)

        def pe_scores(e, L, b, half):
            if half == 0:
                e.wait_ge(L.sem(f"mrow_in{b % 2}"), L.past(f"mrow_in{b % 2}") + 16 * (b // 2 + 1))
            if 2 * b + half >= 1:
                e.wait_ge(L.sem("exp_done"), L.past("exp_done") + 2 * b + half)
            for s, i, j in heads(half):
                at = (4 * i + j) * T + b * P
                mm = e.matmul(bank(4, 2)[:, s * P:(s + 1) * P], L.kstack[:, at:at + P],
                              stackA[:, at:at + P], start=(s % 4 == 0 or not L.self_attn),
                              stop=not L.self_attn, skip_group_check=True)
                if L.self_attn and s % 4 == 3:
                    mm = e.matmul(bank(4 + s // 4), identB[:, :], causal[:, 1, :],
                                  start=False, stop=True, skip_group_check=True)
            mm.then_inc(L.sem("s_mm"), 1)

        def pe_out(e, L, b, half):
            e.wait_ge(L.sem("exp_done"), L.past("exp_done") + 2 * b + half + 1)
            o = bank(6 + b % 2)
            if half == 0:
                e.wait_ge(L.sem("vpad_in"), L.past("vpad_in") + b + 1)
                if b >= 2:
                    e.wait_ge(L.sem("z_read"), L.past("z_read") + b - 1)
                e.wait_ge(L.sem("mT_read"), L.past("mT_read") + min(b + 2, B))
            for n, (s, i, j) in enumerate(heads(half)):
                pt = probs[:, half, s * P:(s + 1) * P]
                rows_ = slice(32 * j, 32 * j + 32)
                e.matmul(o[rows_, 0:P], vpad[:, b % 2, j, 32 * i:32 * i + 32], pt,
                         start=(i == 0), stop=(i == 3), skip_group_check=True)
            for n, (s, i, j) in enumerate(heads(half)):
                pt = probs[:, half, s * P:(s + 1) * P]
                rows_ = slice(32 * j, 32 * j + 32)
                mm = e.matmul(o[rows_, P:2 * P], opad[:, 32 * i:32 * i + 32], pt,
                              start=False, stop=(i == 3), skip_group_check=True)
            mm.then_inc(L.sem("pv_mm"), 1)

        def pe_z(e, L, b):
            e.wait_ge(L.sem("onorm"), L.past("onorm") + b + 1)
            e.matmul(bank(6 + b % 2)[:, 2 * P:3 * P], onorm[:, b % 2, :], mat(L.o),
                     start=True, stop=True).then_inc(L.sem("z_mm"), 1)

        def pe_attn(e, L):
            for b in range(B + 3):
                if b < B:
                    pe_scores_max(e, L, b)
                if 1 <= b <= B:
                    pe_max_rows(e, L, b - 1)
                if 2 <= b < B + 2:
                    pe_scores(e, L, b - 2, 0)
                if b >= 3:
                    pe_out(e, L, b - 3, 1)
                if 2 <= b < B + 2:
                    pe_scores(e, L, b - 2, 1)
                    pe_out(e, L, b - 2, 0)
                if b >= 3:
                    pe_z(e, L, b - 3)

        def act_max_rows(e, L, b):
            e.wait_ge(L.sem("mT_mm"), L.past("mT_mm") + b + 1)
            if b >= 2:
                e.wait_ge(L.sem(f"mrow_in{b % 2}"), L.past(f"mrow_in{b % 2}") + 16 * (b // 2))
            t = bank(6 + (b + 1) % 2)[0:3 * H, 384:384 + P // 2].bitcast(BF16)
            e.copy(mrow[:, b % 2, :], t).then_inc(L.sem("mT_read"), 1)

        def act_exp(e, L, b, half):
            e.wait_ge(L.sem("s_mm"), L.past("s_mm") + 2 * b + half + 1)
            if b >= 1:
                e.wait_ge(L.sem("pv_mm"), L.past("pv_mm") + 2 * b + half - 1)
            e.activation(probs[:, half, :], bank(4, 2), ACT.Exp, scale=L.scale)\
             .then_inc(L.sem("exp_done"), 1)

        def act_attn(e, L):
            for b in range(B + 2):
                if 1 <= b <= B:
                    act_max_rows(e, L, b - 1)
                if b >= 2:
                    act_exp(e, L, b - 2, 0)
                    act_exp(e, L, b - 2, 1)

        def sync_attn(e, L):
            for b in range(B):
                e.wait_ge(L.sem("mT_read"), L.past("mT_read") + b + 1)
                e.dma_start(stack_rows(stackA, ROW_MAX, 3)[:, :, b * P:(b + 1) * P], mrow[:, b % 2, :])\
                 .then_inc(L.sem(f"mrow_in{b % 2}"), 16)

        def pool_attn(e, L):
            for b in range(B):
                e.wait_ge(L.sem("v_out"), L.past("v_out") + b // 4 + 1)
                if b >= 2:
                    e.wait_ge(L.sem("pv_mm"), L.past("pv_mm") + 2 * b - 2)
                e.tensor_copy(
                    vpad[:, b % 2, :, :].rearrange("p j (i c) -> p j i c", c=40)[:, :, :, 0:E],
                    vall[:, b, :].rearrange("p (j i d) -> p j i d", i=4, d=E)).then_inc(L.sem("vpad_in"), 1)

        def dve_max(e, L, b):
            w = b % 2
            for half in range(2):
                e.wait_ge(L.sem("smax_mm"), L.past("smax_mm") + 2 * b + half + 1)
                e.tensor_reduce(maxs[:, w, 8 * half:8 * half + 8],
                                bank(2 * half, 2).rearrange("p (h k) -> p h k", k=P), AX.X, ALU.max)\
                 .then_inc(L.sem("max_done"), 1)
            dve_split_max(e, L.sem("msplit"), L.past("msplit"), L.sem("max_done"), L.past("max_done"),
                          L.sem("mT_mm"), L.past("mT_mm"), L.sem("mparts"), b)

        def dve_norm(e, L, b):
            o = bank(6 + b % 2)
            e.wait_ge(L.sem("pv_mm"), L.past("pv_mm") + 2 * b + 2)
            e.reciprocal(rsum[:, b % 2, :], o[:, P:2 * P]).then_inc(L.sem("rsum"), 1)
            e.wait_ge(L.sem("rsum"), L.past("rsum") + b + 1)
            if b >= 2:
                e.wait_ge(L.sem("z_mm"), L.past("z_mm") + b - 1)
            e.tensor_tensor(onorm[:, b % 2, :], o[:, 0:P], rsum[:, b % 2, :], ALU.mult)\
             .then_inc(L.sem("onorm"), 1)

        def dve_z(e, L, b):
            e.wait_ge(L.sem("z_mm"), L.past("z_mm") + b + 1)
            e.wait_ge(sem(f"resid_{L.n}"), 1)
            e.tensor_tensor(x[:, b, :], bank(6 + b % 2)[:, 2 * P:3 * P], resid[:, b, :], ALU.add)\
             .then_inc(L.sem("z_read"), 1)
            dve_stats(e, L.n, b, L.sem("z_read"), L.past("z_read"))

        def dve_stats(e, n, b, ready, past=0):
            e.wait_ge(ready, past + b + 1)
            e.bn_stats(stats6[:, b, :], x[:, b, :]).then_inc(sem(f"bn_{n}"), 1)
            e.wait_ge(sem(f"bn_{n}"), b + 1)
            e.bn_aggr(stats[:, b, :], stats6[:, b, :]).then_inc(sem(f"stats_{n}"), 1)

        def dve_attn(e, L):
            for b in range(B + 3):
                if b < B:
                    dve_max(e, L, b)
                if b >= 3:
                    dve_norm(e, L, b - 3)
                    dve_z(e, L, b - 3)

        def dve_v(e, L):
            for g in range(2):
                e.wait_ge(L.sem("v_mm"), L.past("v_mm") + g + 1)
                out, src = vall[:, 4 * g:4 * g + 4, :], tok(bank(4 + g))
                if L.bv:
                    e.tensor_tensor(out, src, row(L.bv, 4), ALU.add).then_inc(L.sem("v_out"), 1)
                else:
                    e.tensor_copy(out, src).then_inc(L.sem("v_out"), 1)

        def pool_resid(e, n, bias, ready=None):
            if ready:
                e.wait_ge(sem(ready[0]), ready[1])
            e.tensor_tensor(resid[:, :, :], x[:, :, :], row(bias, B), ALU.add).then_inc(sem(f"resid_{n}"), 1)

        def pool_rstd(e, n, src, kind, eps):
            e.wait_ge(sem(f"stats_{src}"), B)
            if kind == "rms":
                e.wait_ge(sem(f"msq_{n}"), 2)
                var = half_[:, :]
            else:
                var = stats[:, :, 1]
            e.tensor_scalar(rstd[:, :], var, eps, None, ALU.add).then_inc(sem(f"rs_{n}"), 1)
            e.wait_ge(sem(f"rs_{n}"), 1)
            e.tensor_tensor(rstd[:, :], rstd[:, :], small[:, 0:1].broadcast_to([P, B]), ALU.pow)\
             .then_inc(sem(f"rs_{n}"), 1)

        def dve_xn(e, n, src, kind):
            if kind == "plain":
                return
            if kind == "rms":
                e.wait_ge(sem(f"stats_{src}"), B)
                e.tensor_tensor(half_[:, :], stats[:, :, 0], stats[:, :, 0], ALU.mult).then_inc(sem(f"msq_{n}"), 1)
                e.wait_ge(sem(f"msq_{n}"), 1)
                e.tensor_tensor(half_[:, :], half_[:, :], stats[:, :, 1], ALU.add).then_inc(sem(f"msq_{n}"), 1)
            e.wait_ge(sem(f"rs_{n}"), 2)
            for b in range(B):
                if kind == "rms":
                    e.tensor_scalar(xn[:, b, :], x[:, b, :], rstd[:, b:b + 1], None, ALU.mult)\
                     .then_inc(sem(f"xn_{n}"), 1)
                else:
                    e.tensor_scalar(xn[:, b, :], x[:, b, :], stats[:, b, 0:1], rstd[:, b:b + 1],
                                    ALU.subtract, ALU.mult).then_inc(sem(f"xn_{n}"), 1)

        def pe_turn(e, n, kind):
            from_ = x if kind == "plain" else xn
            for g in range(2):
                for b in range(4):
                    if kind != "plain":
                        e.wait_ge(sem(f"xn_{n}"), 4 * g + b + 1)
                    mm = e.transpose(bank(g)[:, b * P:(b + 1) * P], from_[:, 4 * g + b, :], identF[:, :])
                mm.then_inc(sem(f"turn_{n}"), 1)

        def act_turn(e, n, gain=None, bias=None):
            for g in range(2):
                e.wait_ge(sem(f"turn_{n}"), g + 1)
                e.activation(xnT[:, g * HALF:(g + 1) * HALF], bank(g), ACT.Identity,
                             scale=col(gain) if gain else 1.0, bias=col(bias) if bias else 0.0)\
                 .then_inc(sem(f"xnT_{n}"), 1)

        M1 = {
            "qp": region[:, 0:2048].rearrange("p (t q) -> p t q", q=2 * P),
            "kp": region[:, 2048:4096].rearrange("p (t q) -> p t q", q=2 * P),
            "v": region[:, 4096:6144].rearrange("p (b n) -> p b n", b=2),
            "on": region[:, 6144:7168].rearrange("p (t q) -> p t q", q=P),
            "mr": region[:, 7168:8192].bitcast(BF16),
            "xp": region[:, 8192:8448],
            "cp": region[:, 8448:8704],
            "rs": rest[:, 0, :],
            "ones": region[:, 8704:8704 + HD],
        }
        L1 = lambda what: sem(f"{what}_L1")

        def pe_l1(e, i):
            b0 = 2 * i
            e.wait_ge(L1("staged"), 2 * (i + 1))
            for n in range(2 * NT):
                which, t = n % 2, n // 2
                u = i * NT + t
                if u >= 1:
                    e.wait_ge(L1("k_out" if which else "q_out"), 3 * u)
                if n < 2 and i >= 1:
                    e.wait_ge(L1("max_done"), 4 * i)
                    e.wait_ge(L1("mT_read"), 2 * i)
                w = mat("k1" if which else "q1")[:, t * P:(t + 1) * P]
                e.matmul(bank(n % 2)[:, 0:2 * P], w, M1["cp" if which else "xp"], start=True, stop=True)\
                 .then_inc(L1("qk_mm"), 1)
            for bb in range(2):
                for g in range(2):
                    if i >= 1 or bb or g:
                        e.wait_ge(L1("v_out"), 4 * i + 2 * bb + g)
                    if bb == 0 and g == 0 and i >= 1:
                        e.wait_ge(L1("z_read"), 2 * i)
                    e.matmul(bank(6), M1["cp"][:, bb * P:(bb + 1) * P], mat("v1")[:, g * 512:(g + 1) * 512],
                             start=True, stop=True).then_inc(L1("v_mm"), 1)
            e.wait_ge(L1("q_out"), 3 * NT * (i + 1))
            e.wait_ge(L1("k_out"), 3 * NT * (i + 1))
            e.wait_ge(L1("v_out"), 4 * (i + 1))
            for bb in range(2):
                b = b0 + bb
                if bb:
                    e.wait_ge(L1("mT_read"), b)
                for t in range(NT):
                    if b >= 1 and t % 4 == 0:
                        e.wait_ge(L1("max_done"), 2 * b - 1 + t // 4)
                    mm = e.matmul(bank(t // 2)[:, (t % 2) * 256:(t % 2) * 256 + 256],
                                  M1["qp"][:, t, bb * P:(bb + 1) * P],
                                  kdiag[:, 8 * bb + t, :, :].rearrange("p e q -> p (e q)"),
                                  start=True, stop=True)
                    if t % 4 == 3:
                        mm.then_inc(L1("smax_mm"), 1)
                e.wait_ge(L1("mparts"), b + 1)
                e.transpose(bank(0)[0:3 * H, 0:P // 2].bitcast(BF16),
                            mparts[:, b % 2, :, :].rearrange("p a h -> p (a h)"), identB[:, :])\
                 .then_inc(L1("mT_mm"), 1)
                e.wait_ge(L1(f"mrow_in{b % 2}"), 16 * (b // 2 + 1))
                for half in range(2):
                    if 2 * b + half >= 1:
                        e.wait_ge(L1("exp_done"), 2 * b + half)
                    for g in range(2):
                        e.matmul(bank(4 + g), ones[:, 0:P],
                                 M1["mr"][:, (2 * half + g) * 512:(2 * half + g + 1) * 512],
                                 start=True, stop=False, skip_group_check=True)
                        for tt in range(2):
                            t = 4 * half + 2 * g + tt
                            mm = e.matmul(bank(4 + g)[:, tt * 256:(tt + 1) * 256],
                                          M1["kp"][:, t, bb * P:(bb + 1) * P],
                                          qdiag[:, 8 * bb + t, :, :].rearrange("p e q -> p (e q)"),
                                          start=False, stop=(tt == 1), skip_group_check=True)
                    mm.then_inc(L1("s_mm"), 1)
                    e.wait_ge(L1("exp_done"), 2 * b + half + 1)
                    if 2 * b + half >= 1:
                        e.wait_ge(L1("onorm"), 2 * b + half)
                    for s in range(8):
                        t, pp = s // 2, s % 2
                        h = 8 * half + s
                        e.matmul(bank(6)[HD * pp:HD * pp + HD, t * P:(t + 1) * P],
                                 M1["v"][:, bb, h * HD:(h + 1) * HD], probs[:, half, s * P:(s + 1) * P],
                                 start=True, stop=True)
                    pr = probs[:, half, :].rearrange("p (t e q) -> p t e q", e=2, q=P)
                    for pp in range(2):
                        mm = e.matmul(bank(7)[HD * pp:HD * pp + HD, :], M1["ones"], pr[:, :, pp, :],
                                      start=True, stop=True)
                    mm.then_inc(L1("pv_mm"), 1)
                e.wait_ge(L1("onorm"), 2 * b + 2)
                for t in range(NT):
                    mm = e.matmul(bank(7)[:, 0:P], M1["on"][:, t, :], mat("o1")[:, t * P:(t + 1) * P],
                                  start=(t == 0), stop=(t == NT - 1))
                mm.then_inc(L1("z_mm"), 1)
                e.wait_ge(L1("z_read"), b + 1)

        def qk_copies(e, copy, i, n):
            which, t = n % 2, n // 2
            src = bank(n % 2)[:, 0:2 * P]
            plain = M1["kp" if which else "qp"]
            diag = (kdiag if which else qdiag).rearrange("p (b t) e q -> p b t e q", b=2)
            done = L1("k_out" if which else "q_out")
            copy(plain[:, t, :], src).then_inc(done, 1)
            for h in range(2):
                r = slice(HD * h, HD * h + HD)
                copy(diag[r, :, t, h, :], src[r, :].rearrange("p (b q) -> p b q", b=2)).then_inc(done, 1)

        def act_l1(e, i):
            for n in range(0, 2 * NT, 2):
                e.wait_ge(L1("qk_mm"), 2 * NT * i + n + 1)
                if n == 0 and i >= 1:
                    e.wait_ge(L1("s_mm"), 4 * i)
                if n == 0 and i == 0:
                    e.wait_ge(L1("diag0"), 1)
                qk_copies(e, e.copy, i, n)
            for bb in range(2):
                for g in range(2):
                    e.wait_ge(L1("v_mm"), 4 * i + 2 * bb + g + 1)
                    if i >= 1:
                        e.wait_ge(L1("pv_mm"), 4 * i)
                    e.copy(M1["v"][:, bb, g * 512:(g + 1) * 512], bank(6)).then_inc(L1("v_out"), 1)
            for bb in range(2):
                b = 2 * i + bb
                e.wait_ge(L1("mT_mm"), b + 1)
                if b >= 2:
                    e.wait_ge(L1(f"mrow_in{b % 2}"), 16 * (b // 2))
                e.copy(mrow[:, b % 2, :], bank(0)[0:3 * H, 0:P // 2].bitcast(BF16)).then_inc(L1("mT_read"), 1)
                for half in range(2):
                    e.wait_ge(L1("s_mm"), 2 * b + half + 1)
                    if b >= 1:
                        e.wait_ge(L1("pv_mm"), 2 * b + half - 1)
                    e.activation(probs[:, half, :], bank(4, 2), ACT.Exp).then_inc(L1("exp_done"), 1)

        def dve_l1(e, i):
            for n in range(1, 2 * NT, 2):
                e.wait_ge(L1("qk_mm"), 2 * NT * i + n + 1)
                if n == 1 and i >= 1:
                    e.wait_ge(L1("s_mm"), 4 * i)
                if n == 1 and i == 0:
                    e.wait_ge(L1("diag0"), 1)
                qk_copies(e, e.tensor_copy, i, n)
            for bb in range(2):
                b = 2 * i + bb
                w = b % 2
                for half in range(2):
                    e.wait_ge(L1("smax_mm"), 2 * b + half + 1)
                    e.tensor_reduce(maxs[:, w, 8 * half:8 * half + 8],
                                    bank(2 * half, 2).rearrange("p (h k) -> p h k", k=P), AX.X, ALU.max)\
                     .then_inc(L1("max_done"), 1)
                dve_split_max(e, L1("msplit"), 0, L1("max_done"), 0, L1("mT_mm"), 0, L1("mparts"), b)
                for half in range(2):
                    k = 2 * b + half
                    e.wait_ge(L1("pv_mm"), k + 1)
                    e.reciprocal(M1["rs"], bank(7)).then_inc(L1("rsum"), 1)
                    e.wait_ge(L1("rsum"), k + 1)
                    if b >= 1:
                        e.wait_ge(L1("z_mm"), b)
                    e.tensor_tensor(M1["on"][:, 4 * half:4 * half + 4, :].rearrange("p t q -> p (t q)"),
                                    bank(6), M1["rs"], ALU.mult).then_inc(L1("onorm"), 1)
                e.wait_ge(L1("z_mm"), b + 1)
                e.tensor_tensor(x[:, b, :], bank(7)[:, 0:P], x[:, b, :], ALU.add).then_inc(L1("z_read"), 1)
                dve_stats(e, "L1", b, L1("z_read"))

        def dve_split_max(e, chain, chain0, max_done, max0, read, read0, done, b):
            w = b % 2
            e.wait_ge(max_done, max0 + 2 * b + 2)
            if b >= 2:
                e.wait_ge(read, read0 + b - 1)
            e.tensor_scalar(mparts[:, w, 0, :], maxs[:, w, :], -1.0, None, ALU.mult).then_inc(chain, 1)
            e.wait_ge(chain, chain0 + 4 * b + 1)
            e.tensor_tensor(mres[:, w, 0, :], maxs[:, w, :], mparts[:, w, 0, :], ALU.add).then_inc(chain, 1)
            e.wait_ge(chain, chain0 + 4 * b + 2)
            e.tensor_scalar(mparts[:, w, 1, :], mres[:, w, 0, :], -1.0, None, ALU.mult).then_inc(chain, 1)
            e.wait_ge(chain, chain0 + 4 * b + 3)
            e.tensor_tensor(mres[:, w, 1, :], mres[:, w, 0, :], mparts[:, w, 1, :], ALU.add).then_inc(chain, 1)
            e.wait_ge(chain, chain0 + 4 * b + 4)
            e.tensor_scalar(mparts[:, w, 2, :], mres[:, w, 1, :], -1.0, None, ALU.mult).then_inc(done, 1)

        def sync_l1(e, i):
            for bb in range(2):
                b = 2 * i + bb
                e.wait_ge(L1("mT_read"), b + 1)
                if b >= 1:
                    e.wait_ge(L1("s_mm"), 2 * b)
                e.dma_start(M1["mr"][0:3, :].rearrange("d (h t) -> d h t", h=H), mrow[:, b % 2, :])\
                 .then_inc(L1(f"mrow_in{b % 2}"), 16)

        def pool_l1(e, i):
            if i >= 1:
                e.wait_ge(L1("qk_mm"), 2 * NT * i)
                e.wait_ge(L1("v_mm"), 4 * i)
            else:
                e.wait_ge(sem("xnT_T1"), 2)
            e.tensor_copy(M1["xp"], xnT[:, 2 * i * P:2 * (i + 1) * P]).then_inc(L1("staged"), 1)
            e.tensor_copy(M1["cp"], ctxT[:, 2 * i * P:2 * (i + 1) * P]).then_inc(L1("staged"), 1)

        hT = stackA[:, 0:8192].bitcast(F32).rearrange("p (c t) -> p c t", t=T)

        def pe_ff(e):
            e.wait_ge(sem("xnT_TF"), 2)
            for n in range(8):
                c, g = n // 2, n % 2
                if n >= 4:
                    e.wait_ge(sem("h_out"), n - 3)
                e.matmul(bank(2 + n % 4), mat("f1")[:, c * P:(c + 1) * P], xnT[:, g * HALF:(g + 1) * HALF],
                         start=True, stop=True).then_inc(sem("h_mm"), 1)
            e.wait_ge(sem("h_out"), 8)
            for b in range(B):
                if b >= 2:
                    e.wait_ge(sem("ff_read"), b - 1)
                for c in range(4):
                    mm = e.matmul(bank(b % 2)[:, 0:P], hT[:, c, b * P:(b + 1) * P], mat("f2")[:, c * P:(c + 1) * P],
                                  start=(c == 0), stop=(c == 3))
                mm.then_inc(sem("ff_mm"), 1)

        def act_ff(e):
            for n in range(8):
                c, g = n // 2, n % 2
                e.wait_ge(sem("h_mm"), n + 1)
                e.activation(hT[:, c, g * HALF:(g + 1) * HALF], bank(2 + n % 4), ACT.Relu, bias=col(f"f_b{c}"))\
                 .then_inc(sem("h_out"), 1)

        def dve_ff(e):
            for b in range(B):
                e.wait_ge(sem("ff_mm"), b + 1)
                e.wait_ge(sem("resid_FF"), 1)
                e.tensor_tensor(x[:, b, :], bank(b % 2)[:, 0:P], resid[:, b, :], ALU.add).then_inc(sem("ff_read"), 1)

        L0.extra = [("filled", 16 * 20), ("padrows", 48)]
        L2.extra = [("filledA2", 16 * 6), ("filledC", 16 * 10), ("blockrows", 48)]
        LC.extra = [("clearedQC", 16), ("clearedKC", 16)]
        L3.extra = [("clearedQ3", 16 * 10), ("clearedK3", 16)]

        def fill(e, stack, r, n, src, done):
            for k in range(0, n, E):
                m = min(E, n - k)
                e.dma_start(stack_rows(stack, r + k, m), src[0:m * H, :]).then_inc(done, 16)

        def put_row(e, stack, r, n, src, done):
            e.dma_start(stack_rows(stack, r, n), src).then_inc(done, 16)

        block = ctx.enter_context(nc.Block())

        @block.sync
        def _(e):
            c0 = MAT_AT["q2"][0]
            e.dma_start(xnT[:, :], xt_d).then_inc(sem("in_xT"), 16)
            e.dma_start(wmat[:, 0:c0], wmat_d[:, 0:c0]).then_inc(sem("in_w0"), 16)
            e.dma_start(ctxT[:, :], ctxt_d).then_inc(sem("in_ctx"), 16)
            e.dma_start(pad[:, :], mask_d.partition_broadcast(P)).then_inc(sem("in_mask"), 16)
            e.dma_start(wcol[:, :], wcol_d).then_inc(sem("in_cols"), 16)
            e.dma_start(x[:, :, :], x_d).then_inc(sem("in_x"), 16)
            e.dma_start(wrow[:, :], wrow_d.partition_broadcast(P)).then_inc(sem("in_rows"), 16)
            e.dma_start(wmat[:, c0:N_MAT], wmat_d[:, c0:N_MAT]).then_inc(sem("in_w"), 16)
            e.wait_ge(sem("consts"), 4)
            fill(e, stackA, ROW_ZERO, 16, zeros, sem("filled"))
            fill(e, stackB, ROW_ZERO, 48, zeros, sem("filled"))
            fill(e, stackA, ROW_KEY, 32, ones, sem("filled"))
            fill(e, stackB, ROW_MAX, 32, ones, sem("filled"))
            fill(e, stackA, ROW_MAX, 32, zeros, sem("filled"))
            for g in range(2):
                sync_stack(e, L0, 1, g)
                sync_stack(e, L0, 0, g)
            e.wait_ge(sem("padsplit"), 5)
            e.wait_ge(sem("filled"), 16 * 20)
            for n in range(3):
                put_row(e, stackB, ROW_KEY + n, 1, rows[:, n, :], sem("padrows"))
            sync_attn(e, L0)
            for i in range(B // 2):
                sync_l1(e, i)
            e.wait_ge(L1("z_read"), B)
            fill(e, stackA, ROW_ZERO, 16, zeros, sem("filledA2"))
            fill(e, stackA, ROW_MAX, 32, zeros, sem("filledA2"))
            fill(e, stackC, ROW_ZERO, 48, zeros, sem("filledC"))
            fill(e, stackC, ROW_MAX, 32, ones, sem("filledC"))
            fill(e, stackA, ROW_KEY, 32, ones, sem("filledA2b"))
            e.wait_ge(sem("filledC"), 160)
            e.wait_ge(sem("filledA2"), 96)
            e.wait_ge(sem("filledA2b"), 64)
            e.wait_ge(L2.sem("rows_done"), L2.past("rows_done") + 1)
            put_row(e, stackA, ROW_BLOCK, 1, rows[:, 0, :], sem("blockrows"))
            put_row(e, stackA, ROW_KEY, 1, rows[:, 1, :], sem("blockrows"))
            put_row(e, stackC, ROW_KEY, 1, rows[:, 2, :], sem("blockrows"))
            for g in range(2):
                sync_stack(e, L2, 1, g)
                sync_stack(e, L2, 0, g)
            sync_attn(e, L2)
            e.wait_ge(L2.sem("z_read"), L2.past("z_read") + B)
            put_row(e, stackA, ROW_MAX, 4, zeros[0:4 * H, :], sem("clearedQC"))
            put_row(e, stackB, ROW_KEY, 3, zeros[0:3 * H, :], sem("clearedKC"))
            for g in range(2):
                sync_stack(e, LC, 1, g)
            for g in range(2):
                sync_stack(e, LC, 0, g)
            sync_attn(e, LC)
            e.wait_ge(LC.sem("z_read"), LC.past("z_read") + B)
            put_row(e, stackC, ROW_KEY, 1, zeros[0:H, :], sem("clearedK3"))
            for g in range(2):
                sync_stack(e, L3, 1, g)
            e.wait_ge(sem("ff_read"), B)
            fill(e, stackA, ROW_ZERO, 16 + 32, zeros, sem("clearedQ3"))
            fill(e, stackA, ROW_MAX, 32, zeros, sem("clearedQ3"))
            for g in range(2):
                sync_stack(e, L3, 0, g)
            sync_attn(e, L3)
            for b in range(B):
                e.wait_ge(sem("out_ready"), b + 1)
                e.dma_start(out_d[b], xn[:, b, :]).then_inc(sem("stored"), 16)
            e.wait_ge(sem("stored"), 16 * B)

        @block.gpsimd
        def _(e):
            c = sem("consts")
            e.memset(zeros[:, :], 0.0).then_inc(c, 1)
            e.memset(ones[:, :], 1.0).then_inc(c, 1)
            p = sem("pre")
            e.memset(identF[:, :], 0.0).then_inc(p, 1)
            e.memset(identB[:, :], 0.0).then_inc(p, 1)
            e.wait_ge(p, 2)
            for m in (identF, identB):
                e.affine_select(out=m[:, :], in_=m[:, :], compare_op=ALU.not_equal, fill=1.0,
                                base=0, pattern=[[-1, P]], channel_multiplier=1).then_inc(c, 1)
            e.memset(vpad[:, :, :, :], 0.0).then_inc(p, 1)
            e.memset(opad[:, :], 0.0).then_inc(p, 1)
            e.memset(small[:, 0:1], -0.5).then_inc(p, 1)
            e.memset(causal[:, :, :], 0.0).then_inc(p, 1)
            e.wait_ge(p, 6)
            e.memset(opad[:, :].rearrange("p (i c) -> p i c", c=40)[:, :, 0:E], 1.0).then_inc(c, 1)
            cz = causal[:, :, :].rearrange("p a (h k) -> p a h k", k=P)
            e.affine_select(out=cz[:, 0], in_=cz[:, 0], compare_op=ALU.is_ge, fill=CAUSAL,
                            base=0, pattern=[[0, 4], [-1, P]], channel_multiplier=1).then_inc(c, 1)
            e.affine_select(out=cz[:, 1], in_=cz[:, 1], compare_op=ALU.is_ge, fill=CAUSAL,
                            base=0, pattern=[[0, 4], [1, P]], channel_multiplier=-1).then_inc(c, 1)
            pool_split(e, L0, 1)
            pool_split(e, L0, 0)
            e.wait_ge(sem("in_x"), 16)
            e.wait_ge(sem("in_rows"), 16)
            pool_resid(e, "L0", "bo_0")
            pool_attn(e, L0)
            pool_rstd(e, "N0", "L0", "ln", 1e-5)
            pool_rstd(e, "T1", "X1", "rms", 1e-6)
            e.wait_ge(sem("stats_L0"), B)
            e.memset(stackA[:, :].bitcast(F32), 0.0).then_inc(L1("diag0"), 1)
            e.memset(M1["mr"].bitcast(F32), 0.0).then_inc(L1("zero"), 1)
            e.memset(M1["ones"], 1.0).then_inc(L1("zero"), 1)
            for i in range(B // 2):
                pool_l1(e, i)
            pool_rstd(e, "T2", "L1", "ln", 1e-5)
            pool_resid(e, "L2", "bo_2")
            pool_split(e, L2, 1)
            pool_split(e, L2, 0)
            pool_attn(e, L2)
            pool_rstd(e, "TC", "L2", "ln", 1e-5)
            pool_resid(e, "LC", "bo_c")
            pool_split(e, LC, 1)
            pool_split(e, LC, 0)
            pool_attn(e, LC)
            pool_rstd(e, "TF", "LC", "ln", 1e-5)
            pool_resid(e, "FF", "b_ff")
            pool_split(e, L3, 1)
            e.wait_ge(sem("ff_read"), B)
            pool_resid(e, "L3", "bo_3")
            pool_split(e, L3, 0)
            pool_attn(e, L3)
            pool_rstd(e, "N3", "L3", "ln", 1e-5)

        @block.tensor
        def _(e):
            e.wait_ge(sem("in_w0"), 16)
            e.wait_ge(sem("in_xT"), 16)
            pe_q(e, L0, xnT)
            e.wait_ge(sem("padmul"), 1)
            e.wait_ge(sem("in_ctx"), 16)
            pe_kv(e, L0)
            e.wait_ge(sem("consts"), 7)
            pe_attn(e, L0)
            e.wait_ge(sem("in_w"), 16)
            e.wait_ge(L0.sem("z_read"), L0.past("z_read") + B)
            pe_turn(e, "T1", "rms")
            e.wait_ge(sem("xnT_T1"), 2)
            e.wait_ge(L1("zero"), 2)
            for i in range(B // 2):
                pe_l1(e, i)
            pe_turn(e, "T2", "ln")
            e.wait_ge(sem("xnT_T2"), 2)
            pe_kv(e, L2)
            e.wait_ge(sem("router"), 2)
            e.matmul(bank(0)[:, 0:2], mat("r1"), small[:, 4:6], start=True, stop=True).then_inc(sem("r_mm"), 1)
            e.wait_ge(sem("r_hidden"), 2)
            e.matmul(bank(1)[:, 0:2], rest[:, 0, 0:P], small[:, 6:8], start=True, stop=True).then_inc(sem("r_mm"), 1)
            pe_q(e, L2, xnT)
            pe_attn(e, L2)
            e.wait_ge(L2.sem("z_read"), L2.past("z_read") + B)
            pe_kv(e, LC)
            pe_turn(e, "TC", "ln")
            e.wait_ge(sem("xnT_TC"), 2)
            pe_q(e, LC, xnT)
            pe_attn(e, LC)
            e.wait_ge(LC.sem("z_read"), LC.past("z_read") + B)
            pe_turn(e, "TF", "ln")
            pe_ff(e)
            e.wait_ge(sem("ff_read"), B)
            pe_kv(e, L3)
            pe_turn(e, "T3", "plain")
            e.wait_ge(sem("xnT_T3"), 2)
            pe_q(e, L3, xnT)
            pe_attn(e, L3)

        @block.scalar
        def _(e):
            e.wait_ge(sem("in_cols"), 16)
            act_split(e, L0, 0)
            act_split(e, L0, 1)
            act_attn(e, L0)
            act_turn(e, "T1", "norm_w")
            for i in range(B // 2):
                act_l1(e, i)
            act_turn(e, "T2", "n1_g", "n1_b")
            e.wait_ge(sem("r_mm"), 1)
            e.activation(small[:, 6:8], bank(0)[:, 0:2], ACT.Relu, bias=col("r_b1")).then_inc(sem("r_hidden"), 1)
            act_split(e, L2, 1)
            act_split(e, L2, 0)
            act_attn(e, L2)
            act_split(e, LC, 1)
            act_turn(e, "TC", "n2_g", "n2_b")
            act_split(e, LC, 0)
            act_attn(e, LC)
            act_turn(e, "TF", "n3_g", "n3_b")
            act_ff(e)
            act_split(e, L3, 1)
            act_turn(e, "T3")
            act_split(e, L3, 0)
            act_attn(e, L3)

        @block.vector
        def _(e):
            e.wait_ge(sem("in_mask"), 16)
            ps = sem("padsplit")
            u = rest[0:H, 0:2, :].rearrange("p a n -> p (a n)")
            v = rest[0:H, 2:4, :].rearrange("p a n -> p (a n)")
            e.tensor_scalar(u, pad[0:H, :], -1.0, -PAD / L0.scale, ALU.add, ALU.mult).then_inc(ps, 1)
            e.wait_ge(ps, 1)
            e.tensor_copy(rows[:, 0, :], u).then_inc(ps, 1)
            e.wait_ge(ps, 2)
            e.tensor_tensor(v, u, rows[:, 0, :], ALU.subtract).then_inc(ps, 1)
            e.wait_ge(ps, 3)
            e.tensor_copy(rows[:, 1, :], v).then_inc(ps, 1)
            e.wait_ge(ps, 4)
            e.tensor_tensor(rows[:, 2, :], v, rows[:, 1, :], ALU.subtract).then_inc(ps, 1)
            e.wait_ge(ps, 5)
            e.wait_ge(sem("in_ctx"), 16)
            e.tensor_tensor(pad[:, :], ctxT[:, :], pad[:, :], ALU.mult).then_inc(sem("padmul"), 1)
            e.wait_ge(sem("in_cols"), 16)
            dve_split(e, L0, 0)
            dve_split(e, L0, 1)
            dve_v(e, L0)
            dve_attn(e, L0)
            dve_xn(e, "N0", "L0", "ln")
            e.wait_ge(sem("xn_N0"), B)
            e.tensor_tensor(xn[:, :, :], xn[:, :, :], row("g_0", B), ALU.mult).then_inc(sem("aff"), 1)
            e.wait_ge(sem("aff"), 1)
            e.tensor_tensor(x[:, :, :], xn[:, :, :], row("b_0", B), ALU.add).then_inc(sem("aff"), 1)
            for b in range(B):
                e.wait_ge(sem("aff"), 2)
                e.bn_stats(stats6[:, b, :], x[:, b, :]).then_inc(sem("bn_X1"), 1)
                e.wait_ge(sem("bn_X1"), b + 1)
                e.bn_aggr(stats[:, b, :], stats6[:, b, :]).then_inc(sem("stats_X1"), 1)
            dve_xn(e, "T1", "X1", "rms")
            for i in range(B // 2):
                dve_l1(e, i)
            dve_xn(e, "T2", "L1", "ln")
            e.wait_ge(L2.sem("k_mm"), L2.past("k_mm") + 1)
            e.tensor_reduce(small[:, 2:4], bank(2)[:, 0:P].rearrange("p (c t) -> p c t", c=2), AX.X, ALU.add)\
             .then_inc(sem("router"), 1)
            e.wait_ge(sem("router"), 1)
            e.tensor_scalar(small[:, 4:6], small[:, 2:4], 1.0 / BLOCK, None, ALU.mult).then_inc(sem("router"), 1)
            e.tensor_copy(rest[:, 0, 0:P], col("r_w2").broadcast_to([P, P])).then_inc(sem("r_hidden"), 1)
            e.wait_ge(sem("r_mm"), 2)
            k = sem("keep")
            e.tensor_scalar(keep[:, :], bank(1)[:, 0:2], col("r_b2"), 0.0, ALU.add, ALU.is_gt).then_inc(k, 1)
            e.wait_ge(k, 1)
            e.tensor_scalar(keepn[:, 0, :], keep[:, :], -NEG, NEG, ALU.mult, ALU.add).then_inc(k, 1)
            e.tensor_scalar(keepn[:, 1, :], keep[:, :], NEG, None, ALU.mult).then_inc(k, 1)
            e.tensor_scalar(keepn[:, 2, :], keep[:, :], -1.0, 1.0, ALU.mult, ALU.add).then_inc(k, 1)
            e.wait_ge(k, 4)
            for n in range(3):
                ins = e.tensor_copy(rows[:, n, :].rearrange("p (b c t) -> p b c t", c=2, t=BLOCK),
                                    keepn[0:H, n, :].unsqueeze(1).unsqueeze(3).broadcast_to([H, B, 2, BLOCK]))
                ins.then_inc(L2.sem("rows_done") if n == 2 else k, 1)
            dve_split(e, L2, 1)
            dve_split(e, L2, 0)
            dve_v(e, L2)
            dve_attn(e, L2)
            dve_split(e, LC, 1)
            dve_v(e, LC)
            dve_xn(e, "TC", "L2", "ln")
            dve_split(e, LC, 0)
            dve_attn(e, LC)
            dve_xn(e, "TF", "LC", "ln")
            dve_ff(e)
            dve_split(e, L3, 1)
            dve_v(e, L3)
            dve_split(e, L3, 0)
            dve_attn(e, L3)
            dve_xn(e, "N3", "L3", "ln")
            for b in range(B):
                e.wait_ge(sem("xn_N3"), b + 1)
                e.tensor_tensor(xn[:, b, :], xn[:, b, :], row("g_3")[:, 0, :], ALU.mult).then_inc(sem("aff3"), 1)
                e.wait_ge(sem("aff3"), b + 1)
                e.tensor_tensor(xn[:, b, :], xn[:, b, :], row("b_3")[:, 0, :], ALU.add).then_inc(sem("out_ready"), 1)


def kernel(**inputs):
    import concourse.bacc as _bacc
    from concourse.bass_utils import run_bass_kernel_spmd as _run

    a = {k: np.asarray(v) for k, v in inputs.items()}

    def by_feature(w):
        s = w.shape[:-1]
        return w.reshape(*s, 4, 4, E).swapaxes(-1, -3).reshape(*s, P)

    l2, ca = a["L2_xattn_qkv_w"], a["L2_xattn_ca_in_w"]
    cab = a["L2_xattn_ca_in_b"]
    w3 = {k: a[f"L3_xattn_W{k}"].transpose(1, 0, 2).reshape(P, P) for k in "qkv"}
    mats = {
        "q0": by_feature(a["L0_xattn_wq"]), "k0": by_feature(a["L0_xattn_wk"]),
        "v0": a["L0_xattn_wv"], "o0": a["L0_xattn_wo"],
        "q2": by_feature(l2[0:P].T), "k2": by_feature(l2[P:2 * P].T), "v2": l2[2 * P:].T,
        "o2": a["L2_xattn_sa_out_w"].T,
        "qc": by_feature(ca[0:P].T), "kc": by_feature(ca[P:2 * P].T), "vc": ca[2 * P:].T,
        "oc": a["L2_xattn_ca_out_w"].T,
        "q3": by_feature(w3["q"]), "k3": by_feature(w3["k"]), "v3": w3["v"], "o3": a["L3_xattn_Wo"],
        "r1": by_feature(a["L2_xattn_r_w1"]).T,
        "q1": a["L1_xattn_wq"], "k1": a["L1_xattn_wk"], "v1": a["L1_xattn_wv"],
        "o1": a["L1_xattn_wo"].reshape(NT, P, P).transpose(1, 0, 2).reshape(P, NT * P),
        "f1": a["L2_xattn_ff_w1"].T,
        "f2": a["L2_xattn_ff_w2"].T.reshape(4, P, P).transpose(1, 0, 2).reshape(P, FF),
    }
    fb = a["L2_xattn_ff_b1"].reshape(4, P)
    cols = {
        "norm_w": a["L1_xattn_norm_w"], "bq_c": by_feature(cab[0:P]), "bk_c": by_feature(cab[P:2 * P]),
        "bq_3": by_feature(a["L3_xattn_bq"].reshape(P)), "bk_3": by_feature(a["L3_xattn_bk"].reshape(P)),
        "r_b1": a["L2_xattn_r_b1"], "r_w2": a["L2_xattn_r_w2"].reshape(P),
        "r_b2": np.broadcast_to(a["L2_xattn_r_b2"], (P,)),
        **{f"n{n}_{s}": a[f"L2_xattn_n{n}_{s}"] for n in (1, 2, 3) for s in "gb"},
        **{f"f_b{c}": fb[c] for c in range(4)},
    }
    rows = {
        "bo_0": a["L0_xattn_bo"], "g_0": a["L0_xattn_ln_gamma"], "b_0": a["L0_xattn_ln_beta"],
        "bo_2": a["L2_xattn_sa_out_b"], "bv_c": cab[2 * P:], "bo_c": a["L2_xattn_ca_out_b"],
        "b_ff": a["L2_xattn_ff_b2"], "bv_3": a["L3_xattn_bv"].reshape(P), "bo_3": a["L3_xattn_bo"],
        "g_3": a["L3_xattn_gamma"], "b_3": a["L3_xattn_beta"],
    }
    x = a["x"]
    arrays = {
        "xt": x.transpose(2, 0, 1).reshape(P, T),
        "xtok": x.transpose(1, 0, 2),
        "ctxt": a["ctx_1024"].transpose(2, 0, 1).reshape(P, T),
        "mask": a["mask_BxS2_ff1"].reshape(T),
        "wmat": np.concatenate([mats[m] for m in MATS], axis=1),
        "wcol": np.stack([cols[c] for c in COLS], axis=1),
        "wrow": np.concatenate([rows[r] for r in ROWS]),
    }
    nc = _bacc.Bacc("TRN2", target_bir_lowering=False, num_devices=1)
    args, arr = [], {}
    for name, v in arrays.items():
        arr[f"in_{name}"] = np.ascontiguousarray(v)
        args.append(nc.dram_tensor(f"in_{name}", v.shape, F32, kind="ExternalInput").ap())
    args.append(nc.dram_tensor("out_x", (B, P, P), F32, kind="ExternalOutput").ap())
    build(nc, *args)
    r = _run(nc, [arr], core_ids=[0])
    return r.results[0]["out_x"]
```

```python
from contextlib import ExitStack

import numpy as np

import concourse.bass as bass
from concourse import mybir

P = 128
B = 8
T = B * P
HALF = T // 2
H = 16
E = 8
HD = 64
NT = H * HD // P
FF = 512
BLOCK = 64
STEPS = B + 1
SLOT = 160

F32 = mybir.dt.float32
BF16 = mybir.dt.bfloat16
ACT = mybir.ActivationFunctionType
ALU = mybir.AluOpType
AX = mybir.AxisListType

Q_SLOTS = (0, 0, 0, 1, 1, 2)
K_SLOTS = (0, 1, 2, 0, 1, 0)
ROW_ZERO = E * len(Q_SLOTS)
ROW_KEY = 64
ROW_MAX = 96
ROW_BLOCK = ROW_MAX + 3
PAD = -1e10
NEG = -float(2 ** 30)
CAUSAL = -1e30

MATS = ["q0", "k0", "v0", "o0", "q2", "k2", "v2", "o2", "qc", "kc", "vc", "oc", "q3", "k3", "v3",
        "o3", "r1", "a1", "v1", "o1", "f1", "f2"]
WIDTH = {"a1": 2 * H * HD, "v1": H * HD, "o1": H * HD, "f1": FF, "f2": FF}
MAT_AT = {}
_at = 0
for _m in MATS:
    MAT_AT[_m] = (_at, _at + WIDTH.get(_m, P))
    _at += WIDTH.get(_m, P)
N_MAT = _at
COLS = ["norm_w", "n1_g", "n1_b", "n2_g", "n2_b", "n3_g", "n3_b", "bq_c", "bk_c", "bq_3", "bk_3",
        "r_b1", "r_w2", "r_b2", "f_b0", "f_b1", "f_b2", "f_b3"]
ROWS = ["bo_0", "g_0", "b_0", "bo_2", "bv_c", "bo_c", "b_ff", "bv_3", "bo_3", "g_3", "b_3"]


def build(nc, xt_d, x_d, ctxt_d, mask_d, wmat_d, wcol_d, wrow_d, out_d):
    ctx = ExitStack()
    with ctx:
        def sb(name, shape, dt=F32):
            return ctx.enter_context(nc.sbuf_tensor(name, shape, dt))

        sems = {}

        def sem(name):
            if name not in sems:
                sems[name] = ctx.enter_context(nc.semaphore(name))
            return sems[name]

        wmat = sb("wmat", [P, N_MAT])
        wcol = sb("wcol", [P, len(COLS)])
        wrow = sb("wrow", [P, len(ROWS) * P])
        x = sb("x", [P, B, P])
        resid = sb("resid", [P, B, P])
        xn = sb("xn", [P, B, P])
        xnT = sb("xnT", [P, T])
        ctxT = sb("ctxT", [P, T])
        pad = xn[:, :, :].rearrange("p b t -> p (b t)")
        stackA = sb("stackA", [P, H * T], BF16)
        stackB = sb("stackB", [P, H * T], BF16)
        region = sb("region", [P, 8832])
        parts = sb("parts", [P, 6, T], BF16)
        rest = sb("rest", [P, 4, HALF])
        rest4 = rest[:, :, :].rearrange("p (w g) n -> p w g n", w=2)
        probs = sb("probs", [P, 2, T])
        vall = sb("vall", [P, B, P])
        vpad = sb("vpad", [P, 2, 4, SLOT])
        opad = sb("opad", [P, SLOT])
        onorm = sb("onorm", [P, 2, P])
        rsum = sb("rsum", [P, 2, P])
        maxs = sb("maxs", [P, 2, H])
        mres = sb("mres", [P, 2, 2, H])
        mparts = sb("mparts", [P, 2, 3, H], BF16)
        mrow = sb("mrow", [3 * H, 2, P], BF16)
        stats6 = sb("stats6", [P, B, 6])
        stats = sb("stats", [P, B, 2])
        rstd = sb("rstd", [P, B])
        half_ = sb("half_", [P, B])
        small = sb("small", [P, 8])
        keep = sb("keep", [P, 2])
        keepn = sb("keepn", [P, 3, 2])
        identF = sb("identF", [P, P])
        identB = sb("identB", [P, P], BF16)
        causal = sb("causal", [P, 2, HALF], BF16)
        zeros = sb("zeros", [P, T], BF16)
        ones = sb("ones", [P, T], BF16)
        rows = sb("rows", [H, 3, T], BF16)
        stackC = region[:, 0:8192].bitcast(BF16)
        psum = ctx.enter_context(nc.psum_tensor("psum", [P, 8, 512], F32))

        def bank(n, k=1):
            return psum[:, n, :] if k == 1 else psum[:, n:n + k, :].rearrange("p a n -> p (a n)")

        def mat(name):
            return wmat[:, MAT_AT[name][0]:MAT_AT[name][1]]

        def col(name):
            i = COLS.index(name)
            return wcol[:, i:i + 1]

        def row(name, n=1):
            i = ROWS.index(name)
            return wrow[:, i * P:(i + 1) * P].unsqueeze(1).broadcast_to([P, n, P])

        def tok(ap):
            return ap.rearrange("p (b t) -> p b t", t=P)

        class Layer:
            def __init__(self, n, q, k, v, o, scale, kstack, k_in, v_in, bq=None, bk=None, bv=None,
                         self_attn=False, padded=False):
                self.n, self.q, self.k, self.v, self.o = n, q, k, v, o
                self.scale, self.kstack, self.k_in, self.v_in = scale, kstack, k_in, v_in
                self.bq, self.bk, self.bv = bq, bk, bv
                self.self_attn, self.padded = self_attn, padded
                self.prev = None

            PER = dict(q_mm=2, k_mm=2, v_mm=2, q_p0=2, q_p1=2, q_p2=2, k_p0=2, k_p1=2, k_p2=2, q_rest=2,
                       k_rest=2, q_stacked0=96, q_stacked1=96, k_stacked0=96, k_stacked1=96, smax_mm=2 * B,
                       max_done=2 * B, msplit=4 * B, mparts=B, mT_mm=B, mT_read=B, mrow_in0=8 * B, mrow_in1=8 * B,
                       s_mm=2 * B, exp_done=2 * B, pv_mm=2 * B, vpad_in=B, v_out=2, rsum=B, onorm=B,
                       z_mm=B, z_read=B, q_kept=0, k_kept=0)

            def sem(self, what):
                return sem(what)

            def past(self, what):
                return ["L0", "L2", "LC", "L3"].index(self.n) * self.PER[what]

            def before(self, b, n):
                return ["L0", "L2", "LC", "L3"].index(self.n) * B + b >= n

            def behind(self, b, lag):
                if lag <= b < B + lag:
                    return self, b - lag
                if b < lag and self.prev and b + STEPS - lag < B:
                    return self.prev, b + STEPS - lag
                return None

            def bank_of(self, what, g):
                if self.n == "L0":
                    return {"k": 2, "v": 4, "q": 6}[what] + g
                if self.n == "L2" and g == 0:
                    return 7
                return {"k": 3, "v": 3, "q": 2}[what] if self.n == "L2" else {"k": 2, "v": 2 + g, "q": 3}[what]

        L0 = Layer("L0", "q0", "k0", "v0", "o0", E ** -0.5, stackB, pad, ctxT, padded=True)
        L2 = Layer("L2", "q2", "k2", "v2", "o2", P ** -0.5, stackB, xnT, xnT, self_attn=True)
        LC = Layer("LC", "qc", "kc", "vc", "oc", E ** -0.5, stackC, ctxT, ctxT, "bq_c", "bk_c", "bv_c")
        LC.prev = L2
        L3 = Layer("L3", "q3", "k3", "v3", "o3", E ** -0.5, stackB, ctxT, ctxT, "bq_3", "bk_3", "bv_3")

        def heads(e):
            return [(s, 2 * e + s // 4, s % 4) for s in range(8)]

        def pe_k(e, L, g):
            e.matmul(bank(L.bank_of("k", g)), mat(L.k), L.k_in[:, g * HALF:(g + 1) * HALF],
                     start=True, stop=True).then_inc(L.sem("k_mm"), 1)

        def pe_v(e, L, g):
            for b in range(4):
                at = (4 * g + b) * P
                mm = e.matmul(bank(L.bank_of("v", g))[:, b * P:(b + 1) * P], L.v_in[:, at:at + P], mat(L.v),
                              start=True, stop=True)
            mm.then_inc(L.sem("v_mm"), 1)

        def pe_q(e, L, g):
            e.matmul(bank(L.bank_of("q", g)), mat(L.q), xnT[:, g * HALF:(g + 1) * HALF],
                     start=True, stop=True).then_inc(L.sem("q_mm"), 1)

        kept = mat("a1").rearrange("p (w g n) -> p w g n", w=2, g=2)

        def source(L, name, g):
            return kept[:, "qk".index(name), g, :] if L.self_attn else bank(L.bank_of(name, g))

        def left(L, name, g):
            return (kept if L.self_attn else rest4)[:, "qk".index(name), g, :]

        def part(name, n, g):
            return parts[:, 3 * "qk".index(name) + n, g * HALF:(g + 1) * HALF]

        def wait_half(e, L, what, g):
            e.wait_ge(L.sem(what), L.past(what) + g + 1)

        def act_p0(e, L, name, g):
            wait_half(e, L, f"{name}_kept" if L.self_attn else f"{name}_mm", g)
            bias = L.bk if name == "k" else L.bq
            e.activation(part(name, 0, g), source(L, name, g), ACT.Identity,
                         bias=col(bias) if bias else 0.0).then_inc(L.sem(f"{name}_p0"), 1)

        def act_p1(e, L, name, g):
            wait_half(e, L, f"{name}_rest", g)
            e.copy(part(name, 1, g), left(L, name, g)).then_inc(L.sem(f"{name}_p1"), 1)

        def dve_kept(e, L, name, g, src=None):
            if src is None:
                wait_half(e, L, f"{name}_mm", g)
                src = bank(L.bank_of(name, g))
            e.tensor_tensor(
                source(L, name, g).rearrange("p (b c t) -> p b c t", c=2, t=BLOCK),
                src.rearrange("p (b c t) -> p b c t", c=2, t=BLOCK),
                keep[:, :].unsqueeze(1).unsqueeze(3).broadcast_to([P, 4, 2, BLOCK]),
                ALU.mult).then_inc(L.sem(f"{name}_kept"), 1)

        def dve_rest(e, L, name, g):
            bias = L.bk if name == "k" else L.bq
            wait_half(e, L, f"{name}_p0", g)
            e.scalar_tensor_tensor(out=left(L, name, g), in0=source(L, name, g),
                                   scalar=col(bias) if bias else 0.0, in1=part(name, 0, g),
                                   op0=ALU.add, op1=ALU.subtract).then_inc(L.sem(f"{name}_rest"), 1)

        def dve_p2(e, L, name, g):
            wait_half(e, L, f"{name}_p1", g)
            e.tensor_tensor(part(name, 2, g), left(L, name, g), part(name, 1, g), ALU.subtract)\
             .then_inc(L.sem(f"{name}_p2"), 1)

        def dve_v(e, L, g):
            wait_half(e, L, "v_mm", g)
            out, src = L.vall[:, 4 * g:4 * g + 4, :], tok(bank(L.bank_of("v", g)))
            if L.bv:
                e.tensor_tensor(out, src, row(L.bv, 4), ALU.add).then_inc(L.sem("v_out"), 1)
            else:
                e.tensor_copy(out, src).then_inc(L.sem("v_out"), 1)

        def sync_stack(e, L, name, g):
            stack = L.kstack if name == "k" else stackA
            slots = K_SLOTS if name == "k" else Q_SLOTS
            at = slice(g * HALF, (g + 1) * HALF)
            for n, p in sorted(enumerate(slots), key=lambda s: s[1]):
                wait_half(e, L, f"{name}_p{p}", g)
                e.dma_start(stack_rows(stack, E * n, E)[:, :, at], part(name, p, g))\
                 .then_inc(L.sem(f"{name}_stacked{g}"), 16)

        def stack_rows(stack, r, n):
            return stack[r:r + n, :].rearrange("d (h t) -> d h t", h=H)

        N_ST = 16 * len(Q_SLOTS)

        def pe_scores_max(e, L, b, half):
            if b % 4 == 0 and half == 0:
                g = b // 4
                for what in (f"q_stacked{g}", f"k_stacked{g}"):
                    e.wait_ge(L.sem(what), L.past(what) + N_ST)
            for name, count in (L.extra2 if half else L.extra).get(b, []):
                e.wait_ge(sem(name), count)
            if L.before(b, 1):
                e.wait_ge(L.sem("max_done"), L.past("max_done") + 2 * b + half - 1)
            for s, i, j in heads(half):
                at = (4 * i + j) * T + b * P
                mm = e.matmul(bank(2 * half, 2)[:, s * P:(s + 1) * P], stackA[:, at:at + P],
                              L.kstack[:, at:at + P], start=(s % 4 == 0 or not L.self_attn),
                              stop=not L.self_attn, skip_group_check=True)
                if L.self_attn and s % 4 == 3:
                    mm = e.matmul(bank(2 * half + s // 4), identB[:, :], causal[:, 0, :],
                                  start=False, stop=True, skip_group_check=True)
            mm.then_inc(L.sem("smax_mm"), 1)

        def pe_max_rows(e, L, b):
            e.wait_ge(L.sem("mparts"), L.past("mparts") + b + 1)
            if L.before(b, 3):
                e.wait_ge(L.sem("z_read"), L.past("z_read") + b - 2)
            t = bank(6 + (b + 1) % 2)[0:3 * H, 384:384 + P // 2].bitcast(BF16)
            e.transpose(t, mparts[:, b % 2, :, :].rearrange("p a h -> p (a h)"), identB[:, :])\
             .then_inc(L.sem("mT_mm"), 1)

        def pe_scores(e, L, b, half):
            if half == 0:
                e.wait_ge(L.sem(f"mrow_in{b % 2}"), L.past(f"mrow_in{b % 2}") + 16 * (b // 2 + 1))
            if L.before(b, 1) or half:
                e.wait_ge(L.sem("exp_done"), L.past("exp_done") + 2 * b + half)
            for s, i, j in heads(half):
                at = (4 * i + j) * T + b * P
                mm = e.matmul(bank(4, 2)[:, s * P:(s + 1) * P], L.kstack[:, at:at + P],
                              stackA[:, at:at + P], start=(s % 4 == 0 or not L.self_attn),
                              stop=not L.self_attn, skip_group_check=True)
                if L.self_attn and s % 4 == 3:
                    mm = e.matmul(bank(4 + s // 4), identB[:, :], causal[:, 1, :],
                                  start=False, stop=True, skip_group_check=True)
            mm.then_inc(L.sem("s_mm"), 1)

        def pe_out(e, L, b, half, turned):
            e.wait_ge(L.sem("exp_done"), L.past("exp_done") + 2 * b + half + 1)
            o = bank(6 + b % 2)
            if half == 0:
                e.wait_ge(L.sem("vpad_in"), L.past("vpad_in") + b + 1)
                if L.before(b, 2):
                    e.wait_ge(L.sem("z_read"), L.past("z_read") + b - 1)
            e.wait_ge(L.sem("mT_read"), turned)
            for n, (s, i, j) in enumerate(heads(half)):
                pt = probs[:, half, s * P:(s + 1) * P]
                rows_ = slice(32 * j, 32 * j + 32)
                e.matmul(o[rows_, 0:P], vpad[:, b % 2, j, 32 * i:32 * i + 32], pt,
                         start=(i == 0), stop=(i == 3), skip_group_check=True)
            for n, (s, i, j) in enumerate(heads(half)):
                pt = probs[:, half, s * P:(s + 1) * P]
                rows_ = slice(32 * j, 32 * j + 32)
                mm = e.matmul(o[rows_, P:2 * P], opad[:, 32 * i:32 * i + 32], pt,
                              start=False, stop=(i == 3), skip_group_check=True)
            mm.then_inc(L.sem("pv_mm"), 1)

        def pe_z(e, L, b):
            e.wait_ge(L.sem("onorm"), L.past("onorm") + b + 1)
            e.matmul(bank(6 + b % 2)[:, 2 * P:3 * P], onorm[:, b % 2, :], mat(L.o),
                     start=True, stop=True).then_inc(L.sem("z_mm"), 1)

        def product_of(L, b):
            it = L.behind(b, 4)
            return it if it and it[1] < B - 1 else None

        def pe_attn(e, L, steps, before=None, between=None, after=None):
            for b in range(steps):
                late, last, product = L.behind(b, 2), L.behind(b, 3), product_of(L, b)
                turned = L.past("mT_read") + min(b, B)
                joint = L.prev and b < 2
                if before:
                    before(b)
                if b < B and not joint:
                    pe_scores_max(e, L, b, 0)
                if product:
                    pe_z(e, *product)
                if b < B and not joint:
                    pe_scores_max(e, L, b, 1)
                if late:
                    pe_scores(e, *late, 0)
                if 1 <= b <= B and not joint:
                    pe_max_rows(e, L, b - 1)
                if between:
                    between(b)
                if last:
                    pe_out(e, *last, 1, turned - (b == 1 if L.prev else 0))
                if late:
                    pe_scores(e, *late, 1)
                    pe_out(e, *late, 0, turned)
                if joint:
                    pe_scores_max(e, L, b, 0)
                    pe_scores_max(e, L, b, 1)
                if joint and b == 1:
                    e.wait_ge(last[0].sem("onorm"), last[0].past("onorm") + B)
                    pe_max_rows(e, L, 0)
                    e.wait_ge(L.sem("mT_read"), turned)
                if last and last[1] == B - 1:
                    pe_z(e, *last)
                if after:
                    after(b)

        def act_max_rows(e, L, b):
            e.wait_ge(L.sem("mT_mm"), L.past("mT_mm") + b + 1)
            if L.before(b, 2):
                e.wait_ge(L.sem(f"mrow_in{b % 2}"), L.past(f"mrow_in{b % 2}") + 16 * (b // 2))
            t = bank(6 + (b + 1) % 2)[0:3 * H, 384:384 + P // 2].bitcast(BF16)
            e.copy(mrow[:, b % 2, :], t).then_inc(L.sem("mT_read"), 1)

        def act_exp(e, L, b, half):
            e.wait_ge(L.sem("s_mm"), L.past("s_mm") + 2 * b + half + 1)
            if L.before(b, 1):
                e.wait_ge(L.sem("pv_mm"), L.past("pv_mm") + 2 * b + half - 1)
            e.activation(probs[:, half, :], bank(4, 2), ACT.Exp, scale=L.scale)\
             .then_inc(L.sem("exp_done"), 1)

        def act_attn(e, L, steps, before=None, between=None, after=None):
            for b in range(steps):
                late = L.behind(b, 2)
                if before:
                    before(b)
                if 1 <= b <= B:
                    act_max_rows(e, L, b - 1)
                if late:
                    act_exp(e, *late, 0)
                if between:
                    between(b)
                if late:
                    act_exp(e, *late, 1)
                if after:
                    after(b)

        def sync_rows(e, L, b):
            e.wait_ge(L.sem("mT_read"), L.past("mT_read") + b + 1)
            e.dma_start(stack_rows(stackA, ROW_MAX, 3)[:, :, b * P:(b + 1) * P], mrow[:, b % 2, :])\
             .then_inc(L.sem(f"mrow_in{b % 2}"), 16)

        def pool_v(e, L, b):
            e.wait_ge(L.sem("v_out"), L.past("v_out") + b // 4 + 1)
            if L.before(b, 2):
                e.wait_ge(L.sem("pv_mm"), L.past("pv_mm") + 2 * b - 2)
            e.tensor_copy(
                vpad[:, b % 2, :, :].rearrange("p j (i c) -> p j i c", c=40)[:, :, :, 0:E],
                L.vall[:, b, :].rearrange("p (j i d) -> p j i d", i=4, d=E)).then_inc(L.sem("vpad_in"), 1)

        def pool_attn(e, L, steps, before=None, after=None):
            for b in range(steps):
                late = L.behind(b, 2)
                if before:
                    before(b)
                if late:
                    pool_v(e, *late)
                if b < B:
                    pool_split_max(e, L, b)
                if after:
                    after(b)

        def pool_split_max(e, L, b):
            w = b % 2
            chain, n = L.sem("msplit"), L.past("msplit") + 4 * b
            e.wait_ge(L.sem("max_done"), L.past("max_done") + 2 * b + 2)
            if L.before(b, 2):
                e.wait_ge(L.sem("mT_mm"), L.past("mT_mm") + b - 1)
            e.tensor_copy(mparts[:, w, 0, :], maxs[:, w, :]).then_inc(chain, 1)
            e.wait_ge(chain, n + 1)
            e.tensor_tensor(mres[:, w, 0, :], maxs[:, w, :], mparts[:, w, 0, :], ALU.subtract).then_inc(chain, 1)
            e.wait_ge(chain, n + 2)
            e.tensor_copy(mparts[:, w, 1, :], mres[:, w, 0, :]).then_inc(chain, 1)
            e.wait_ge(chain, n + 3)
            e.tensor_tensor(mres[:, w, 1, :], mres[:, w, 0, :], mparts[:, w, 1, :], ALU.subtract).then_inc(chain, 1)
            e.wait_ge(chain, n + 4)
            e.tensor_copy(mparts[:, w, 2, :], mres[:, w, 1, :]).then_inc(L.sem("mparts"), 1)

        def dve_max(e, L, b, half):
            e.wait_ge(L.sem("smax_mm"), L.past("smax_mm") + 2 * b + half + 1)
            if L.before(b, 2) and half == 0:
                e.wait_ge(L.sem("mparts"), L.past("mparts") + b - 1)
            e.tensor_reduce(maxs[:, b % 2, 8 * half:8 * half + 8],
                            bank(2 * half, 2).rearrange("p (h k) -> p h k", k=P), AX.X, ALU.max, negate=True)\
             .then_inc(L.sem("max_done"), 1)

        def dve_norm(e, L, b):
            o = bank(6 + b % 2)
            e.wait_ge(L.sem("pv_mm"), L.past("pv_mm") + 2 * b + 2)
            e.reciprocal(rsum[:, b % 2, :], o[:, P:2 * P]).then_inc(L.sem("rsum"), 1)
            e.wait_ge(L.sem("rsum"), L.past("rsum") + b + 1)
            if L.before(b, 2):
                e.wait_ge(L.sem("z_mm"), L.past("z_mm") + b - 1)
            e.tensor_tensor(onorm[:, b % 2, :], o[:, 0:P], rsum[:, b % 2, :], ALU.mult)\
             .then_inc(L.sem("onorm"), 1)

        def dve_z(e, L, b):
            e.wait_ge(L.sem("z_mm"), L.past("z_mm") + b + 1)
            e.wait_ge(sem(f"resid_{L.n}"), b // 4 + 1)
            e.tensor_tensor(x[:, b, :], bank(6 + b % 2)[:, 2 * P:3 * P], resid[:, b, :], ALU.add)\
             .then_inc(L.sem("z_read"), 1)

        def dve_stats6(e, n, b, ready, past=0):
            e.wait_ge(ready, past + b + 1)
            e.bn_stats(stats6[:, b, :], x[:, b, :]).then_inc(sem(f"bn_{n}"), 1)

        def dve_aggr(e, n, b):
            e.wait_ge(sem(f"bn_{n}"), b + 1)
            e.bn_aggr(stats[:, b, :], stats6[:, b, :]).then_inc(sem(f"stats_{n}"), 1)

        def dve_stats(e, n, b, ready, past=0):
            dve_stats6(e, n, b, ready, past)
            dve_aggr(e, n, b)

        def dve_attn(e, L, steps, before=None, between=None, after=None):
            for b in range(steps):
                last, product = L.behind(b, 3), product_of(L, b)
                joint = last and last[0] is not L
                if before:
                    before(b)
                if product:
                    dve_z(e, *product)
                if joint:
                    dve_norm(e, *last)
                if b < B:
                    dve_max(e, L, b, 0)
                if product:
                    M, p = product
                    dve_stats6(e, M.n, p, M.sem("z_read"), M.past("z_read"))
                if b < B:
                    dve_max(e, L, b, 1)
                if product:
                    dve_aggr(e, M.n, p)
                if between:
                    between(b)
                if last and not joint:
                    dve_norm(e, *last)
                if after:
                    after(b)
                if last and last[1] == B - 1:
                    dve_z(e, *last)
                    dve_stats(e, last[0].n, B - 1, last[0].sem("z_read"), last[0].past("z_read"))

        def pool_resid(e, n, bias, g, ready, count):
            e.wait_ge(sem(ready), count)
            e.tensor_tensor(resid[:, 4 * g:4 * g + 4, :], x[:, 4 * g:4 * g + 4, :], row(bias, 4), ALU.add)\
             .then_inc(sem(f"resid_{n}"), 1)

        def pool_rstd(e, n, src, kind, eps, b0, nb):
            done = sem(f"rs_{n}")
            rs = rstd[:, b0:b0 + nb]
            count = 2 * (b0 // nb) if b0 % nb == 0 else None
            e.wait_ge(sem(f"stats_{src}"), b0 + nb)
            if kind == "rms":
                e.wait_ge(sem(f"msq_{n}"), count + 2)
                var = half_[:, b0:b0 + nb]
            else:
                var = stats[:, b0:b0 + nb, 1]
            e.tensor_scalar(rs, var, eps, None, ALU.add).then_inc(done, 1)
            e.wait_ge(done, count + 1)
            e.tensor_tensor(rs, rs, small[:, 0:1].broadcast_to([P, nb]), ALU.pow).then_inc(done, 1)

        def dve_msq(e, n, src, g):
            at = slice(4 * g, 4 * g + 4)
            m = sem(f"msq_{n}")
            e.wait_ge(sem(f"stats_{src}"), 4 * g + 4)
            e.tensor_tensor(half_[:, at], stats[:, at, 0], stats[:, at, 0], ALU.mult).then_inc(m, 1)
            e.wait_ge(m, 2 * g + 1)
            e.tensor_tensor(half_[:, at], half_[:, at], stats[:, at, 1], ALU.add).then_inc(m, 1)

        def dve_xn(e, n, kind, b0, nb):
            e.wait_ge(sem(f"rs_{n}"), 2 * (b0 // nb) + 2)
            for b in range(b0, b0 + nb):
                if kind == "rms":
                    e.tensor_scalar(xn[:, b, :], x[:, b, :], rstd[:, b:b + 1], None, ALU.mult)\
                     .then_inc(sem(f"xn_{n}"), 1)
                else:
                    e.tensor_scalar(xn[:, b, :], x[:, b, :], stats[:, b, 0:1], rstd[:, b:b + 1],
                                    ALU.subtract, ALU.mult).then_inc(sem(f"xn_{n}"), 1)

        def pe_turn(e, n, g, to, plain=False):
            for b in range(4):
                if not plain:
                    e.wait_ge(sem(f"xn_{n}"), 4 * g + b + 1)
                mm = e.transpose(bank(to)[:, b * P:(b + 1) * P], (x if plain else xn)[:, 4 * g + b, :], identF[:, :])
            mm.then_inc(sem(f"turn_{n}"), 1)

        def act_turn(e, n, g, to, gain=None, bias=None):
            e.wait_ge(sem(f"turn_{n}"), g + 1)
            e.activation(xnT[:, g * HALF:(g + 1) * HALF], bank(to), ACT.Identity,
                         scale=col(gain) if gain else 1.0, bias=col(bias) if bias else 0.0)\
             .then_inc(sem(f"xnT_{n}"), 1)

        u32 = stackA[:, :].bitcast(F32).rearrange("p (w h k) -> p w h k", w=2, h=H)
        v1 = region[:, 0:B * H * HD].rearrange("p (b n) -> p b n", b=B)
        pT = rest[:, :, :].rearrange("p (a c) n -> p a (c n)", a=2)
        on1 = [resid[:, 2 * t:2 * t + 2, :] for t in range(4)] + \
              [tok(wmat[:, t * 2 * P:(t + 1) * 2 * P]) for t in range(2)] + \
              [xn[:, 4 + 2 * t:6 + 2 * t, :] for t in range(2)]
        z1 = onorm[:, :, :].rearrange("p a q -> p (a q)")
        a1 = mat("a1").rearrange("p (h n) -> p h n", n=P)
        L1 = lambda what: sem(f"{what}_L1")

        def pe_a1(e):
            for g in range(NT // 4):
                if g >= 1:
                    e.wait_ge(sem("a_out"), g)
                for t in range(4):
                    for h in range(2):
                        r = slice(HD * h, HD * h + HD)
                        at = 2 * (4 * g + t)
                        mm = e.matmul(bank(h)[:, t * P:(t + 1) * P], a1[r, at + 1, :], a1[r, at, :],
                                      start=True, stop=True)
                mm.then_inc(sem("a_mm"), 1)

        def act_a1(e):
            for g in range(NT // 4):
                e.wait_ge(sem("a_mm"), g + 1)
                e.copy(a1[:, 8 * g:8 * g + 8, :].rearrange("p (t h) n -> p h t n", h=2),
                       psum[:, 0:2, :].rearrange("p h (t n) -> p h t n", n=P)).then_inc(sem("a_out"), 1)

        def pe_v1(e):
            e.wait_ge(sem("a_out"), NT // 4)
            for n in range(2 * B):
                if n >= 2:
                    e.wait_ge(L1("v_out"), n - 1)
                e.matmul(bank(n % 2), ctxT[:, n // 2 * P:(n // 2 + 1) * P],
                         mat("v1")[:, n % 2 * 512:(n % 2 + 1) * 512], start=True, stop=True)\
                 .then_inc(L1("v_mm"), 1)

        def act_v1(e):
            for n in range(2 * B):
                e.wait_ge(L1("v_mm"), n + 1)
                e.copy(v1[:, n // 2, n % 2 * 512:(n % 2 + 1) * 512], bank(n % 2)).then_inc(L1("v_out"), 1)

        def pe_u1(e, i, g):
            wait = g - 1 if i == 0 else i * NT + g
            if (i, g) == (1, 1):
                e.wait_ge(sem("xnT_T1"), 2)
            if wait >= 1:
                e.wait_ge(L1("u_out"), wait)
            for h in range(2):
                mm = e.matmul(bank(7 if i else g % 2)[:, 2 * h * P:2 * (h + 1) * P], a1[:, 2 * g + h, :],
                              ctxT[:, 2 * i * P:2 * (i + 1) * P], start=True, stop=True)
            mm.then_inc(L1("u_mm"), 1)

        def act_u1(e, i, g):
            e.wait_ge(L1("u_mm"), i * NT + g + 1)
            e.copy(u32[:, i % 2, 2 * g:2 * g + 2, :], bank(7 if i else g % 2).rearrange("p (h k) -> p h k", h=2))\
             .then_inc(L1("u_out"), 1)

        def chunks(b):
            if b // 2 + 1 >= B // 2:
                return [(), (), (), ()]
            return [(4 * (b % 2) + n,) for n in range(4)]

        def pe_s1(e, b, half):
            i, bb = b // 2, b % 2
            e.wait_ge(L1("u_out"), i * NT + 4 * half + 4 if b else NT)
            if b >= 1:
                e.wait_ge(L1("exp_done"), 2 * b + half - 1)
            for g in range(2):
                h0 = 8 * half + 4 * g
                mm = e.matmul(bank(2 * half + g), xnT[:, b * P:(b + 1) * P],
                              u32[:, i % 2, h0:h0 + 4, bb * P:(bb + 1) * P], start=True, stop=True)
            mm.then_inc(L1("s_mm"), 1)

        def pe_turn1(e, b, half):
            e.wait_ge(L1("norm"), 2 * b + half + 1)
            if 2 * b + half >= 1:
                e.wait_ge(L1("pT_out"), 2 * b + half)
            for s in range(8):
                mm = e.transpose(bank(4, 2)[:, s * P:(s + 1) * P], probs[:, half, s * P:(s + 1) * P], identF[:, :])
            mm.then_inc(L1("turn_mm"), 1)

        def pe_out1(e, b, half):
            e.wait_ge(L1("pT_out"), 2 * b + half + 1)
            if 2 * b + half >= 1:
                e.wait_ge(L1("o_out"), 2 * b + half)
            if b >= 2 and b % 2 == 0 and half == 0:
                e.wait_ge(L1("z_read"), b // 2)
            for s in range(8):
                t, pp, h = s // 2, s % 2, 8 * half + s
                mm = e.matmul(bank(6)[HD * pp:HD * pp + HD, t * P:(t + 1) * P],
                              v1[:, b, h * HD:(h + 1) * HD], pT[:, half, s * P:(s + 1) * P],
                              start=True, stop=True)
            mm.then_inc(L1("pv_mm"), 1)

        def pe_z1(e, i):
            e.wait_ge(L1("o_out"), 4 * (i + 1))
            for t in range(NT):
                mm = e.matmul(bank(6)[:, 0:2 * P], mat("o1")[:, t * P:(t + 1) * P], on1[t],
                              start=(t == 0), stop=(t == NT - 1))
            mm.then_inc(L1("z_mm"), 1)

        def pe_zturn1(e, i):
            e.wait_ge(L1("z_out"), i + 1)
            for bb in range(2):
                mm = e.transpose(bank(6)[:, (2 + bb) * P:(3 + bb) * P], z1[:, bb * P:(bb + 1) * P], identF[:, :])
            mm.then_inc(L1("zt_mm"), 1)

        def pe_l1(e, more):
            pe_s1(e, 0, 0)
            pe_s1(e, 0, 1)
            for b in range(B):
                c = chunks(b)
                if b + 1 < B:
                    pe_s1(e, b + 1, 0)
                if b >= 2 and b % 2 == 0:
                    pe_z1(e, b // 2 - 1)
                for g in c[0]:
                    pe_u1(e, b // 2 + 1, g)
                more(b, 0)
                if b >= 2 and b % 2 == 0:
                    pe_zturn1(e, b // 2 - 1)
                pe_turn1(e, b, 0)
                for g in c[1]:
                    pe_u1(e, b // 2 + 1, g)
                more(b, 1)
                pe_out1(e, b, 0)
                for g in c[2]:
                    pe_u1(e, b // 2 + 1, g)
                more(b, 2)
                pe_turn1(e, b, 1)
                for g in c[3]:
                    pe_u1(e, b // 2 + 1, g)
                more(b, 3)
                if b + 1 < B:
                    pe_s1(e, b + 1, 1)
                pe_out1(e, b, 1)
            pe_z1(e, B // 2 - 1)
            pe_zturn1(e, B // 2 - 1)

        def act_exp1(e, b, half):
            e.wait_ge(L1("max_done"), 2 * b + half + 1)
            if b >= 1:
                e.wait_ge(L1("turn_mm"), 2 * b + half - 1)
            for s in range(8):
                ins = e.activation(probs[:, half, s * P:(s + 1) * P], bank(2 * half, 2)[:, s * P:(s + 1) * P],
                                   ACT.Exp, bias=maxs[:, b % 2, 8 * half + s:8 * half + s + 1])
            ins.then_inc(L1("exp_done"), 1)

        def act_pT1(e, b, half):
            e.wait_ge(L1("turn_mm"), 2 * b + half + 1)
            if b >= 1:
                e.wait_ge(L1("pv_mm"), 2 * b + half - 1)
            e.copy(pT[:, half, :], bank(4, 2)).then_inc(L1("pT_out"), 1)

        def act_out1(e, b, half):
            e.wait_ge(L1("pv_mm"), 2 * b + half + 1)
            if b >= 2 and b % 2 == 0:
                e.wait_ge(L1("z_mm"), b // 2)
            if b == 0 and half:
                e.wait_ge(sem("turn_T1"), 2)
            src = bank(6).rearrange("p (t q) -> p t q", q=P)
            bb = b % 2
            if half == 0:
                to = resid[:, :, :].rearrange("p (t c) q -> p t c q", c=2)[:, :, bb, :]
                e.copy(to, src).then_inc(L1("o_out"), 1)
            else:
                to = tok(wmat[:, 0:4 * P]).rearrange("p (t c) q -> p t c q", c=2)[:, :, bb, :]
                e.copy(to, src[:, 0:2, :])
                to = xn[:, 4:8, :].rearrange("p (t c) q -> p t c q", c=2)[:, :, bb, :]
                e.copy(to, src[:, 2:4, :]).then_inc(L1("o_out"), 1)

        def act_z1(e, i):
            e.wait_ge(L1("z_mm"), i + 1)
            if i >= 1:
                e.wait_ge(L1("zt_mm"), i)
            e.copy(z1, bank(6)[:, 0:2 * P]).then_inc(L1("z_out"), 1)

        def act_l1(e, more):
            act_exp1(e, 0, 0)
            act_exp1(e, 0, 1)
            for b in range(B):
                c = chunks(b)
                if b >= 2 and b % 2 == 0:
                    act_z1(e, b // 2 - 1)
                for g in c[0]:
                    act_u1(e, b // 2 + 1, g)
                more(b, 0)
                act_pT1(e, b, 0)
                for g in c[1]:
                    act_u1(e, b // 2 + 1, g)
                more(b, 1)
                if b + 1 < B:
                    act_exp1(e, b + 1, 0)
                act_out1(e, b, 0)
                for g in c[2]:
                    act_u1(e, b // 2 + 1, g)
                more(b, 2)
                act_pT1(e, b, 1)
                for g in c[3]:
                    act_u1(e, b // 2 + 1, g)
                more(b, 3)
                act_out1(e, b, 1)
                if b + 1 < B:
                    act_exp1(e, b + 1, 1)
            act_z1(e, B // 2 - 1)

        def dve_max1(e, b, half):
            e.wait_ge(L1("s_mm"), 2 * b + half + 1)
            e.tensor_reduce(maxs[:, b % 2, 8 * half:8 * half + 8],
                            bank(2 * half, 2).rearrange("p (h k) -> p h k", k=P), AX.X, ALU.max, negate=True)\
             .then_inc(L1("max_done"), 1)

        def dve_norm1(e, b, half):
            n = 2 * b + half + 1
            p8 = probs[:, half, :].rearrange("p (h k) -> p h k", k=P)
            sums = mres[:, half, 0, 0:8]
            rec = mres[:, half, 1, 0:8]
            e.wait_ge(L1("exp_done"), n)
            e.tensor_reduce(sums, p8, AX.X, ALU.add).then_inc(L1("sum"), 1)
            e.wait_ge(L1("sum"), n)
            e.reciprocal(rec, sums).then_inc(L1("rec"), 1)
            e.wait_ge(L1("rec"), n)
            e.tensor_tensor(p8, p8, rec.unsqueeze(2).broadcast_to([P, 8, P]), ALU.mult).then_inc(L1("norm"), 1)

        def dve_z1(e, i):
            e.wait_ge(L1("zt_mm"), i + 1)
            xs = x[:, 2 * i:2 * i + 2, :]
            e.tensor_tensor(xs, tok(bank(6)[:, 2 * P:4 * P]), xs, ALU.add).then_inc(L1("z_read"), 1)
            for b in (2 * i, 2 * i + 1):
                dve_stats(e, "L1", b, L1("z_read"), i - b)

        def dve_l1(e, more):
            dve_max1(e, 0, 0)
            dve_max1(e, 0, 1)
            dve_norm1(e, 0, 0)
            for b in range(B):
                if b + 1 < B:
                    dve_max1(e, b + 1, 0)
                dve_norm1(e, b, 1)
                if b >= 2 and b % 2 == 0:
                    dve_z1(e, b // 2 - 1)
                more(b, 0)
                if b + 1 < B:
                    dve_norm1(e, b + 1, 0)
                more(b, 1)
                if b + 1 < B:
                    dve_max1(e, b + 1, 1)
                more(b, 2)
            dve_z1(e, B // 2 - 1)

        hT = mat("a1").rearrange("p (c t) -> p c t", c=4)
        y32 = mat("o1").rearrange("p (g t) -> p g t", g=2)

        def pe_f1(e, g, c):
            e.matmul(bank(c), mat("f1")[:, c * P:(c + 1) * P], xnT[:, g * HALF:(g + 1) * HALF],
                     start=True, stop=True).then_inc(sem("h_mm"), 1)

        def act_f1(e, g, c):
            e.wait_ge(sem("h_mm"), 4 * g + c + 1)
            e.activation(hT[:, c, :], bank(c), ACT.Relu, bias=col(f"f_b{c}")).then_inc(sem("h_out"), 1)

        def pe_f2(e, g):
            e.wait_ge(sem("h_out"), 4 * g + 4)
            for c in range(4):
                mm = e.matmul(bank(0), mat("f2")[:, c * P:(c + 1) * P], hT[:, c, :], start=(c == 0), stop=(c == 3))
            mm.then_inc(sem("f2_mm"), 1)

        def act_f2(e, g):
            e.wait_ge(sem("f2_mm"), g + 1)
            e.copy(y32[:, g, :], bank(0)).then_inc(sem("f2_out"), 1)

        def pe_fturn(e, g):
            e.wait_ge(sem("f2_out"), g + 1)
            for b in range(4):
                mm = e.transpose(bank(1)[:, b * P:(b + 1) * P], y32[:, g, b * P:(b + 1) * P], identF[:, :])
            mm.then_inc(sem("ft_mm"), 1)

        def dve_ff(e, g):
            e.wait_ge(sem("ft_mm"), g + 1)
            e.wait_ge(sem("resid_FF"), g + 1)
            at = slice(4 * g, 4 * g + 4)
            e.tensor_tensor(x[:, at, :], tok(bank(1)), resid[:, at, :], ALU.add).then_inc(sem("ff_read"), 1)

        def done(L, what, n):
            return what, L.past(what) + n

        L0.vall = L2.vall = L3.vall = vall
        LC.vall = tok(mat("v1"))
        L0.extra = {0: [("filled", 16 * 20), ("padrows", 48), ("v_out_L1", 2 * B), done(L0, "k_rest", 2),
                        done(L0, "q_rest", 2), done(L0, "v_out", 2)]}
        L2.extra = {0: [("blockrows", 48)], 2: [("z_read_L1", B // 2)]}
        LC.extra = {0: [("filledC", 16 * 10), ("clearedQ0", 16)], 4: [("clearedQ1", 16)]}
        L3.extra = {0: [("clearedQ0", 32), ("clearedK3", 16), ("ff_read", 2)], 4: [("clearedQ1", 32)]}
        L0.extra2 = {}
        L2.extra2 = {3: [done(L2, "k_kept", 2), done(L2, "q_kept", 2)], 4: [done(L2, "v_out", 2)],
                     5: [done(LC, "k_rest", 1)], 6: [done(LC, "k_rest", 2)], 7: [done(LC, "v_out", 2)]}
        LC.extra2 = {0: [done(LC, "q_rest", 1)], 3: [done(LC, "q_rest", 2)], 4: [done(L3, "k_rest", 1)],
                     5: [done(L3, "k_rest", 2)], 6: [done(L3, "v_out", 2)]}
        L3.extra2 = {0: [done(L3, "q_rest", 1)], 3: [done(L3, "q_rest", 2)]}

        def fill(e, stack, r, n, src, done):
            for k in range(0, n, E):
                m = min(E, n - k)
                e.dma_start(stack_rows(stack, r + k, m), src[0:m * H, :]).then_inc(done, 16)

        def put_row(e, stack, r, n, src, done):
            e.dma_start(stack_rows(stack, r, n), src).then_inc(done, 16)

        def clear_max(e, L, g):
            e.wait_ge(L.sem("s_mm"), L.past("s_mm") + 8 * (g + 1))
            e.dma_start(stack_rows(stackA, ROW_MAX, 4)[:, :, g * HALF:(g + 1) * HALF], zeros[0:4 * H, 0:HALF])\
             .then_inc(sem(f"clearedQ{g}"), 16)

        block = ctx.enter_context(nc.Block())

        @block.sync
        def _(e):
            c0 = MAT_AT["q2"][0]
            e.dma_start(xnT[:, :], xt_d).then_inc(sem("in_xT"), 16)
            e.dma_start(wmat[:, 0:c0], wmat_d[:, 0:c0]).then_inc(sem("in_w0"), 16)
            e.dma_start(ctxT[:, :], ctxt_d).then_inc(sem("in_ctx"), 16)
            e.dma_start(pad[:, :], mask_d.partition_broadcast(P)).then_inc(sem("in_mask"), 16)
            e.dma_start(wcol[:, :], wcol_d).then_inc(sem("in_cols"), 16)
            e.dma_start(x[:, :, :], x_d).then_inc(sem("in_x"), 16)
            e.dma_start(wrow[:, :], wrow_d.partition_broadcast(P)).then_inc(sem("in_rows"), 16)
            e.dma_start(wmat[:, c0:N_MAT], wmat_d[:, c0:N_MAT]).then_inc(sem("in_w"), 16)
            e.wait_ge(sem("consts"), 4)
            fill(e, stackA, ROW_ZERO, 16, zeros, sem("filled"))
            fill(e, stackB, ROW_ZERO, 48, zeros, sem("filled"))
            fill(e, stackA, ROW_KEY, 32, ones, sem("filled"))
            fill(e, stackB, ROW_MAX, 32, ones, sem("filled"))
            fill(e, stackA, ROW_MAX, 32, zeros, sem("filled"))
            sync_stack(e, L0, "q", 0)
            sync_stack(e, L0, "k", 0)
            e.wait_ge(sem("padsplit"), 5)
            e.wait_ge(sem("filled"), 16 * 20)
            for n in range(3):
                put_row(e, stackB, ROW_KEY + n, 1, rows[:, n, :], sem("padrows"))
            sync_stack(e, L0, "q", 1)
            sync_stack(e, L0, "k", 1)
            for b in range(B):
                sync_rows(e, L0, b)
            e.wait_ge(L0.sem("z_read"), L0.past("z_read") + B)
            fill(e, stackB, ROW_ZERO, 48, zeros, sem("filledB2"))
            fill(e, stackB, ROW_MAX, 32, ones, sem("filledB2"))
            e.wait_ge(L1("s_mm"), 2 * B)
            fill(e, stackA, ROW_ZERO, 16, zeros, sem("filledA2"))
            fill(e, stackA, ROW_MAX, 32, zeros, sem("filledA2"))
            fill(e, stackA, ROW_KEY, 32, ones, sem("filledA2"))
            sync_stack(e, L2, "k", 0)
            sync_stack(e, L2, "q", 0)
            e.wait_ge(sem("filledB2"), 16 * 10)
            e.wait_ge(sem("filledA2"), 16 * 10)
            e.wait_ge(sem("rows_done"), 3)
            put_row(e, stackA, ROW_BLOCK, 1, rows[:, 0, :], sem("blockrows"))
            put_row(e, stackA, ROW_KEY, 1, rows[:, 1, :], sem("blockrows"))
            put_row(e, stackB, ROW_KEY, 1, rows[:, 2, :], sem("blockrows"))
            sync_rows(e, L2, 0)
            fill(e, stackC, ROW_ZERO, 16, zeros, sem("filledC"))
            sync_rows(e, L2, 1)
            fill(e, stackC, ROW_KEY, 32, zeros, sem("filledC"))
            sync_rows(e, L2, 2)
            sync_stack(e, L2, "k", 1)
            sync_stack(e, L2, "q", 1)
            sync_rows(e, L2, 3)
            fill(e, stackC, ROW_MAX, 32, ones, sem("filledC"))
            sync_rows(e, L2, 4)
            sync_stack(e, LC, "k", 0)
            sync_rows(e, L2, 5)
            sync_stack(e, LC, "k", 1)
            sync_rows(e, L2, 6)
            sync_rows(e, L2, 7)
            clear_max(e, L2, 0)
            sync_stack(e, LC, "q", 0)
            clear_max(e, L2, 1)
            sync_rows(e, LC, 0)
            sync_rows(e, LC, 1)
            sync_rows(e, LC, 2)
            sync_stack(e, LC, "q", 1)
            put_row(e, stackB, ROW_KEY, 1, zeros[0:H, :], sem("clearedK3"))
            sync_rows(e, LC, 3)
            sync_stack(e, L3, "k", 0)
            sync_rows(e, LC, 4)
            sync_stack(e, L3, "k", 1)
            for b in range(5, B):
                sync_rows(e, LC, b)
            clear_max(e, LC, 0)
            clear_max(e, LC, 1)
            sync_stack(e, L3, "q", 0)
            for b in range(3):
                sync_rows(e, L3, b)
            sync_stack(e, L3, "q", 1)
            for b in range(3, B):
                sync_rows(e, L3, b)
            for b in range(B):
                e.wait_ge(sem("out_ready"), b + 1)
                e.dma_start(out_d[b], xn[:, b, :]).then_inc(sem("stored"), 16)
            e.wait_ge(sem("stored"), 16 * B)

        @block.gpsimd
        def _(e):
            c = sem("consts")
            e.memset(zeros[:, :], 0.0).then_inc(c, 1)
            e.memset(ones[:, :], 1.0).then_inc(c, 1)
            p = sem("pre")
            e.memset(identF[:, :], 0.0).then_inc(p, 1)
            e.memset(identB[:, :], 0.0).then_inc(p, 1)
            e.wait_ge(p, 2)
            for m in (identF, identB):
                e.affine_select(out=m[:, :], in_=m[:, :], compare_op=ALU.not_equal, fill=1.0,
                                base=0, pattern=[[-1, P]], channel_multiplier=1).then_inc(c, 1)
            e.memset(vpad[:, :, :, :], 0.0).then_inc(p, 1)
            e.memset(opad[:, :], 0.0).then_inc(p, 1)
            e.memset(small[:, 0:1], -0.5).then_inc(p, 1)
            e.memset(causal[:, :, :], 0.0).then_inc(p, 1)
            e.wait_ge(p, 6)
            e.memset(opad[:, :].rearrange("p (i c) -> p i c", c=40)[:, :, 0:E], 1.0).then_inc(c, 1)
            cz = causal[:, :, :].rearrange("p a (h k) -> p a h k", k=P)
            e.affine_select(out=cz[:, 0], in_=cz[:, 0], compare_op=ALU.is_ge, fill=CAUSAL,
                            base=0, pattern=[[0, 4], [-1, P]], channel_multiplier=1).then_inc(c, 1)
            e.affine_select(out=cz[:, 1], in_=cz[:, 1], compare_op=ALU.is_ge, fill=CAUSAL,
                            base=0, pattern=[[0, 4], [1, P]], channel_multiplier=-1).then_inc(c, 1)
            e.wait_ge(sem("in_rows"), 16)
            for g in range(2):
                pool_resid(e, "L0", "bo_0", g, "in_x", 16)

            def norms0(g):
                pool_rstd(e, "N0", "L0", "ln", 1e-5, 4 * g, 4)
                pool_rstd(e, "T1", "X1", "rms", 1e-6, 4 * g, 4)

            pool_attn(e, L0, B + 3, after=lambda b: norms0(0) if b == 8 else None)
            norms0(1)
            pool_rstd(e, "T2", "L1", "ln", 1e-5, 0, 4)
            e.wait_ge(sem("keep"), 4)
            for n in range(3):
                e.tensor_copy(rows[:, n, :].rearrange("p (b c t) -> p b c t", c=2, t=BLOCK),
                              keepn[0:H, n, :].unsqueeze(1).unsqueeze(3).broadcast_to([H, B, 2, BLOCK]))\
                 .then_inc(sem("rows_done"), 1)

            def during2(b):
                if b == 0:
                    pool_rstd(e, "T2", "L1", "ln", 1e-5, 4, 4)
                    for g in range(2):
                        pool_resid(e, "L2", "bo_2", g, "stats_L1", B)
                if b == 8:
                    pool_resid(e, "LC", "bo_c", 0, "stats_L2", 4)

            def duringC(b):
                if b == 1:
                    pool_rstd(e, "TC", "L2", "ln", 1e-5, 4, 4)
                    pool_resid(e, "LC", "bo_c", 1, "stats_L2", B)
                if b == 8:
                    pool_resid(e, "FF", "b_ff", 0, "stats_LC", 4)

            def first_half(n, src):
                return lambda b: pool_rstd(e, n, src, "ln", 1e-5, 0, 4) if b == 7 else None

            pool_attn(e, L2, STEPS, before=first_half("TC", "L2"), after=during2)
            pool_attn(e, LC, B + 3, before=first_half("TF", "LC"), after=duringC)
            pool_rstd(e, "TF", "LC", "ln", 1e-5, 4, 4)
            pool_resid(e, "FF", "b_ff", 1, "stats_LC", B)
            for g in range(2):
                pool_resid(e, "L3", "bo_3", g, "ff_read", g + 1)
            pool_attn(e, L3, B + 3, before=first_half("N3", "L3"))
            pool_rstd(e, "N3", "L3", "ln", 1e-5, 4, 4)

        @block.tensor
        def _(e):
            e.wait_ge(sem("in_w0"), 16)
            e.wait_ge(sem("in_xT"), 16)
            pe_q(e, L0, 0)
            pe_q(e, L0, 1)
            e.wait_ge(sem("padmul"), 1)
            e.wait_ge(sem("in_ctx"), 16)
            for g in range(2):
                pe_k(e, L0, g)
            for g in range(2):
                pe_v(e, L0, g)
            e.wait_ge(sem("consts"), 7)
            e.wait_ge(sem("in_w"), 16)
            pe_a1(e)
            pe_v1(e)

            def between0(b):
                if b == 9:
                    pe_turn(e, "T1", 0, 2)

            def before0(b):
                if b == 10:
                    pe_u1(e, 0, 0)
                    pe_u1(e, 0, 1)

            pe_attn(e, L0, B + 3, before=before0, between=between0)
            for g in range(2, NT):
                pe_u1(e, 0, g)
            e.wait_ge(L0.sem("z_read"), L0.past("z_read") + B)
            e.wait_ge(sem("xnT_T1"), 1)

            def during1(b, place):
                if (b, place) == (0, 0):
                    e.wait_ge(L1("u_out"), NT + 1)
                    pe_turn(e, "T1", 1, 7)
                if (b, place) == (6, 0):
                    e.wait_ge(L1("u_out"), NT * B // 2)
                    pe_turn(e, "T2", 0, 7)
                if (b, place) == (6, 1):
                    e.wait_ge(sem("xnT_T2"), 1)
                    pe_k(e, L2, 0)
                if (b, place) == (6, 2):
                    e.wait_ge(sem("router"), 3)
                    e.matmul(bank(7)[:, 0:2], mat("r1"), small[:, 4:6], start=True, stop=True)\
                     .then_inc(sem("r_mm"), 1)
                if (b, place) == (6, 3):
                    e.wait_ge(sem("r_hidden"), 2)
                    e.matmul(bank(7)[:, 0:2], mat("v1")[:, 0:P], small[:, 6:8], start=True, stop=True)\
                     .then_inc(sem("r_mm"), 1)
                if (b, place) == (7, 0):
                    e.wait_ge(sem("keep"), 1)
                    pe_v(e, L2, 0)
                if (b, place) == (7, 1):
                    e.wait_ge(L2.sem("v_out"), L2.past("v_out") + 1)
                    pe_q(e, L2, 0)

            pe_l1(e, during1)

            def free(L, b):
                e.wait_ge(L.sem("max_done"), L.past("max_done") + 2 * b)

            def second_half(L, n, b, plain=False):
                if b == 3:
                    e.wait_ge(sem(f"xnT_{n}"), 2)
                    if L.self_attn:
                        pe_k(e, L, 1)
                    pe_q(e, L, 1)

            def next_kv(L, N, b, at):
                if at <= b <= at + 2:
                    free(L, b)
                if b in (at, at + 1):
                    pe_k(e, N, b - at)
                if b == at + 2:
                    pe_v(e, N, 0)
                    pe_v(e, N, 1)

            def turn_second(L, n, b, plain=False):
                if b == 2:
                    free(L, 3)
                    pe_turn(e, n, 1, 2, plain)

            def before2(b):
                second_half(L2, "T2", b)
                if b == 4:
                    free(L2, 4)
                    pe_v(e, L2, 1)
                next_kv(L2, LC, b, 5)
                if b == 8:
                    free(L2, 8)
                    pe_turn(e, "TC", 0, 2)

            def between2(b):
                if b == 8:
                    e.wait_ge(sem("xnT_TC"), 1)
                    pe_q(e, LC, 0)

            def beforeC(b):
                second_half(LC, "TC", b)
                next_kv(LC, L3, b, 4)
                if b == 8:
                    free(LC, 8)
                    pe_turn(e, "TF", 0, 2)
                if b == 9:
                    pe_f2(e, 0)
                if b == 10:
                    pe_fturn(e, 0)

            def betweenC(b):
                if b == 8:
                    e.wait_ge(sem("xnT_TF"), 1)
                    for c in range(4):
                        pe_f1(e, 0, c)

            pe_attn(e, L2, STEPS, before2, between2, lambda b: turn_second(L2, "T2", b))
            pe_attn(e, LC, B + 3, beforeC, betweenC, lambda b: turn_second(LC, "TC", b))
            e.wait_ge(sem("ff_read"), 1)
            pe_turn(e, "T3", 0, 2, plain=True)
            e.wait_ge(sem("xnT_T3"), 1)
            pe_q(e, L3, 0)
            pe_turn(e, "TF", 1, 2)
            e.wait_ge(sem("xnT_TF"), 2)
            for c in range(4):
                if c == 3:
                    e.wait_ge(L3.sem("q_rest"), L3.past("q_rest") + 1)
                pe_f1(e, 1, c)
            pe_f2(e, 1)
            pe_fturn(e, 1)
            pe_attn(e, L3, B + 3, lambda b: second_half(L3, "T3", b), None,
                    lambda b: turn_second(L3, "T3", b, plain=True))

        @block.scalar
        def _(e):
            e.wait_ge(sem("in_cols"), 16)
            for name in "qk":
                for g in range(2):
                    act_p0(e, L0, name, g)
                for g in range(2):
                    act_p1(e, L0, name, g)
            act_a1(e)
            act_v1(e)

            def before0(b):
                if b == 10:
                    act_u1(e, 0, 0)
                    act_u1(e, 0, 1)

            act_attn(e, L0, B + 3, before=before0,
                     between=lambda b: act_turn(e, "T1", 0, 2, "norm_w") if b == 9 else None)
            for g in range(2, NT):
                act_u1(e, 0, g)

            def during1(b, place):
                if (b, place) == (0, 0):
                    act_turn(e, "T1", 1, 7, "norm_w")
                if (b, place) == (6, 0):
                    act_turn(e, "T2", 0, 7, "n1_g", "n1_b")
                if (b, place) == (6, 2):
                    e.wait_ge(sem("r_mm"), 1)
                    e.activation(small[:, 6:8], bank(7)[:, 0:2], ACT.Relu, bias=col("r_b1"))\
                     .then_inc(sem("r_hidden"), 1)
                if (b, place) == (7, 0):
                    act_p0(e, L2, "k", 0)
                if (b, place) == (7, 1):
                    act_p1(e, L2, "k", 0)
                if (b, place) == (7, 2):
                    act_p0(e, L2, "q", 0)
                if (b, place) == (7, 3):
                    act_p1(e, L2, "q", 0)

            act_l1(e, during1)

            def second_half(L, n, b, gain=None, bias=None):
                if b == 3:
                    act_turn(e, n, 1, 2, gain, bias)
                    if L.self_attn:
                        act_p0(e, L, "k", 1)
                    act_p0(e, L, "q", 1)

            def second_rest(L, b):
                if b == 3:
                    if L.self_attn:
                        act_p1(e, L, "k", 1)
                    act_p1(e, L, "q", 1)

            def before2(b):
                second_half(L2, "T2", b, "n1_g", "n1_b")
                if b in (5, 6):
                    act_p0(e, LC, "k", b - 5)
                if b == 8:
                    act_turn(e, "TC", 0, 2, "n2_g", "n2_b")

            def between2(b):
                second_rest(L2, b)
                if b in (5, 6):
                    act_p1(e, LC, "k", b - 5)
                if b == 8:
                    act_p0(e, LC, "q", 0)
                    act_p1(e, LC, "q", 0)

            def beforeC(b):
                second_half(LC, "TC", b, "n2_g", "n2_b")
                if b in (4, 5):
                    act_p0(e, L3, "k", b - 4)
                if b == 8:
                    act_turn(e, "TF", 0, 2, "n3_g", "n3_b")
                if b == 10:
                    act_f2(e, 0)

            def betweenC(b):
                second_rest(LC, b)
                if b in (4, 5):
                    act_p1(e, L3, "k", b - 4)
                if b == 8:
                    for c in range(4):
                        act_f1(e, 0, c)

            act_attn(e, L2, STEPS, before2, between2)
            act_attn(e, LC, B + 3, beforeC, betweenC)
            act_turn(e, "T3", 0, 2)
            act_p0(e, L3, "q", 0)
            act_p1(e, L3, "q", 0)
            act_turn(e, "TF", 1, 2, "n3_g", "n3_b")
            for c in range(4):
                act_f1(e, 1, c)
            act_f2(e, 1)
            act_attn(e, L3, B + 3, lambda b: second_half(L3, "T3", b), lambda b: second_rest(L3, b))

        @block.vector
        def _(e):
            e.wait_ge(sem("in_mask"), 16)
            ps = sem("padsplit")
            u = rest[0:H, 0:2, :].rearrange("p a n -> p (a n)")
            v = rest[0:H, 2:4, :].rearrange("p a n -> p (a n)")
            e.tensor_scalar(u, pad[0:H, :], -1.0, -PAD / L0.scale, ALU.add, ALU.mult).then_inc(ps, 1)
            e.wait_ge(ps, 1)
            e.tensor_copy(rows[:, 0, :], u).then_inc(ps, 1)
            e.wait_ge(ps, 2)
            e.tensor_tensor(v, u, rows[:, 0, :], ALU.subtract).then_inc(ps, 1)
            e.wait_ge(ps, 3)
            e.tensor_copy(rows[:, 1, :], v).then_inc(ps, 1)
            e.wait_ge(ps, 4)
            e.tensor_tensor(rows[:, 2, :], v, rows[:, 1, :], ALU.subtract).then_inc(ps, 1)
            e.wait_ge(ps, 5)
            e.wait_ge(sem("in_ctx"), 16)
            e.tensor_tensor(pad[:, :], ctxT[:, :], pad[:, :], ALU.mult).then_inc(sem("padmul"), 1)
            e.wait_ge(sem("in_cols"), 16)
            for name in "qk":
                for g in range(2):
                    dve_rest(e, L0, name, g)
                for g in range(2):
                    dve_p2(e, L0, name, g)
            for g in range(2):
                dve_v(e, L0, g)

            def norm0(g):
                at = slice(4 * g, 4 * g + 4)
                dve_xn(e, "N0", "ln", 4 * g, 4)
                e.wait_ge(sem("xn_N0"), 4 * g + 4)
                e.tensor_tensor(xn[:, at, :], xn[:, at, :], row("g_0", 4), ALU.mult).then_inc(sem("aff"), 1)
                e.wait_ge(sem("aff"), 2 * g + 1)
                e.tensor_tensor(x[:, at, :], xn[:, at, :], row("b_0", 4), ALU.add).then_inc(sem("aff"), 1)

            def input1(g):
                for b in range(4 * g, 4 * g + 4):
                    dve_stats(e, "X1", b, sem("aff"), 2 * g + 1 - b)
                dve_msq(e, "T1", "X1", g)
                dve_xn(e, "T1", "rms", 4 * g, 4)

            def between0(b):
                if b == 8:
                    norm0(0)
                if b == 9:
                    input1(0)

            dve_attn(e, L0, B + 3, between=between0)
            norm0(1)
            input1(1)

            def during1(b, place):
                if (b, place) == (4, 2):
                    dve_xn(e, "T2", "ln", 0, 4)
                if (b, place) == (6, 0):
                    wait_half(e, L2, "k_mm", 0)
                    r = sem("router")
                    e.tensor_copy(kept[:, 1, 0, :], bank(7)).then_inc(r, 1)
                    e.wait_ge(r, 1)
                    e.tensor_reduce(small[:, 2:4], kept[:, 1, 0, 0:P].rearrange("p (c t) -> p c t", c=2),
                                    AX.X, ALU.add).then_inc(r, 1)
                    e.wait_ge(r, 2)
                    e.tensor_scalar(small[:, 4:6], small[:, 2:4], 1.0 / BLOCK, None, ALU.mult).then_inc(r, 1)
                    e.tensor_copy(mat("v1")[:, 0:P], col("r_w2").broadcast_to([P, P])).then_inc(sem("r_hidden"), 1)
                if (b, place) == (6, 2):
                    e.wait_ge(sem("r_mm"), 2)
                    k = sem("keep")
                    e.tensor_scalar(keep[:, :], bank(7)[:, 0:2], col("r_b2"), 0.0, ALU.add, ALU.is_gt).then_inc(k, 1)
                    e.wait_ge(k, 1)
                    e.tensor_scalar(keepn[:, 0, :], keep[:, :], -NEG, NEG, ALU.mult, ALU.add).then_inc(k, 1)
                    e.tensor_scalar(keepn[:, 1, :], keep[:, :], NEG, None, ALU.mult).then_inc(k, 1)
                    e.tensor_scalar(keepn[:, 2, :], keep[:, :], -1.0, 1.0, ALU.mult, ALU.add).then_inc(k, 1)
                    dve_kept(e, L2, "k", 0, kept[:, 1, 0, :])
                if (b, place) == (7, 0):
                    dve_rest(e, L2, "k", 0)
                    dve_v(e, L2, 0)
                if (b, place) == (7, 1):
                    dve_p2(e, L2, "k", 0)
                    dve_kept(e, L2, "q", 0)
                if (b, place) == (7, 2):
                    dve_rest(e, L2, "q", 0)
                    dve_p2(e, L2, "q", 0)

            dve_l1(e, during1)

            def before2(b):
                if b == 2:
                    dve_xn(e, "T2", "ln", 4, 4)
                if b == 3:
                    dve_kept(e, L2, "k", 1)
                    dve_kept(e, L2, "q", 1)
                    dve_rest(e, L2, "k", 1)
                    dve_rest(e, L2, "q", 1)
                if b == 4:
                    dve_v(e, L2, 1)
                if b in (5, 6):
                    dve_rest(e, LC, "k", b - 5)
                if b == 7:
                    dve_v(e, LC, 0)
                    dve_v(e, LC, 1)

            def between2(b):
                if b == 3:
                    dve_p2(e, L2, "k", 1)
                    dve_p2(e, L2, "q", 1)
                if b in (5, 6):
                    dve_p2(e, LC, "k", b - 5)
                if b == 7:
                    dve_xn(e, "TC", "ln", 0, 4)
                if b == 8:
                    dve_rest(e, LC, "q", 0)

            def beforeC(b):
                if b == 2:
                    dve_xn(e, "TC", "ln", 4, 4)
                if b == 3:
                    dve_rest(e, LC, "q", 1)
                if b in (4, 5):
                    dve_rest(e, L3, "k", b - 4)
                if b == 6:
                    dve_v(e, L3, 0)
                    dve_v(e, L3, 1)
                if b == 10:
                    dve_ff(e, 0)

            def betweenC(b):
                if b == 3:
                    dve_p2(e, LC, "q", 1)
                if b in (4, 5):
                    dve_p2(e, L3, "k", b - 4)
                if b == 7:
                    dve_xn(e, "TF", "ln", 0, 4)

            dve_attn(e, L2, STEPS, before2, between2,
                     lambda b: dve_p2(e, LC, "q", 0) if b == 8 else None)
            dve_attn(e, LC, B + 3, beforeC, betweenC)
            dve_rest(e, L3, "q", 0)
            dve_xn(e, "TF", "ln", 4, 4)
            dve_p2(e, L3, "q", 0)
            dve_ff(e, 1)

            def output(b0, nb):
                dve_xn(e, "N3", "ln", b0, nb)
                for b in range(b0, b0 + nb):
                    e.wait_ge(sem("xn_N3"), b + 1)
                    e.tensor_tensor(xn[:, b, :], xn[:, b, :], row("g_3")[:, 0, :], ALU.mult).then_inc(sem("aff3"), 1)
                for b in range(b0, b0 + nb):
                    e.wait_ge(sem("aff3"), b + 1)
                    e.tensor_tensor(xn[:, b, :], xn[:, b, :], row("b_3")[:, 0, :], ALU.add)\
                     .then_inc(sem("out_ready"), 1)

            def before3(b):
                if b == 3:
                    dve_rest(e, L3, "q", 1)
                if b == 9:
                    output(0, 4)

            dve_attn(e, L3, B + 3, before3, lambda b: dve_p2(e, L3, "q", 1) if b == 3 else None)
            output(4, 4)


def kernel(**inputs):
    import concourse.bacc as _bacc
    from concourse.bass_utils import run_bass_kernel_spmd as _run

    a = {k: np.asarray(v) for k, v in inputs.items()}

    def by_feature(w):
        s = w.shape[:-1]
        return w.reshape(*s, 4, 4, E).swapaxes(-1, -3).reshape(*s, P)

    l2, ca = a["L2_xattn_qkv_w"], a["L2_xattn_ca_in_w"]
    cab = a["L2_xattn_ca_in_b"]
    w3 = {k: a[f"L3_xattn_W{k}"].transpose(1, 0, 2).reshape(P, P) for k in "qkv"}
    mats = {
        "q0": by_feature(a["L0_xattn_wq"]), "k0": by_feature(a["L0_xattn_wk"]),
        "v0": a["L0_xattn_wv"], "o0": a["L0_xattn_wo"],
        "q2": by_feature(l2[0:P].T), "k2": by_feature(l2[P:2 * P].T), "v2": l2[2 * P:].T,
        "o2": a["L2_xattn_sa_out_w"].T,
        "qc": by_feature(ca[0:P].T), "kc": by_feature(ca[P:2 * P].T), "vc": ca[2 * P:].T,
        "oc": a["L2_xattn_ca_out_w"].T,
        "q3": by_feature(w3["q"]), "k3": by_feature(w3["k"]), "v3": w3["v"], "o3": a["L3_xattn_Wo"],
        "r1": by_feature(a["L2_xattn_r_w1"]).T,
        "a1": np.stack([a["L1_xattn_wq"].T.reshape(NT, P, P), a["L1_xattn_wk"].T.reshape(NT, P, P)], axis=1)
              .transpose(2, 0, 1, 3).reshape(P, 2 * H * HD), "v1": a["L1_xattn_wv"],
        "o1": a["L1_xattn_wo"].reshape(NT, P, P).transpose(1, 0, 2).reshape(P, NT * P),
        "f1": a["L2_xattn_ff_w1"].T,
        "f2": a["L2_xattn_ff_w2"].T.reshape(4, P, P).transpose(1, 0, 2).reshape(P, FF),
    }
    fb = a["L2_xattn_ff_b1"].reshape(4, P)
    cols = {
        "norm_w": a["L1_xattn_norm_w"], "bq_c": by_feature(cab[0:P]), "bk_c": by_feature(cab[P:2 * P]),
        "bq_3": by_feature(a["L3_xattn_bq"].reshape(P)), "bk_3": by_feature(a["L3_xattn_bk"].reshape(P)),
        "r_b1": a["L2_xattn_r_b1"], "r_w2": a["L2_xattn_r_w2"].reshape(P),
        "r_b2": np.broadcast_to(a["L2_xattn_r_b2"], (P,)),
        **{f"n{n}_{s}": a[f"L2_xattn_n{n}_{s}"] for n in (1, 2, 3) for s in "gb"},
        **{f"f_b{c}": fb[c] for c in range(4)},
    }
    rows = {
        "bo_0": a["L0_xattn_bo"], "g_0": a["L0_xattn_ln_gamma"], "b_0": a["L0_xattn_ln_beta"],
        "bo_2": a["L2_xattn_sa_out_b"], "bv_c": cab[2 * P:], "bo_c": a["L2_xattn_ca_out_b"],
        "b_ff": a["L2_xattn_ff_b2"], "bv_3": a["L3_xattn_bv"].reshape(P), "bo_3": a["L3_xattn_bo"],
        "g_3": a["L3_xattn_gamma"], "b_3": a["L3_xattn_beta"],
    }
    x = a["x"]
    arrays = {
        "xt": x.transpose(2, 0, 1).reshape(P, T),
        "xtok": x.transpose(1, 0, 2),
        "ctxt": a["ctx_1024"].transpose(2, 0, 1).reshape(P, T),
        "mask": a["mask_BxS2_ff1"].reshape(T),
        "wmat": np.concatenate([mats[m] for m in MATS], axis=1),
        "wcol": np.stack([cols[c] for c in COLS], axis=1),
        "wrow": np.concatenate([rows[r] for r in ROWS]),
    }
    nc = _bacc.Bacc("TRN2", target_bir_lowering=False, num_devices=1)
    args, arr = [], {}
    for name, v in arrays.items():
        arr[f"in_{name}"] = np.ascontiguousarray(v)
        args.append(nc.dram_tensor(f"in_{name}", v.shape, F32, kind="ExternalInput").ap())
    args.append(nc.dram_tensor("out_x", (B, P, P), F32, kind="ExternalOutput").ap())
    build(nc, *args)
    r = _run(nc, [arr], core_ids=[0])
    return r.results[0]["out_x"]
```

```python
from contextlib import ExitStack

import numpy as np

import concourse.bass as bass
from concourse import mybir

P = 128
B = 8
T = B * P
HALF = T // 2
H = 16
E = 8
HD = 64
NT = H * HD // P
FF = 512
BLOCK = 64
STEPS = B + 1
SLOT = 160

F32 = mybir.dt.float32
BF16 = mybir.dt.bfloat16
ACT = mybir.ActivationFunctionType
ALU = mybir.AluOpType
AX = mybir.AxisListType

Q_SLOTS = (0, 0, 0, 1, 1, 2)
K_SLOTS = (0, 1, 2, 0, 1, 0)
ROW_ZERO = E * len(Q_SLOTS)
ROW_KEY = 64
ROW_MAX = 96
ROW_BLOCK = ROW_MAX + 3
PAD = -1e10
NEG = -float(2 ** 30)
TWO_ONES = float(np.array([0x3F803F80], np.uint32).view(np.float32)[0])
CAUSAL = -1e30

MATS = ["q0", "k0", "v0", "o0", "a1", "v1", "q2", "k2", "v2", "o2", "qc", "kc", "vc", "oc", "q3", "k3",
        "v3", "o3", "r1", "o1", "f1", "f2"]
WIDTH = {"a1": 2 * H * HD, "v1": H * HD, "o1": H * HD, "f1": FF, "f2": FF}
MAT_AT = {}
_at = 0
for _m in MATS:
    MAT_AT[_m] = (_at, _at + WIDTH.get(_m, P))
    _at += WIDTH.get(_m, P)
N_MAT = _at
COLS = ["norm_w", "n1_g", "n1_b", "n2_g", "n2_b", "n3_g", "n3_b", "bq_c", "bk_c", "bq_3", "bk_3",
        "r_b1", "r_w2", "r_b2", "f_b0", "f_b1", "f_b2", "f_b3"]
ROWS = ["bo_0", "g_0", "b_0", "bo_2", "bv_c", "bo_c", "b_ff", "bv_3", "bo_3", "g_3", "b_3"]


def build(nc, xt_d, x_d, ctxt_d, mask_d, wmat_d, wcol_d, wrow_d, out_d):
    ctx = ExitStack()
    with ctx:
        def sb(name, shape, dt=F32):
            return ctx.enter_context(nc.sbuf_tensor(name, shape, dt))

        sems = {}

        def sem(name):
            if name not in sems:
                sems[name] = ctx.enter_context(nc.semaphore(name))
            return sems[name]

        wmat = sb("wmat", [P, N_MAT])
        wcol = sb("wcol", [P, len(COLS)])
        wrow = sb("wrow", [P, len(ROWS) * P])
        x = sb("x", [P, B, P])
        resid = sb("resid", [P, B, P])
        xn = sb("xn", [P, B, P])
        xnT = sb("xnT", [P, T])
        ctxT = sb("ctxT", [P, T])
        pad = xn[:, :, :].rearrange("p b t -> p (b t)")
        stackA = sb("stackA", [P, H * T], BF16)
        stackB = sb("stackB", [P, H * T], BF16)
        region = sb("region", [P, B * H * HD])
        parts = sb("parts", [P, 6, T], BF16)
        rest = sb("rest", [P, 4, HALF])
        rest4 = rest[:, :, :].rearrange("p (w g) n -> p w g n", w=2)
        probs = sb("probs", [P, 2, T])
        vall = sb("vall", [P, B, P])
        vpad = sb("vpad", [P, 2, 4, SLOT])
        opad = sb("opad", [P, SLOT])
        onorm = sb("onorm", [P, 2, P])
        rsum = sb("rsum", [P, 2, P])
        maxs = sb("maxs", [P, 2, H])
        mres = sb("mres", [P, 2, 2, H])
        mparts = sb("mparts", [P, 2, 3, H], BF16)
        mrow = sb("mrow", [3 * H, 2, P], BF16)
        stats6 = sb("stats6", [P, B, 6])
        stats = sb("stats", [P, B, 2])
        rstd = sb("rstd", [P, B])
        meansq = sb("meansq", [P, B])
        small = sb("small", [P, 8])
        keep = sb("keep", [P, 2])
        keepn = sb("keepn", [P, 3, 2])
        identF = sb("identF", [P, P])
        identB = sb("identB", [P, P], BF16)
        causal = sb("causal", [P, 2, HALF], BF16)
        zeros = sb("zeros", [P, T], BF16)
        ones = sb("ones", [P, T], BF16)
        rows = sb("rows", [H, 3, T], BF16)
        stackC = region[:, :].bitcast(BF16)
        psum = ctx.enter_context(nc.psum_tensor("psum", [P, 8, 512], F32))

        def bank(n, k=1):
            return psum[:, n, :] if k == 1 else psum[:, n:n + k, :].rearrange("p a n -> p (a n)")

        def mat(name):
            return wmat[:, MAT_AT[name][0]:MAT_AT[name][1]]

        def col(name):
            i = COLS.index(name)
            return wcol[:, i:i + 1]

        def row(name, n=1):
            i = ROWS.index(name)
            return wrow[:, i * P:(i + 1) * P].unsqueeze(1).broadcast_to([P, n, P])

        def tok(ap):
            return ap.rearrange("p (b t) -> p b t", t=P)

        class Layer:
            def __init__(self, n, q, k, v, o, scale, kstack, k_in, v_in, bq=None, bk=None, bv=None,
                         self_attn=False):
                self.n, self.q, self.k, self.v, self.o = n, q, k, v, o
                self.scale, self.kstack, self.k_in, self.v_in = scale, kstack, k_in, v_in
                self.bq, self.bk, self.bv = bq, bk, bv
                self.self_attn = self_attn
                self.prev = None

            PER = dict(q_mm=2, k_mm=2, v_mm=2, q_p0=2, q_p1=2, q_p2=2, k_p0=2, k_p1=2, k_p2=2, q_rest=2,
                       k_rest=2, q_stacked0=96, q_stacked1=96, k_stacked0=96, k_stacked1=96, smax_mm=2 * B,
                       max_done=2 * B, msplit=4 * B, mparts=B, mT_mm=B, mT_read=B, mrow_in0=8 * B, mrow_in1=8 * B,
                       s_mm=2 * B, exp_done=2 * B, pv_mm=2 * B, vpad_in=B, v_out=2, rsum=B, onorm=B,
                       z_mm=B, z_read=B, q_kept=0, k_kept=0)

            def sem(self, what):
                return sem(what)

            def past(self, what):
                return ["L0", "L2", "LC", "L3"].index(self.n) * self.PER[what]

            def before(self, b, n):
                return ["L0", "L2", "LC", "L3"].index(self.n) * B + b >= n

            def behind(self, b, lag):
                if lag <= b < B + lag:
                    return self, b - lag
                if b < lag and self.prev and b + STEPS - lag < B:
                    return self.prev, b + STEPS - lag
                return None

            def bank_of(self, what, g):
                if self.n == "L0":
                    return {"k": 2, "v": 4, "q": 6}[what] + g
                if self.n == "L2" and g == 0:
                    return 7
                if self.n == "L2":
                    return {"k": 5, "v": 3, "q": 4}[what]
                return {"k": 2, "v": 2 + g, "q": 7 if g else 3}[what]

        L0 = Layer("L0", "q0", "k0", "v0", "o0", E ** -0.5, stackB, pad, ctxT)
        L2 = Layer("L2", "q2", "k2", "v2", "o2", P ** -0.5, stackB, xnT, xnT, self_attn=True)
        LC = Layer("LC", "qc", "kc", "vc", "oc", E ** -0.5, stackC, ctxT, ctxT, "bq_c", "bk_c", "bv_c")
        LC.prev = L2
        L3 = Layer("L3", "q3", "k3", "v3", "o3", E ** -0.5, stackB, ctxT, ctxT, "bq_3", "bk_3", "bv_3")

        def heads(e):
            return [(s, 2 * e + s // 4, s % 4) for s in range(8)]

        def pe_k(e, L, g):
            e.matmul(bank(L.bank_of("k", g)), mat(L.k), L.k_in[:, g * HALF:(g + 1) * HALF],
                     start=True, stop=True).then_inc(L.sem("k_mm"), 1)

        def pe_v(e, L, g):
            for b in range(4):
                at = (4 * g + b) * P
                mm = e.matmul(bank(L.bank_of("v", g))[:, b * P:(b + 1) * P], L.v_in[:, at:at + P], mat(L.v),
                              start=True, stop=True)
            mm.then_inc(L.sem("v_mm"), 1)

        def pe_q(e, L, g):
            e.matmul(bank(L.bank_of("q", g)), mat(L.q), xnT[:, g * HALF:(g + 1) * HALF],
                     start=True, stop=True).then_inc(L.sem("q_mm"), 1)

        kept = mat("a1").rearrange("p (w g n) -> p w g n", w=2, g=2)

        def source(L, name, g):
            return kept[:, "qk".index(name), g, :] if L.self_attn else bank(L.bank_of(name, g))

        def left(L, name, g):
            return (kept if L.self_attn else rest4)[:, "qk".index(name), g, :]

        def part(name, n, g):
            return parts[:, 3 * "qk".index(name) + n, g * HALF:(g + 1) * HALF]

        def wait_half(e, L, what, g):
            e.wait_ge(L.sem(what), L.past(what) + g + 1)

        def act_p0(e, L, name, g):
            wait_half(e, L, f"{name}_kept" if L.self_attn else f"{name}_mm", g)
            bias = L.bk if name == "k" else L.bq
            e.activation(part(name, 0, g), source(L, name, g), ACT.Identity,
                         bias=col(bias) if bias else 0.0).then_inc(L.sem(f"{name}_p0"), 1)

        def act_p1(e, L, name, g):
            wait_half(e, L, f"{name}_rest", g)
            e.copy(part(name, 1, g), left(L, name, g)).then_inc(L.sem(f"{name}_p1"), 1)

        def dve_kept(e, L, name, g, src=None):
            if src is None:
                wait_half(e, L, f"{name}_mm", g)
                src = bank(L.bank_of(name, g))
            e.tensor_tensor(
                source(L, name, g).rearrange("p (b c t) -> p b c t", c=2, t=BLOCK),
                src.rearrange("p (b c t) -> p b c t", c=2, t=BLOCK),
                keep[:, :].unsqueeze(1).unsqueeze(3).broadcast_to([P, 4, 2, BLOCK]),
                ALU.mult).then_inc(L.sem(f"{name}_kept"), 1)

        def dve_rest(e, L, name, g):
            bias = L.bk if name == "k" else L.bq
            wait_half(e, L, f"{name}_p0", g)
            e.scalar_tensor_tensor(out=left(L, name, g), in0=source(L, name, g),
                                   scalar=col(bias) if bias else 0.0, in1=part(name, 0, g),
                                   op0=ALU.add, op1=ALU.subtract).then_inc(L.sem(f"{name}_rest"), 1)

        def dve_p2(e, L, name, g):
            wait_half(e, L, f"{name}_p1", g)
            e.tensor_tensor(part(name, 2, g), left(L, name, g), part(name, 1, g), ALU.subtract)\
             .then_inc(L.sem(f"{name}_p2"), 1)

        def dve_v(e, L, g):
            wait_half(e, L, "v_mm", g)
            out, src = L.vall[:, 4 * g:4 * g + 4, :], tok(bank(L.bank_of("v", g)))
            if L.bv:
                e.tensor_tensor(out, src, row(L.bv, 4), ALU.add).then_inc(L.sem("v_out"), 1)
            else:
                e.tensor_copy(out, src).then_inc(L.sem("v_out"), 1)

        def sync_stack(e, L, name, g, some=(0, 1, 2)):
            stack = L.kstack if name == "k" else stackA
            slots = K_SLOTS if name == "k" else Q_SLOTS
            at = slice(g * HALF, (g + 1) * HALF)
            for n, p in sorted(((n, p) for n, p in enumerate(slots) if p in some), key=lambda s: s[1]):
                wait_half(e, L, f"{name}_p{p}", g)
                e.dma_start(stack_rows(stack, E * n, E)[:, :, at], part(name, p, g))\
                 .then_inc(L.sem(f"{name}_stacked{g}"), 16)

        def stack_rows(stack, r, n):
            return stack[r:r + n, :].rearrange("d (h t) -> d h t", h=H)

        N_ST = 16 * len(Q_SLOTS)

        def pe_scores_max(e, L, b, half):
            if b % 4 == 0 and half == 0:
                g = b // 4
                for what in (f"q_stacked{g}", f"k_stacked{g}"):
                    e.wait_ge(L.sem(what), L.past(what) + N_ST)
            for name, count in (L.extra2 if half else L.extra).get(b, []):
                e.wait_ge(sem(name), count)
            if L.before(b, 1):
                e.wait_ge(L.sem("max_done"), L.past("max_done") + 2 * b + half - 1)
            for s, i, j in heads(half):
                at = (4 * i + j) * T + b * P
                mm = e.matmul(bank(2 * half, 2)[:, s * P:(s + 1) * P], stackA[:, at:at + P],
                              L.kstack[:, at:at + P], start=(s % 4 == 0 or not L.self_attn),
                              stop=not L.self_attn, skip_group_check=True)
                if L.self_attn and s % 4 == 3:
                    mm = e.matmul(bank(2 * half + s // 4), identB[:, :], causal[:, 0, :],
                                  start=False, stop=True, skip_group_check=True)
            mm.then_inc(L.sem("smax_mm"), 1)

        def pe_max_rows(e, L, b):
            e.wait_ge(L.sem("mparts"), L.past("mparts") + b + 1)
            if L.before(b, 3):
                e.wait_ge(L.sem("z_read"), L.past("z_read") + b - 2)
            if L in (LC, L3) and b == 2:
                e.wait_ge(L.sem("q_rest"), L.past("q_rest") + 2)
            if L is L3 and b == 1:
                e.wait_ge(sem("ff_read"), 2)
            if L is L2 and b == 0:
                e.wait_ge(L1("z_read"), B // 2)
            t = bank(6 + (b + 1) % 2)[0:3 * H, 384:384 + P // 2].bitcast(BF16)
            e.transpose(t, mparts[:, b % 2, :, :].rearrange("p a h -> p (a h)"), identB[:, :])\
             .then_inc(L.sem("mT_mm"), 1)

        def pe_scores(e, L, b, half):
            if L is L0 and b == 0 and half == 0:
                e.wait_ge(L1("v_out"), 2 * B)
            if L.self_attn and b == 0 and half == 0:
                e.wait_ge(L.sem("k_kept"), L.past("k_kept") + 2)
                e.wait_ge(L.sem("q_kept"), L.past("q_kept") + 2)
            if half == 0:
                e.wait_ge(L.sem(f"mrow_in{b % 2}"), L.past(f"mrow_in{b % 2}") + 16 * (b // 2 + 1))
            if L.before(b, 1) or half:
                e.wait_ge(L.sem("exp_done"), L.past("exp_done") + 2 * b + half)
            for s, i, j in heads(half):
                at = (4 * i + j) * T + b * P
                mm = e.matmul(bank(4, 2)[:, s * P:(s + 1) * P], L.kstack[:, at:at + P],
                              stackA[:, at:at + P], start=(s % 4 == 0 or not L.self_attn),
                              stop=not L.self_attn, skip_group_check=True)
                if L.self_attn and s % 4 == 3:
                    mm = e.matmul(bank(4 + s // 4), identB[:, :], causal[:, 1, :],
                                  start=False, stop=True, skip_group_check=True)
            mm.then_inc(L.sem("s_mm"), 1)

        def pe_out(e, L, b, half, turned):
            e.wait_ge(L.sem("exp_done"), L.past("exp_done") + 2 * b + half + 1)
            o = bank(6 + b % 2)
            if half == 0:
                e.wait_ge(L.sem("vpad_in"), L.past("vpad_in") + b + 1)
                if L.before(b, 2):
                    e.wait_ge(L.sem("z_read"), L.past("z_read") + b - 1)
            e.wait_ge(L.sem("mT_read"), turned)
            for n, (s, i, j) in enumerate(heads(half)):
                pt = probs[:, half, s * P:(s + 1) * P]
                rows_ = slice(32 * j, 32 * j + 32)
                e.matmul(o[rows_, 0:P], vpad[:, b % 2, j, 32 * i:32 * i + 32], pt,
                         start=(i == 0), stop=(i == 3), skip_group_check=True)
            for n, (s, i, j) in enumerate(heads(half)):
                pt = probs[:, half, s * P:(s + 1) * P]
                rows_ = slice(32 * j, 32 * j + 32)
                mm = e.matmul(o[rows_, P:2 * P], opad[:, 32 * i:32 * i + 32], pt,
                              start=False, stop=(i == 3), skip_group_check=True)
            mm.then_inc(L.sem("pv_mm"), 1)

        def pe_z(e, L, b):
            e.wait_ge(L.sem("onorm"), L.past("onorm") + b + 1)
            e.matmul(bank(6 + b % 2)[:, 2 * P:3 * P], onorm[:, b % 2, :], mat(L.o),
                     start=True, stop=True).then_inc(L.sem("z_mm"), 1)

        def product_of(L, b):
            it = L.behind(b, 4)
            return it if it and it[1] < B - 1 else None

        def pe_attn(e, L, steps, before=None, between=None, after=None, meanwhile=None):
            for b in range(steps):
                late, last, product = L.behind(b, 2), L.behind(b, 3), product_of(L, b)
                turned = L.past("mT_read") + min(b, B)
                joint = L.prev and b < 2
                if before:
                    before(b)
                if b < B and not joint:
                    pe_scores_max(e, L, b, 0)
                if product:
                    pe_z(e, *product)
                if b < B and not joint:
                    pe_scores_max(e, L, b, 1)
                if late:
                    pe_scores(e, *late, 0)
                if 1 <= b <= B and not joint:
                    pe_max_rows(e, L, b - 1)
                if between:
                    between(b)
                if last:
                    other_bank = 3 <= b <= B or (b == 1 and joint)
                    pe_out(e, *last, 1, turned - 1 if other_bank else turned)
                if late:
                    pe_scores(e, *late, 1)
                    pe_out(e, *late, 0, turned)
                if joint:
                    pe_scores_max(e, L, b, 0)
                    pe_scores_max(e, L, b, 1)
                if joint and b == 1:
                    e.wait_ge(last[0].sem("onorm"), last[0].past("onorm") + B)
                    pe_max_rows(e, L, 0)
                    e.wait_ge(L.sem("mT_read"), turned)
                if last and last[1] == B - 1:
                    if meanwhile and last[0] is L:
                        meanwhile()
                    pe_z(e, *last)
                if after:
                    after(b)

        def act_max_rows(e, L, b):
            e.wait_ge(L.sem("mT_mm"), L.past("mT_mm") + b + 1)
            if L.before(b, 2):
                e.wait_ge(L.sem(f"mrow_in{b % 2}"), L.past(f"mrow_in{b % 2}") + 16 * (b // 2))
            t = bank(6 + (b + 1) % 2)[0:3 * H, 384:384 + P // 2].bitcast(BF16)
            e.copy(mrow[:, b % 2, :], t).then_inc(L.sem("mT_read"), 1)

        def act_exp(e, L, b, half):
            e.wait_ge(L.sem("s_mm"), L.past("s_mm") + 2 * b + half + 1)
            if L.before(b, 1):
                e.wait_ge(L.sem("pv_mm"), L.past("pv_mm") + 2 * b + half - 1)
            e.activation(probs[:, half, :], bank(4, 2), ACT.Exp, scale=L.scale)\
             .then_inc(L.sem("exp_done"), 1)

        def act_attn(e, L, steps, before=None, between=None, after=None):
            for b in range(steps):
                late = L.behind(b, 2)
                if before:
                    before(b)
                if 1 <= b <= B:
                    act_max_rows(e, L, b - 1)
                if late:
                    act_exp(e, *late, 0)
                if between:
                    between(b)
                if late:
                    act_exp(e, *late, 1)
                if after:
                    after(b)

        def sync_rows(e, L, b):
            e.wait_ge(L.sem("mT_read"), L.past("mT_read") + b + 1)
            e.dma_start(stack_rows(stackA, ROW_MAX, 3)[:, :, b * P:(b + 1) * P], mrow[:, b % 2, :])\
             .then_inc(L.sem(f"mrow_in{b % 2}"), 16)

        def pool_v(e, L, b):
            e.wait_ge(L.sem("v_out"), L.past("v_out") + b // 4 + 1)
            if L.before(b, 2):
                e.wait_ge(L.sem("pv_mm"), L.past("pv_mm") + 2 * b - 2)
            e.tensor_copy(
                vpad[:, b % 2, :, :].rearrange("p j (i c) -> p j i c", c=40)[:, :, :, 0:E],
                L.vall[:, b, :].rearrange("p (j i d) -> p j i d", i=4, d=E)).then_inc(L.sem("vpad_in"), 1)

        def pool_attn(e, L, steps, before=None, after=None):
            for b in range(steps):
                late = L.behind(b, 2)
                if late:
                    pool_v(e, *late)
                if before:
                    before(b)
                if b < B:
                    pool_split_max(e, L, b)
                if after:
                    after(b)

        def pool_split_max(e, L, b):
            w = b % 2
            chain, n = L.sem("msplit"), L.past("msplit") + 4 * b
            e.wait_ge(L.sem("max_done"), L.past("max_done") + 2 * b + 2)
            if L.before(b, 2):
                e.wait_ge(L.sem("mT_mm"), L.past("mT_mm") + b - 1)
            e.tensor_copy(mparts[:, w, 0, :], maxs[:, w, :]).then_inc(chain, 1)
            e.wait_ge(chain, n + 1)
            e.tensor_tensor(mres[:, w, 0, :], maxs[:, w, :], mparts[:, w, 0, :], ALU.subtract).then_inc(chain, 1)
            e.wait_ge(chain, n + 2)
            e.tensor_copy(mparts[:, w, 1, :], mres[:, w, 0, :]).then_inc(chain, 1)
            e.wait_ge(chain, n + 3)
            e.tensor_tensor(mres[:, w, 1, :], mres[:, w, 0, :], mparts[:, w, 1, :], ALU.subtract).then_inc(chain, 1)
            e.wait_ge(chain, n + 4)
            e.tensor_copy(mparts[:, w, 2, :], mres[:, w, 1, :]).then_inc(L.sem("mparts"), 1)

        def dve_max(e, L, b, half):
            e.wait_ge(L.sem("smax_mm"), L.past("smax_mm") + 2 * b + half + 1)
            if L.before(b, 2) and half == 0:
                e.wait_ge(L.sem("mparts"), L.past("mparts") + b - 1)
            e.tensor_reduce(maxs[:, b % 2, 8 * half:8 * half + 8],
                            bank(2 * half, 2).rearrange("p (h k) -> p h k", k=P), AX.X, ALU.max, negate=True)\
             .then_inc(L.sem("max_done"), 1)

        def dve_norm(e, L, b):
            o = bank(6 + b % 2)
            e.wait_ge(L.sem("pv_mm"), L.past("pv_mm") + 2 * b + 2)
            e.reciprocal(rsum[:, b % 2, :], o[:, P:2 * P]).then_inc(L.sem("rsum"), 1)
            e.wait_ge(L.sem("rsum"), L.past("rsum") + b + 1)
            if L.before(b, 2):
                e.wait_ge(L.sem("z_mm"), L.past("z_mm") + b - 1)
            e.tensor_tensor(onorm[:, b % 2, :], o[:, 0:P], rsum[:, b % 2, :], ALU.mult)\
             .then_inc(L.sem("onorm"), 1)

        def dve_z(e, L, b):
            e.wait_ge(L.sem("z_mm"), L.past("z_mm") + b + 1)
            e.wait_ge(sem(f"resid_{L.n}"), b // 4 + 1)
            e.tensor_tensor(x[:, b, :], bank(6 + b % 2)[:, 2 * P:3 * P], resid[:, b, :], ALU.add)\
             .then_inc(L.sem("z_read"), 1)

        def dve_stats6(e, n, b, ready, past=0):
            e.wait_ge(ready, past + b + 1)
            e.bn_stats(stats6[:, b, :], x[:, b, :]).then_inc(sem(f"bn_{n}"), 1)

        def dve_aggr(e, n, b):
            e.wait_ge(sem(f"bn_{n}"), b + 1)
            e.bn_aggr(stats[:, b, :], stats6[:, b, :]).then_inc(sem(f"stats_{n}"), 1)

        def dve_stats(e, n, b, ready, past=0):
            dve_stats6(e, n, b, ready, past)
            dve_aggr(e, n, b)

        def dve_attn(e, L, steps, before=None, between=None, after=None):
            for b in range(steps):
                last, product = L.behind(b, 3), product_of(L, b)
                joint = last and last[0] is not L
                if before:
                    before(b)
                if product:
                    dve_z(e, *product)
                if joint:
                    dve_norm(e, *last)
                if b < B:
                    dve_max(e, L, b, 0)
                if product:
                    M, p = product
                    dve_stats6(e, M.n, p, M.sem("z_read"), M.past("z_read"))
                if b < B:
                    dve_max(e, L, b, 1)
                if product:
                    dve_aggr(e, M.n, p)
                if between:
                    between(b)
                if last and not joint:
                    dve_norm(e, *last)
                if after:
                    after(b)
                if last and last[1] == B - 1:
                    dve_z(e, *last)
                    dve_stats(e, last[0].n, B - 1, last[0].sem("z_read"), last[0].past("z_read"))

        def pool_resid(e, n, bias, g, ready, count):
            e.wait_ge(sem(ready), count)
            e.tensor_tensor(resid[:, 4 * g:4 * g + 4, :], x[:, 4 * g:4 * g + 4, :], row(bias, 4), ALU.add)\
             .then_inc(sem(f"resid_{n}"), 1)

        def pool_rstd(e, n, src, kind, eps, b0, nb):
            done = sem(f"rs_{n}")
            rs = rstd[:, b0:b0 + nb]
            count = 2 * (b0 // nb)
            e.wait_ge(sem(f"stats_{src}"), b0 + nb)
            if kind == "rms":
                e.wait_ge(sem(f"msq_{n}"), count + 2)
                var = meansq[:, b0:b0 + nb]
            else:
                var = stats[:, b0:b0 + nb, 1]
            e.tensor_scalar(rs, var, eps, None, ALU.add).then_inc(done, 1)
            e.wait_ge(done, count + 1)
            e.tensor_tensor(rs, rs, small[:, 0:1].broadcast_to([P, nb]), ALU.pow).then_inc(done, 1)

        def dve_msq(e, n, src, g):
            at = slice(4 * g, 4 * g + 4)
            m = sem(f"msq_{n}")
            e.wait_ge(sem(f"stats_{src}"), 4 * g + 4)
            e.tensor_tensor(meansq[:, at], stats[:, at, 0], stats[:, at, 0], ALU.mult).then_inc(m, 1)
            e.wait_ge(m, 2 * g + 1)
            e.tensor_tensor(meansq[:, at], meansq[:, at], stats[:, at, 1], ALU.add).then_inc(m, 1)

        def dve_xn(e, n, kind, b0, nb):
            e.wait_ge(sem(f"rs_{n}"), 2 * (b0 // nb) + 2)
            for b in range(b0, b0 + nb):
                if kind == "rms":
                    e.tensor_scalar(xn[:, b, :], x[:, b, :], rstd[:, b:b + 1], None, ALU.mult)\
                     .then_inc(sem(f"xn_{n}"), 1)
                else:
                    e.tensor_scalar(xn[:, b, :], x[:, b, :], stats[:, b, 0:1], rstd[:, b:b + 1],
                                    ALU.subtract, ALU.mult).then_inc(sem(f"xn_{n}"), 1)

        def pe_turn(e, n, g, to, plain=False):
            for b in range(4):
                if not plain:
                    e.wait_ge(sem(f"xn_{n}"), 4 * g + b + 1)
                mm = e.transpose(bank(to)[:, b * P:(b + 1) * P], (x if plain else xn)[:, 4 * g + b, :], identF[:, :])
            mm.then_inc(sem(f"turn_{n}"), 1)

        def act_turn(e, n, g, to, gain=None, bias=None):
            e.wait_ge(sem(f"turn_{n}"), g + 1)
            e.activation(xnT[:, g * HALF:(g + 1) * HALF], bank(to), ACT.Identity,
                         scale=col(gain) if gain else 1.0, bias=col(bias) if bias else 0.0)\
             .then_inc(sem(f"xnT_{n}"), 1)

        u32 = stackA[:, :].bitcast(F32).rearrange("p (w h k) -> p w h k", w=2, h=H)
        v1 = region[:, 0:B * H * HD].rearrange("p (b n) -> p b n", b=B)
        pT = rest[:, :, :].rearrange("p (a c) n -> p a (c n)", a=2)
        on1 = [resid[:, 2 * t:2 * t + 2, :] for t in range(4)] + \
              [tok(wmat[:, t * 2 * P:(t + 1) * 2 * P]) for t in range(2)] + \
              [xn[:, 4 + 2 * t:6 + 2 * t, :] for t in range(2)]
        z1 = onorm[:, :, :].rearrange("p a q -> p (a q)")
        a1 = mat("a1").rearrange("p (h n) -> p h n", n=P)
        L1 = lambda what: sem(f"{what}_L1")

        def pe_a1(e, g):
            if g >= 1:
                e.wait_ge(sem("a_out"), g)
            for t in range(4):
                for h in range(2):
                    r = slice(HD * h, HD * h + HD)
                    at = 2 * (4 * g + t)
                    mm = e.matmul(bank(h)[:, t * P:(t + 1) * P], a1[r, at + 1, :], a1[r, at, :],
                                  start=True, stop=True)
            mm.then_inc(sem("a_mm"), 1)

        def act_a1(e):
            for g in range(NT // 4):
                e.wait_ge(sem("a_mm"), g + 1)
                e.copy(a1[:, 8 * g:8 * g + 8, :].rearrange("p (t h) n -> p h t n", h=2),
                       psum[:, 0:2, :].rearrange("p h (t n) -> p h t n", n=P)).then_inc(sem("a_out"), 1)

        def v1_bank(n):
            return bank((0 if n < B else 4) + n % 2)

        def pe_v1(e, chunks):
            for n in chunks:
                if n >= 2 and n != B and n != B + 1:
                    e.wait_ge(L1("v_out"), n - 1)
                e.matmul(v1_bank(n), ctxT[:, n // 2 * P:(n // 2 + 1) * P],
                         mat("v1")[:, n % 2 * 512:(n % 2 + 1) * 512], start=True, stop=True)\
                 .then_inc(L1("v_mm"), 1)

        def act_v1(e, chunks):
            for n in chunks:
                e.wait_ge(L1("v_mm"), n + 1)
                e.copy(v1[:, n // 2, n % 2 * 512:(n % 2 + 1) * 512], v1_bank(n)).then_inc(L1("v_out"), 1)

        V1_IN_STEP = [range(8, 11), range(11, 2 * B)]

        def pe_u1(e, i, g):
            wait = g - 1 if i == 0 else i * NT + g
            if (i, g) == (1, 4):
                e.wait_ge(sem("xnT_T1"), 2)
            if wait >= 1:
                e.wait_ge(L1("u_out"), wait)
            for h in range(2):
                mm = e.matmul(bank(7 if i else g % 2)[:, 2 * h * P:2 * (h + 1) * P], a1[:, 2 * g + h, :],
                              ctxT[:, 2 * i * P:2 * (i + 1) * P], start=True, stop=True)
            mm.then_inc(L1("u_mm"), 1)

        def act_u1(e, i, g):
            e.wait_ge(L1("u_mm"), i * NT + g + 1)
            e.copy(u32[:, i % 2, 2 * g:2 * g + 2, :], bank(7 if i else g % 2).rearrange("p (h k) -> p h k", h=2))\
             .then_inc(L1("u_out"), 1)

        def chunks(b):
            if b // 2 + 1 >= B // 2:
                return [(), (), (), ()]
            return [(4 * (b % 2) + n,) for n in range(4)]

        def pe_s1(e, b, half):
            i, bb = b // 2, b % 2
            e.wait_ge(L1("u_out"), i * NT + 4 * half + 4 if b else NT)
            if b >= 1:
                e.wait_ge(L1("exp_done"), 2 * b + half - 1)
            for g in range(2):
                h0 = 8 * half + 4 * g
                mm = e.matmul(bank(2 * half + g), xnT[:, b * P:(b + 1) * P],
                              u32[:, i % 2, h0:h0 + 4, bb * P:(bb + 1) * P], start=True, stop=True)
            mm.then_inc(L1("s_mm"), 1)

        def pe_turn1(e, b, half):
            e.wait_ge(L1("norm"), 2 * b + half + 1)
            if 2 * b + half >= 1:
                e.wait_ge(L1("pT_out"), 2 * b + half)
            for s in range(8):
                mm = e.transpose(bank(4, 2)[:, s * P:(s + 1) * P], probs[:, half, s * P:(s + 1) * P], identF[:, :])
            mm.then_inc(L1("turn_mm"), 1)

        def pe_out1(e, b, half):
            e.wait_ge(L1("pT_out"), 2 * b + half + 1)
            if 2 * b + half >= 1:
                e.wait_ge(L1("o_out"), 2 * b + half)
            if b >= 2 and b % 2 == 0 and half == 0:
                e.wait_ge(L1("z_read"), b // 2)
            for s in range(8):
                t, pp, h = s // 2, s % 2, 8 * half + s
                mm = e.matmul(bank(6)[HD * pp:HD * pp + HD, t * P:(t + 1) * P],
                              v1[:, b, h * HD:(h + 1) * HD], pT[:, half, s * P:(s + 1) * P],
                              start=True, stop=True)
            mm.then_inc(L1("pv_mm"), 1)

        def z1_bank(i):
            return bank(7 if i == B // 2 - 1 else 6)

        def pe_z1(e, i, tiles=range(NT)):
            e.wait_ge(L1("o_out"), 4 * (i + 1) - (tiles[-1] < NT - 1))
            for t in tiles:
                mm = e.matmul(z1_bank(i)[:, 0:2 * P], mat("o1")[:, t * P:(t + 1) * P], on1[t],
                              start=(t == 0), stop=(t == NT - 1))
            if tiles[-1] == NT - 1:
                mm.then_inc(L1("z_mm"), 1)

        def pe_zturn1(e, i):
            e.wait_ge(L1("z_out"), i + 1)
            for bb in range(2):
                mm = e.transpose(z1_bank(i)[:, (2 + bb) * P:(3 + bb) * P], z1[:, bb * P:(bb + 1) * P], identF[:, :])
            mm.then_inc(L1("zt_mm"), 1)

        def pe_l1(e, more):
            pe_s1(e, 0, 0)
            pe_s1(e, 0, 1)
            for b in range(B):
                c = chunks(b)
                if b + 1 < B:
                    pe_s1(e, b + 1, 0)
                if b >= 2 and b % 2 == 0:
                    pe_z1(e, b // 2 - 1)
                for g in c[0]:
                    pe_u1(e, b // 2 + 1, g)
                more(b, 0)
                if b >= 2 and b % 2 == 0:
                    pe_zturn1(e, b // 2 - 1)
                pe_turn1(e, b, 0)
                for g in c[1]:
                    pe_u1(e, b // 2 + 1, g)
                more(b, 1)
                pe_out1(e, b, 0)
                for g in c[2]:
                    pe_u1(e, b // 2 + 1, g)
                more(b, 2)
                pe_turn1(e, b, 1)
                for g in c[3]:
                    pe_u1(e, b // 2 + 1, g)
                more(b, 3)
                if b + 1 < B:
                    pe_s1(e, b + 1, 1)
                if b == B - 1:
                    e.wait_ge(L2.sem("q_kept"), L2.past("q_kept") + 1)
                    pe_z1(e, B // 2 - 1, range(0, NT // 2))
                pe_out1(e, b, 1)
                more(b, 4)
            pe_z1(e, B // 2 - 1, range(NT // 2, NT))

        def act_exp1(e, b, half):
            e.wait_ge(L1("max_done"), 2 * b + half + 1)
            if b >= 1:
                e.wait_ge(L1("turn_mm"), 2 * b + half - 1)
            for s in range(8):
                ins = e.activation(probs[:, half, s * P:(s + 1) * P], bank(2 * half, 2)[:, s * P:(s + 1) * P],
                                   ACT.Exp, bias=maxs[:, b % 2, 8 * half + s:8 * half + s + 1])
            ins.then_inc(L1("exp_done"), 1)

        def act_pT1(e, b, half):
            e.wait_ge(L1("turn_mm"), 2 * b + half + 1)
            if b >= 1:
                e.wait_ge(L1("pv_mm"), 2 * b + half - 1)
            e.copy(pT[:, half, :], bank(4, 2)).then_inc(L1("pT_out"), 1)

        def act_out1(e, b, half):
            e.wait_ge(L1("pv_mm"), 2 * b + half + 1)
            if b >= 2 and b % 2 == 0:
                e.wait_ge(L1("z_mm"), b // 2)
            if b == 0 and half:
                e.wait_ge(sem("turn_T1"), 2)
            src = bank(6).rearrange("p (t q) -> p t q", q=P)
            bb = b % 2
            if half == 0:
                to = resid[:, :, :].rearrange("p (t c) q -> p t c q", c=2)[:, :, bb, :]
                e.copy(to, src).then_inc(L1("o_out"), 1)
            else:
                to = tok(wmat[:, 0:4 * P]).rearrange("p (t c) q -> p t c q", c=2)[:, :, bb, :]
                e.copy(to, src[:, 0:2, :])
                to = xn[:, 4:8, :].rearrange("p (t c) q -> p t c q", c=2)[:, :, bb, :]
                e.copy(to, src[:, 2:4, :]).then_inc(L1("o_out"), 1)

        def act_z1(e, i):
            e.wait_ge(L1("z_mm"), i + 1)
            if i >= 1:
                e.wait_ge(L1("zt_mm"), i)
            e.copy(z1, z1_bank(i)[:, 0:2 * P]).then_inc(L1("z_out"), 1)

        def act_l1(e, more):
            act_exp1(e, 0, 0)
            act_exp1(e, 0, 1)
            for b in range(B):
                c = chunks(b)
                if b >= 2 and b % 2 == 0:
                    act_z1(e, b // 2 - 1)
                for g in c[0]:
                    act_u1(e, b // 2 + 1, g)
                more(b, 0)
                act_pT1(e, b, 0)
                for g in c[1]:
                    act_u1(e, b // 2 + 1, g)
                more(b, 1)
                if b + 1 < B:
                    act_exp1(e, b + 1, 0)
                for g in c[2]:
                    act_u1(e, b // 2 + 1, g)
                act_out1(e, b, 0)
                more(b, 2)
                act_pT1(e, b, 1)
                for g in c[3]:
                    act_u1(e, b // 2 + 1, g)
                more(b, 3)
                act_out1(e, b, 1)
                if b + 1 < B:
                    act_exp1(e, b + 1, 1)
            act_z1(e, B // 2 - 1)

        def dve_max1(e, b, half):
            e.wait_ge(L1("s_mm"), 2 * b + half + 1)
            e.tensor_reduce(maxs[:, b % 2, 8 * half:8 * half + 8],
                            bank(2 * half, 2).rearrange("p (h k) -> p h k", k=P), AX.X, ALU.max, negate=True)\
             .then_inc(L1("max_done"), 1)

        def dve_norm1(e, b, half):
            n = 2 * b + half + 1
            p8 = probs[:, half, :].rearrange("p (h k) -> p h k", k=P)
            sums = mres[:, half, 0, 0:8]
            rec = mres[:, half, 1, 0:8]
            e.wait_ge(L1("exp_done"), n)
            e.tensor_reduce(sums, p8, AX.X, ALU.add).then_inc(L1("sum"), 1)
            e.wait_ge(L1("sum"), n)
            e.reciprocal(rec, sums).then_inc(L1("rec"), 1)
            e.wait_ge(L1("rec"), n)
            e.tensor_tensor(p8, p8, rec.unsqueeze(2).broadcast_to([P, 8, P]), ALU.mult).then_inc(L1("norm"), 1)

        def dve_z1(e, i):
            e.wait_ge(L1("zt_mm"), i + 1)
            xs = x[:, 2 * i:2 * i + 2, :]
            e.tensor_tensor(xs, tok(z1_bank(i)[:, 2 * P:4 * P]), xs, ALU.add).then_inc(L1("z_read"), 1)
            for b in (2 * i, 2 * i + 1):
                dve_stats(e, "L1", b, L1("z_read"), i - b)

        def dve_l1(e, more):
            dve_max1(e, 0, 0)
            dve_max1(e, 0, 1)
            dve_norm1(e, 0, 0)
            for b in range(B):
                if b + 1 < B:
                    dve_max1(e, b + 1, 0)
                dve_norm1(e, b, 1)
                if b >= 2 and b % 2 == 0:
                    dve_z1(e, b // 2 - 1)
                more(b, 0)
                if b + 1 < B:
                    dve_norm1(e, b + 1, 0)
                more(b, 1)
                if b + 1 < B:
                    dve_max1(e, b + 1, 1)
                more(b, 2)

        hT = mat("a1").rearrange("p (c t) -> p c t", c=4)
        y32 = mat("o1").rearrange("p (g t) -> p g t", g=2)

        def ff_bank(g, n):
            return bank(4 * g + n % 4)

        def pe_f1(e, g, c):
            e.matmul(ff_bank(g, c + 1), mat("f1")[:, c * P:(c + 1) * P], xnT[:, g * HALF:(g + 1) * HALF],
                     start=True, stop=True).then_inc(sem("h_mm"), 1)

        def act_f1(e, g, c):
            e.wait_ge(sem("h_mm"), 4 * g + c + 1)
            e.activation(hT[:, c, :], ff_bank(g, c + 1), ACT.Relu, bias=col(f"f_b{c}")).then_inc(sem("h_out"), 1)

        def pe_f2(e, g):
            e.wait_ge(sem("h_out"), 4 * g + 4)
            for c in range(4):
                mm = e.matmul(ff_bank(g, 1), mat("f2")[:, c * P:(c + 1) * P], hT[:, c, :], start=(c == 0), stop=(c == 3))
            mm.then_inc(sem("f2_mm"), 1)

        def act_f2(e, g):
            e.wait_ge(sem("f2_mm"), g + 1)
            e.copy(y32[:, g, :], ff_bank(g, 1)).then_inc(sem("f2_out"), 1)

        def pe_fturn(e, g):
            e.wait_ge(sem("f2_out"), g + 1)
            for b in range(4):
                mm = e.transpose(ff_bank(g, 2)[:, b * P:(b + 1) * P], y32[:, g, b * P:(b + 1) * P], identF[:, :])
            mm.then_inc(sem("ft_mm"), 1)

        def dve_ff(e, g):
            e.wait_ge(sem("ft_mm"), g + 1)
            e.wait_ge(sem("resid_FF"), g + 1)
            at = slice(4 * g, 4 * g + 4)
            e.tensor_tensor(x[:, at, :], tok(ff_bank(g, 2)), resid[:, at, :], ALU.add).then_inc(sem("ff_read"), 1)

        def done(L, what, n):
            return what, L.past(what) + n

        L0.vall = L2.vall = L3.vall = vall
        LC.vall = tok(mat("v1"))
        L0.extra = {0: [("filled", 16 * 4), ("padrows", 48), ("v_out_L1", 8), done(L0, "k_rest", 2),
                        done(L0, "q_rest", 2), done(L0, "v_out", 2)]}
        L2.extra = {0: [("blockrows", 48)], 2: [("z_read_L1", B // 2)]}
        LC.extra = {0: [("filledC", 16 * 10), ("clearedQ0", 16)], 4: [("clearedQ1", 16)]}
        L3.extra = {0: [("clearedQ0", 32), ("clearedK3", 16), ("ff_read", 1)], 4: [("clearedQ1", 32)]}
        L0.extra2 = {}
        L2.extra2 = {4: [done(L2, "v_out", 2)],
                     5: [done(LC, "k_rest", 1)], 6: [done(LC, "k_rest", 2)], 7: [done(LC, "v_out", 2)]}
        LC.extra2 = {0: [done(LC, "q_rest", 1)], 4: [done(L3, "k_rest", 1)],
                     5: [done(L3, "k_rest", 2)], 6: [done(L3, "v_out", 2)]}
        L3.extra2 = {0: [done(L3, "q_rest", 1)]}

        def fill(e, stack, r, n, src, done):
            for k in range(0, n, E):
                m = min(E, n - k)
                e.dma_start(stack_rows(stack, r + k, m), src[0:m * H, :]).then_inc(done, 16)

        def put_row(e, stack, r, n, src, done):
            e.dma_start(stack_rows(stack, r, n), src).then_inc(done, 16)

        def clear_max(e, L, g):
            e.wait_ge(L.sem("s_mm"), L.past("s_mm") + 8 * (g + 1))
            e.dma_start(stack_rows(stackA, ROW_MAX, 4)[:, :, g * HALF:(g + 1) * HALF], zeros[0:4 * H, 0:HALF])\
             .then_inc(sem(f"clearedQ{g}"), 16)

        def block_row(e, n):
            e.wait_ge(sem("keep"), 4)
            copy = e.copy if e is nc.scalar else e.tensor_copy
            copy(rows[:, n, :].rearrange("p (b c t) -> p b c t", c=2, t=BLOCK),
                 keepn[0:H, n, :].unsqueeze(1).unsqueeze(3).broadcast_to([H, B, 2, BLOCK])).then_inc(sem("rows_done"), 1)

        block = ctx.enter_context(nc.Block())

        @block.sync
        def _(e):
            c0, c1 = MAT_AT["a1"][0], MAT_AT["q2"][0]
            e.dma_start(wmat[:, 0:c0], wmat_d[:, 0:c0]).then_inc(sem("in_w0"), 16)
            e.dma_start(xnT[:, 0:HALF], xt_d[:, 0:HALF]).then_inc(sem("in_xT0"), 16)
            e.dma_start(xnT[:, HALF:T], xt_d[:, HALF:T]).then_inc(sem("in_xT1"), 16)
            e.dma_start(pad[:, :], mask_d.partition_broadcast(P)).then_inc(sem("in_mask"), 16)
            e.dma_start(ctxT[:, :], ctxt_d).then_inc(sem("in_ctx"), 16)
            e.dma_start(wcol[:, :], wcol_d).then_inc(sem("in_cols"), 16)
            e.dma_start(wmat[:, c0:c1], wmat_d[:, c0:c1]).then_inc(sem("in_w1"), 16)
            e.wait_ge(sem("consts"), 2)
            e.wait_ge(sem("blankB"), 1)
            fill(e, stackB, ROW_MAX, 32, ones, sem("filled"))
            e.wait_ge(sem("blankA"), 2)
            sync_stack(e, L0, "q", 0)
            sync_stack(e, L0, "k", 0)
            e.wait_ge(sem("padsplit"), 5)
            for n in range(3):
                put_row(e, stackB, ROW_KEY + n, 1, rows[:, n, :], sem("padrows"))
            sync_stack(e, L0, "q", 1)
            sync_stack(e, L0, "k", 1)
            e.dma_start(x[:, :, :], x_d).then_inc(sem("in_x"), 16)
            e.dma_start(wrow[:, :], wrow_d.partition_broadcast(P)).then_inc(sem("in_rows"), 16)
            for b in range(B):
                sync_rows(e, L0, b)
                if b == 1:
                    e.dma_start(wmat[:, c1:N_MAT], wmat_d[:, c1:N_MAT]).then_inc(sem("in_w2"), 16)
            e.wait_ge(sem("blankB"), 3)
            sync_stack(e, L2, "k", 0)
            e.wait_ge(sem("rows_done"), 3)
            put_row(e, stackB, ROW_KEY, 1, rows[:, 2, :], sem("blockrows"))
            e.wait_ge(sem("blankA"), 6)
            put_row(e, stackA, ROW_BLOCK, 1, rows[:, 0, :], sem("blockrows"))
            put_row(e, stackA, ROW_KEY, 1, rows[:, 1, :], sem("blockrows"))
            sync_stack(e, L2, "q", 0)
            sync_rows(e, L2, 0)
            sync_rows(e, L2, 1)
            sync_stack(e, L2, "k", 1)
            sync_stack(e, L2, "q", 1)
            sync_rows(e, L2, 2)
            fill(e, stackC, ROW_ZERO, 48, zeros, sem("filledC"))
            sync_rows(e, L2, 3)
            fill(e, stackC, ROW_MAX, 32, ones, sem("filledC"))
            sync_rows(e, L2, 4)
            sync_stack(e, LC, "k", 0)
            sync_rows(e, L2, 5)
            sync_stack(e, LC, "k", 1)
            sync_rows(e, L2, 6)
            sync_rows(e, L2, 7)
            clear_max(e, L2, 0)
            sync_stack(e, LC, "q", 0)
            clear_max(e, L2, 1)
            sync_rows(e, LC, 0)
            sync_rows(e, LC, 1)
            sync_stack(e, LC, "q", 1, [0])
            sync_rows(e, LC, 2)
            sync_stack(e, LC, "q", 1, [1, 2])
            put_row(e, stackB, ROW_KEY, 1, zeros[0:H, :], sem("clearedK3"))
            sync_rows(e, LC, 3)
            sync_stack(e, L3, "k", 0)
            sync_rows(e, LC, 4)
            sync_stack(e, L3, "k", 1)
            for b in range(5, B):
                sync_rows(e, LC, b)
            clear_max(e, LC, 0)
            clear_max(e, LC, 1)
            sync_stack(e, L3, "q", 0)
            for b in range(2):
                sync_rows(e, L3, b)
            sync_stack(e, L3, "q", 1, [0])
            sync_rows(e, L3, 2)
            sync_stack(e, L3, "q", 1, [1, 2])
            for b in range(3, B):
                sync_rows(e, L3, b)
            for b in range(B):
                e.wait_ge(sem("out_ready"), b // 2 + 1)
                e.dma_start(out_d[b], xn[:, b, :]).then_inc(sem("stored"), 16)
            e.wait_ge(sem("stored"), 16 * B)

        @block.gpsimd
        def _(e):
            c = sem("consts")
            e.memset(zeros[:, :], 0.0).then_inc(c, 1)
            e.memset(ones[:, :], 1.0).then_inc(c, 1)
            e.memset(stackA[:, :].bitcast(F32), 0.0).then_inc(sem("blankA"), 1)
            e.wait_ge(sem("blankA"), 1)
            e.memset(stackA[ROW_KEY:ROW_MAX, :].bitcast(F32), TWO_ONES).then_inc(sem("blankA"), 1)
            e.wait_ge(sem("blankA"), 2)
            p = sem("pre")
            e.memset(identF[:, :], 0.0).then_inc(p, 1)
            e.memset(identB[:, :], 0.0).then_inc(p, 1)
            e.wait_ge(p, 2)
            for m in (identF, identB):
                e.affine_select(out=m[:, :], in_=m[:, :], compare_op=ALU.not_equal, fill=1.0,
                                base=0, pattern=[[-1, P]], channel_multiplier=1).then_inc(c, 1)
            e.memset(vpad[:, :, :, :], 0.0).then_inc(p, 1)
            e.memset(opad[:, :], 0.0).then_inc(p, 1)
            e.memset(small[:, 0:1], -0.5).then_inc(p, 1)
            e.memset(causal[:, :, :], 0.0).then_inc(p, 1)
            e.wait_ge(p, 6)
            e.memset(opad[:, :].rearrange("p (i c) -> p i c", c=40)[:, :, 0:E], 1.0).then_inc(c, 1)
            cz = causal[:, :, :].rearrange("p a (h k) -> p a h k", k=P)
            e.affine_select(out=cz[:, 0], in_=cz[:, 0], compare_op=ALU.is_ge, fill=CAUSAL,
                            base=0, pattern=[[0, 4], [-1, P]], channel_multiplier=1).then_inc(c, 1)
            e.affine_select(out=cz[:, 1], in_=cz[:, 1], compare_op=ALU.is_ge, fill=CAUSAL,
                            base=0, pattern=[[0, 4], [1, P]], channel_multiplier=-1).then_inc(c, 1)
            def after0(b):
                if b == 1:
                    e.wait_ge(sem("in_rows"), 16)
                    for g in range(2):
                        pool_resid(e, "L0", "bo_0", g, "in_x", 16)
                if b == 8:
                    pool_rstd(e, "N0", "L0", "ln", 1e-5, 0, 4)
                if b == 9:
                    pool_rstd(e, "T1", "X1", "rms", 1e-6, 0, 4)

            pool_attn(e, L0, B + 3, after=after0)
            pool_rstd(e, "N0", "L0", "ln", 1e-5, 4, 4)
            pool_rstd(e, "T1", "X1", "rms", 1e-6, 4, 4)
            f32B = stackB[:, :].bitcast(F32)
            f32A = stackA[:, :].bitcast(F32)
            half = H * T // 4
            e.wait_ge(L0.sem("z_read"), L0.past("z_read") + B)
            e.memset(f32B, 0.0).then_inc(sem("blankB"), 1)
            e.wait_ge(sem("blankB"), 2)
            e.memset(f32B[ROW_MAX:P, :], TWO_ONES).then_inc(sem("blankB"), 1)
            e.wait_ge(sem("blankB"), 3)
            pool_rstd(e, "T2", "L1", "ln", 1e-5, 0, 4)
            e.wait_ge(L1("s_mm"), 2 * 6)
            e.memset(f32A[:, 0:half], 0.0).then_inc(sem("blankA"), 1)
            e.wait_ge(sem("blankA"), 3)
            e.memset(f32A[ROW_KEY:ROW_MAX, 0:half], TWO_ONES).then_inc(sem("blankA"), 1)
            e.wait_ge(sem("blankA"), 4)
            block_row(e, 0)
            e.wait_ge(L1("s_mm"), 2 * B)
            e.memset(f32A[:, half:], 0.0).then_inc(sem("blankA"), 1)
            e.wait_ge(sem("blankA"), 5)
            e.memset(f32A[ROW_KEY:ROW_MAX, half:], TWO_ONES).then_inc(sem("blankA"), 1)
            e.wait_ge(sem("blankA"), 6)

            def during2(b):
                if b == 0:
                    pool_rstd(e, "T2", "L1", "ln", 1e-5, 4, 4)
                if b == 1:
                    for g in range(2):
                        pool_resid(e, "L2", "bo_2", g, "stats_L1", B)
                if b == 8:
                    pool_resid(e, "LC", "bo_c", 0, "stats_L2", 4)

            def duringC(b):
                if b == 1:
                    pool_rstd(e, "TC", "L2", "ln", 1e-5, 4, 4)
                    pool_resid(e, "LC", "bo_c", 1, "stats_L2", B)
                if b == 8:
                    pool_resid(e, "FF", "b_ff", 0, "stats_LC", 4)

            def first_half(n, src):
                return lambda b: pool_rstd(e, n, src, "ln", 1e-5, 0, 4) if b == 7 else None

            pool_attn(e, L2, STEPS, before=first_half("TC", "L2"), after=during2)
            pool_attn(e, LC, B + 3, before=first_half("TF", "LC"), after=duringC)
            pool_rstd(e, "TF", "LC", "ln", 1e-5, 4, 4)
            pool_resid(e, "FF", "b_ff", 1, "stats_LC", B)
            pool_resid(e, "L3", "bo_3", 0, "ff_read", 1)
            def after3(b):
                if b == 2:
                    pool_resid(e, "L3", "bo_3", 1, "ff_read", 2)
                if b in (7, 8, 9):
                    pool_rstd(e, "N3", "L3", "ln", 1e-5, 2 * b - 14, 2)

            pool_attn(e, L3, B + 3, after=after3)
            pool_rstd(e, "N3", "L3", "ln", 1e-5, 6, 2)

        @block.tensor
        def _(e):
            e.wait_ge(sem("in_w0"), 16)
            for g in range(2):
                e.wait_ge(sem(f"in_xT{g}"), 16)
                pe_q(e, L0, g)
            e.wait_ge(sem("padmul"), 1)
            e.wait_ge(sem("in_ctx"), 16)
            for g in range(2):
                pe_k(e, L0, g)
            e.wait_ge(sem("in_w1"), 16)
            pe_a1(e, 0)
            for g in range(2):
                pe_v(e, L0, g)
            pe_a1(e, 1)
            e.wait_ge(sem("a_out"), NT // 4)
            pe_v1(e, range(8))
            e.wait_ge(sem("consts"), 7)

            def after0(b):
                if b < 2:
                    pe_v1(e, V1_IN_STEP[b])
                if b == 9:
                    for g in range(3):
                        pe_u1(e, 0, g)

            def meanwhile0():
                for g in range(3, 6):
                    pe_u1(e, 0, g)

            pe_attn(e, L0, B + 3, after=after0, meanwhile=meanwhile0)
            pe_turn(e, "T1", 0, 2)
            for g in range(6, NT):
                pe_u1(e, 0, g)
            e.wait_ge(L0.sem("z_read"), L0.past("z_read") + B)
            e.wait_ge(sem("xnT_T1"), 1)

            def during1(b, place):
                if (b, place) == (0, 3):
                    e.wait_ge(L1("u_out"), NT + 4)
                    pe_turn(e, "T1", 1, 7)
                if (b, place) == (5, 3):
                    e.wait_ge(L1("u_out"), NT * B // 2)
                    pe_turn(e, "T2", 0, 7)
                if (b, place) == (5, 4):
                    e.wait_ge(sem("xnT_T2"), 1)
                    pe_k(e, L2, 0)
                if (b, place) == (6, 0):
                    e.wait_ge(sem("router"), 3)
                    e.matmul(bank(7)[:, 0:2], mat("r1"), small[:, 4:6], start=True, stop=True)\
                     .then_inc(sem("r_mm"), 1)
                if (b, place) == (6, 1):
                    e.wait_ge(sem("r_hidden"), 2)
                    e.matmul(bank(7)[:, 0:2], mat("v1")[:, 0:P], small[:, 6:8], start=True, stop=True)\
                     .then_inc(sem("r_mm"), 1)
                if (b, place) == (6, 2):
                    e.wait_ge(sem("keep"), 1)
                    pe_v(e, L2, 0)
                if (b, place) == (6, 4):
                    e.wait_ge(L2.sem("v_out"), L2.past("v_out") + 1)
                    pe_q(e, L2, 0)

            e.wait_ge(sem("in_w2"), 16)
            pe_l1(e, during1)

            def free(L, b):
                e.wait_ge(L.sem("max_done"), L.past("max_done") + 2 * b)

            def turn_second(L, n, b, plain=False):
                if b == 2:
                    if L is LC:
                        e.wait_ge(L2.sem("z_read"), L2.past("z_read") + B)
                    e.wait_ge(L.sem("mT_read"), L.past("mT_read") + 1)
                    pe_turn(e, n, 1, 7, plain)

            def q_second(L, n, b):
                if b == 2:
                    e.wait_ge(sem(f"xnT_{n}"), 2)
                    pe_q(e, L, 1)

            def next_kv(L, N, b, at):
                if at <= b <= at + 2:
                    free(L, b)
                if b in (at, at + 1):
                    pe_k(e, N, b - at)
                if b == at + 2:
                    pe_v(e, N, 0)
                    pe_v(e, N, 1)

            def before2(b):
                if b == 1:
                    pe_zturn1(e, B // 2 - 1)
                if b == 2:
                    e.wait_ge(sem("xnT_T2"), 2)
                    pe_k(e, L2, 1)
                    pe_q(e, L2, 1)
                if b == 4:
                    free(L2, 4)
                    pe_v(e, L2, 1)
                next_kv(L2, LC, b, 5)
                if b == 8:
                    free(L2, 8)
                    pe_turn(e, "TC", 0, 2)

            def between2(b):
                if b == 1:
                    pe_turn(e, "T2", 1, 4)
                if b == 8:
                    e.wait_ge(sem("xnT_TC"), 1)
                    pe_q(e, LC, 0)

            def beforeC(b):
                next_kv(LC, L3, b, 4)
                if b == 8:
                    free(LC, 8)
                    pe_turn(e, "TF", 0, 0)
                if b == 9:
                    pe_f2(e, 0)
                if b == 10:
                    pe_fturn(e, 0)

            def betweenC(b):
                turn_second(LC, "TC", b)
                if b == 8:
                    e.wait_ge(sem("xnT_TF"), 1)
                    for c in range(4):
                        pe_f1(e, 0, c)

            pe_attn(e, L2, STEPS, before2, between2)
            def meanwhileC():
                e.wait_ge(sem("ff_read"), 1)
                pe_turn(e, "T3", 0, 2, plain=True)

            pe_attn(e, LC, B + 3, beforeC, betweenC, lambda b: q_second(LC, "TC", b), meanwhileC)
            e.wait_ge(sem("xnT_T3"), 1)
            pe_q(e, L3, 0)
            e.wait_ge(LC.sem("z_read"), LC.past("z_read") + B)
            pe_turn(e, "TF", 1, 4)
            e.wait_ge(sem("xnT_TF"), 2)
            for c in range(4):
                pe_f1(e, 1, c)

            def before3(b):
                if b == 1:
                    pe_f2(e, 1)

            def between3(b):
                if b == 1:
                    pe_fturn(e, 1)
                turn_second(L3, "T3", b, plain=True)

            pe_attn(e, L3, B + 3, before3, between3, lambda b: q_second(L3, "T3", b))

        @block.scalar
        def _(e):
            e.wait_ge(sem("consts"), 1)
            e.copy(stackB[:, :].bitcast(F32).rearrange("p (h t) -> p h t", h=H),
                   zeros[:, :].bitcast(F32).unsqueeze(1).broadcast_to([P, H, T // 2])).then_inc(sem("blankB"), 1)
            e.wait_ge(sem("in_cols"), 16)
            for name in "qk":
                for g in range(2):
                    act_p0(e, L0, name, g)
                for g in range(2):
                    act_p1(e, L0, name, g)
            act_a1(e)
            act_v1(e, range(8))

            act_attn(e, L0, B + 2, after=lambda b: act_v1(e, V1_IN_STEP[b]) if b < 2 else None)
            for g in range(6):
                act_u1(e, 0, g)
            act_turn(e, "T1", 0, 2, "norm_w")
            for g in range(6, NT):
                act_u1(e, 0, g)

            def during1(b, place):
                if (b, place) == (0, 3):
                    act_turn(e, "T1", 1, 7, "norm_w")
                if (b, place) == (5, 3):
                    act_turn(e, "T2", 0, 7, "n1_g", "n1_b")
                if (b, place) == (6, 0):
                    e.wait_ge(sem("r_mm"), 1)
                    e.activation(small[:, 6:8], bank(7)[:, 0:2], ACT.Relu, bias=col("r_b1"))\
                     .then_inc(sem("r_hidden"), 1)
                if (b, place) == (6, 2):
                    act_p0(e, L2, "k", 0)
                if (b, place) == (6, 3):
                    block_row(e, 1)
                    act_p1(e, L2, "k", 0)
                if (b, place) == (7, 0):
                    act_p0(e, L2, "q", 0)
                if (b, place) == (7, 1):
                    act_p1(e, L2, "q", 0)

            act_l1(e, during1)

            def turn_second(n, b, gain=None, bias=None):
                if b == 2:
                    act_turn(e, n, 1, 7, gain, bias)

            def q_second(L, b):
                if b == 2:
                    act_p0(e, L, "q", 1)
                    act_p1(e, L, "q", 1)

            def before2(b):
                if b == 2:
                    act_p0(e, L2, "k", 1)
                    act_p0(e, L2, "q", 1)
                if b in (5, 6):
                    act_p0(e, LC, "k", b - 5)
                if b == 8:
                    act_turn(e, "TC", 0, 2, "n2_g", "n2_b")

            def between2(b):
                if b == 1:
                    act_turn(e, "T2", 1, 4, "n1_g", "n1_b")
                if b == 2:
                    act_p1(e, L2, "k", 1)
                    act_p1(e, L2, "q", 1)
                if b in (5, 6):
                    act_p1(e, LC, "k", b - 5)
                if b == 8:
                    act_p0(e, LC, "q", 0)
                    act_p1(e, LC, "q", 0)

            def beforeC(b):
                if b in (4, 5):
                    act_p0(e, L3, "k", b - 4)
                if b == 8:
                    act_turn(e, "TF", 0, 0, "n3_g", "n3_b")
                if b == 10:
                    act_f2(e, 0)

            def betweenC(b):
                turn_second("TC", b, "n2_g", "n2_b")
                if b in (4, 5):
                    act_p1(e, L3, "k", b - 4)
                if b == 8:
                    for c in range(4):
                        act_f1(e, 0, c)

            act_attn(e, L2, STEPS, before2, between2)
            act_attn(e, LC, B + 3, beforeC, betweenC, lambda b: q_second(LC, b))
            act_turn(e, "T3", 0, 2)
            act_p0(e, L3, "q", 0)
            act_p1(e, L3, "q", 0)
            act_turn(e, "TF", 1, 4, "n3_g", "n3_b")
            for c in range(4):
                act_f1(e, 1, c)

            def before3(b):
                if b == 1:
                    act_f2(e, 1)

            act_attn(e, L3, B + 2, before3, lambda b: turn_second("T3", b), lambda b: q_second(L3, b))

        @block.vector
        def _(e):
            e.wait_ge(sem("in_mask"), 16)
            ps = sem("padsplit")
            u = rest[0:H, 0:2, :].rearrange("p a n -> p (a n)")
            v = rest[0:H, 2:4, :].rearrange("p a n -> p (a n)")
            e.tensor_scalar(u, pad[0:H, :], -1.0, -PAD / L0.scale, ALU.add, ALU.mult).then_inc(ps, 1)
            e.wait_ge(ps, 1)
            e.wait_ge(sem("in_ctx"), 16)
            e.tensor_tensor(pad[:, :], ctxT[:, :], pad[:, :], ALU.mult).then_inc(sem("padmul"), 1)
            e.tensor_copy(rows[:, 0, :], u).then_inc(ps, 1)
            e.wait_ge(ps, 2)
            e.tensor_tensor(v, u, rows[:, 0, :], ALU.subtract).then_inc(ps, 1)
            e.wait_ge(ps, 3)
            e.tensor_copy(rows[:, 1, :], v).then_inc(ps, 1)
            e.wait_ge(ps, 4)
            e.tensor_tensor(rows[:, 2, :], v, rows[:, 1, :], ALU.subtract).then_inc(ps, 1)
            e.wait_ge(ps, 5)
            e.wait_ge(sem("in_cols"), 16)
            for name in "qk":
                for g in range(2):
                    dve_rest(e, L0, name, g)
                for g in range(2):
                    dve_p2(e, L0, name, g)
            for g in range(2):
                dve_v(e, L0, g)

            def norm0(g):
                at = slice(4 * g, 4 * g + 4)
                dve_xn(e, "N0", "ln", 4 * g, 4)
                e.wait_ge(sem("xn_N0"), 4 * g + 4)
                e.tensor_tensor(xn[:, at, :], xn[:, at, :], row("g_0", 4), ALU.mult).then_inc(sem("aff"), 1)
                e.wait_ge(sem("aff"), 2 * g + 1)
                e.tensor_tensor(x[:, at, :], xn[:, at, :], row("b_0", 4), ALU.add).then_inc(sem("aff"), 1)

            def input1(g):
                for b in range(4 * g, 4 * g + 4):
                    dve_stats(e, "X1", b, sem("aff"), 2 * g + 1 - b)
                dve_msq(e, "T1", "X1", g)
                dve_xn(e, "T1", "rms", 4 * g, 4)

            def after0(b):
                if b == 8:
                    norm0(0)
                if b == 9:
                    input1(0)

            dve_attn(e, L0, B + 3, after=after0)
            norm0(1)

            def during1(b, place):
                if (b, place) == (0, 0):
                    input1(1)
                if (b, place) == (4, 2):
                    dve_xn(e, "T2", "ln", 0, 4)
                if (b, place) == (5, 2):
                    wait_half(e, L2, "k_mm", 0)
                    r = sem("router")
                    e.tensor_copy(kept[:, 1, 0, :], bank(7)).then_inc(r, 1)
                    e.wait_ge(r, 1)
                    e.tensor_reduce(small[:, 2:4], kept[:, 1, 0, 0:P].rearrange("p (c t) -> p c t", c=2),
                                    AX.X, ALU.add).then_inc(r, 1)
                    e.wait_ge(r, 2)
                    e.tensor_scalar(small[:, 4:6], small[:, 2:4], 1.0 / BLOCK, None, ALU.mult).then_inc(r, 1)
                    e.tensor_copy(mat("v1")[:, 0:P], col("r_w2").broadcast_to([P, P])).then_inc(sem("r_hidden"), 1)
                if (b, place) == (6, 0):
                    e.wait_ge(sem("r_mm"), 2)
                    k = sem("keep")
                    e.tensor_scalar(keep[:, :], bank(7)[:, 0:2], col("r_b2"), 0.0, ALU.add, ALU.is_gt).then_inc(k, 1)
                    e.wait_ge(k, 1)
                    e.tensor_scalar(keepn[:, 0, :], keep[:, :], -NEG, NEG, ALU.mult, ALU.add).then_inc(k, 1)
                    e.tensor_scalar(keepn[:, 1, :], keep[:, :], NEG, None, ALU.mult).then_inc(k, 1)
                    e.tensor_scalar(keepn[:, 2, :], keep[:, :], -1.0, 1.0, ALU.mult, ALU.add).then_inc(k, 1)
                    dve_kept(e, L2, "k", 0, kept[:, 1, 0, :])
                if (b, place) == (6, 1):
                    dve_v(e, L2, 0)
                    dve_rest(e, L2, "k", 0)
                    block_row(e, 2)
                if (b, place) == (6, 2):
                    dve_kept(e, L2, "q", 0)
                    dve_p2(e, L2, "k", 0)
                if (b, place) == (7, 0):
                    dve_rest(e, L2, "q", 0)
                if (b, place) == (7, 1):
                    dve_p2(e, L2, "q", 0)

            dve_l1(e, during1)

            def before2(b):
                if b == 1:
                    dve_z1(e, B // 2 - 1)
                    dve_xn(e, "T2", "ln", 4, 4)
                if b == 2:
                    dve_kept(e, L2, "k", 1)
                    dve_kept(e, L2, "q", 1)
                    dve_rest(e, L2, "k", 1)
                    dve_rest(e, L2, "q", 1)
                if b == 4:
                    dve_v(e, L2, 1)
                if b in (5, 6):
                    dve_rest(e, LC, "k", b - 5)
                if b == 7:
                    dve_v(e, LC, 0)
                    dve_v(e, LC, 1)

            def between2(b):
                if b == 2:
                    dve_p2(e, L2, "k", 1)
                    dve_p2(e, L2, "q", 1)
                if b in (5, 6):
                    dve_p2(e, LC, "k", b - 5)
                if b == 7:
                    dve_xn(e, "TC", "ln", 0, 4)
                if b == 8:
                    dve_rest(e, LC, "q", 0)

            def beforeC(b):
                if b == 2:
                    dve_xn(e, "TC", "ln", 4, 4)
                if b in (4, 5):
                    dve_rest(e, L3, "k", b - 4)
                if b == 6:
                    dve_v(e, L3, 0)
                    dve_v(e, L3, 1)
                if b == 10:
                    dve_ff(e, 0)

            def betweenC(b):
                if b == 2:
                    dve_rest(e, LC, "q", 1)
                    dve_p2(e, LC, "q", 1)
                if b in (4, 5):
                    dve_p2(e, L3, "k", b - 4)
                if b == 7:
                    dve_xn(e, "TF", "ln", 0, 4)

            dve_attn(e, L2, STEPS, before2, between2,
                     lambda b: dve_p2(e, LC, "q", 0) if b == 8 else None)
            dve_attn(e, LC, B + 3, beforeC, betweenC)
            dve_rest(e, L3, "q", 0)
            dve_xn(e, "TF", "ln", 4, 4)
            dve_p2(e, L3, "q", 0)

            def output(b0):
                at, n = slice(b0, b0 + 2), b0 // 2
                dve_xn(e, "N3", "ln", b0, 2)
                e.wait_ge(sem("xn_N3"), b0 + 2)
                e.tensor_tensor(xn[:, at, :], xn[:, at, :], row("g_3", 2), ALU.mult).then_inc(sem("aff3"), 1)
                e.wait_ge(sem("aff3"), n + 1)
                e.tensor_tensor(xn[:, at, :], xn[:, at, :], row("b_3", 2), ALU.add).then_inc(sem("out_ready"), 1)

            def before3(b):
                if b == 9:
                    output(0)
                    output(2)
                if b == 10:
                    output(4)

            def between3(b):
                if b == 1:
                    dve_ff(e, 1)
                if b == 2:
                    dve_rest(e, L3, "q", 1)
                    dve_p2(e, L3, "q", 1)

            dve_attn(e, L3, B + 3, before3, between3)
            output(6)


def kernel(**inputs):
    import concourse.bacc as _bacc
    from concourse.bass_utils import run_bass_kernel_spmd as _run

    a = {k: np.asarray(v) for k, v in inputs.items()}

    def by_feature(w):
        s = w.shape[:-1]
        return w.reshape(*s, 4, 4, E).swapaxes(-1, -3).reshape(*s, P)

    l2, ca = a["L2_xattn_qkv_w"], a["L2_xattn_ca_in_w"]
    cab = a["L2_xattn_ca_in_b"]
    w3 = {k: a[f"L3_xattn_W{k}"].transpose(1, 0, 2).reshape(P, P) for k in "qkv"}
    mats = {
        "q0": by_feature(a["L0_xattn_wq"]), "k0": by_feature(a["L0_xattn_wk"]),
        "v0": a["L0_xattn_wv"], "o0": a["L0_xattn_wo"],
        "q2": by_feature(l2[0:P].T), "k2": by_feature(l2[P:2 * P].T), "v2": l2[2 * P:].T,
        "o2": a["L2_xattn_sa_out_w"].T,
        "qc": by_feature(ca[0:P].T), "kc": by_feature(ca[P:2 * P].T), "vc": ca[2 * P:].T,
        "oc": a["L2_xattn_ca_out_w"].T,
        "q3": by_feature(w3["q"]), "k3": by_feature(w3["k"]), "v3": w3["v"], "o3": a["L3_xattn_Wo"],
        "r1": by_feature(a["L2_xattn_r_w1"]).T,
        "a1": np.stack([a["L1_xattn_wq"].T.reshape(NT, P, P), a["L1_xattn_wk"].T.reshape(NT, P, P)], axis=1)
              .transpose(2, 0, 1, 3).reshape(P, 2 * H * HD), "v1": a["L1_xattn_wv"],
        "o1": a["L1_xattn_wo"].reshape(NT, P, P).transpose(1, 0, 2).reshape(P, NT * P),
        "f1": a["L2_xattn_ff_w1"].T,
        "f2": a["L2_xattn_ff_w2"].T.reshape(4, P, P).transpose(1, 0, 2).reshape(P, FF),
    }
    fb = a["L2_xattn_ff_b1"].reshape(4, P)
    cols = {
        "norm_w": a["L1_xattn_norm_w"], "bq_c": by_feature(cab[0:P]), "bk_c": by_feature(cab[P:2 * P]),
        "bq_3": by_feature(a["L3_xattn_bq"].reshape(P)), "bk_3": by_feature(a["L3_xattn_bk"].reshape(P)),
        "r_b1": a["L2_xattn_r_b1"], "r_w2": a["L2_xattn_r_w2"].reshape(P),
        "r_b2": np.broadcast_to(a["L2_xattn_r_b2"], (P,)),
        **{f"n{n}_{s}": a[f"L2_xattn_n{n}_{s}"] for n in (1, 2, 3) for s in "gb"},
        **{f"f_b{c}": fb[c] for c in range(4)},
    }
    rows = {
        "bo_0": a["L0_xattn_bo"], "g_0": a["L0_xattn_ln_gamma"], "b_0": a["L0_xattn_ln_beta"],
        "bo_2": a["L2_xattn_sa_out_b"], "bv_c": cab[2 * P:], "bo_c": a["L2_xattn_ca_out_b"],
        "b_ff": a["L2_xattn_ff_b2"], "bv_3": a["L3_xattn_bv"].reshape(P), "bo_3": a["L3_xattn_bo"],
        "g_3": a["L3_xattn_gamma"], "b_3": a["L3_xattn_beta"],
    }
    x = a["x"]
    arrays = {
        "xt": x.transpose(2, 0, 1).reshape(P, T),
        "xtok": x.transpose(1, 0, 2),
        "ctxt": a["ctx_1024"].transpose(2, 0, 1).reshape(P, T),
        "mask": a["mask_BxS2_ff1"].reshape(T),
        "wmat": np.concatenate([mats[m] for m in MATS], axis=1),
        "wcol": np.stack([cols[c] for c in COLS], axis=1),
        "wrow": np.concatenate([rows[r] for r in ROWS]),
    }
    nc = _bacc.Bacc("TRN2", target_bir_lowering=False, num_devices=1)
    args, arr = [], {}
    for name, v in arrays.items():
        arr[f"in_{name}"] = np.ascontiguousarray(v)
        args.append(nc.dram_tensor(f"in_{name}", v.shape, F32, kind="ExternalInput").ap())
    args.append(nc.dram_tensor("out_x", (B, P, P), F32, kind="ExternalOutput").ap())
    build(nc, *args)
    r = _run(nc, [arr], core_ids=[0])
    return r.results[0]["out_x"]
```
